# Optimizing a Trainium2 kernel written in Bass

```python
import numpy as np
import jax
import jax.numpy as jnp

def _softmax(x, axis=-1):
    return jax.nn.softmax(x, axis=axis)

def _gelu(x):
    return jax.nn.gelu(x, approximate=True)

def _silu(x):
    return jax.nn.silu(x)

def _sigmoid(x):
    return jax.nn.sigmoid(x)

def _layernorm(x, axis=-1, eps=1e-05):
    m = jnp.mean(x, axis=axis, keepdims=True)
    v = jnp.var(x, axis=axis, keepdims=True)
    return (x - m) / jnp.sqrt(v + eps)

def _scatter_add(tgt, idx, src, axis=0):
    return tgt.at[idx].add(src)

def _segment_sum(src, seg, n):
    return jax.ops.segment_sum(src, seg, n)
kernel_name = 'mk_perceiver_d4_seqx_r4_e94038'

def setup_inputs(seed: int=0):
    np.random.seed(seed)
    _w = jnp.asarray

    def _rec_inputs():
        import jax
        import jax.numpy as jnp
        _rk = jax.random.key(seed)
        x = -0.0003929 + 0.9999 * jax.random.normal(jax.random.fold_in(_rk, 1), (8, 64, 256), jnp.float32)
        _lenS = 64 - jax.random.randint(jax.random.fold_in(_rk, 7), (8,), 0, max(1, 64 // 4) + 1, jnp.int32)
        _lenS2 = 1024 - jax.random.randint(jax.random.fold_in(_rk, 8), (8,), 0, max(1, 1024 // 4) + 1, jnp.int32)
        _ctx_768P = jax.random.normal(jax.random.fold_in(_rk, 11), (8, 16, 192), jnp.float32)
        _ctx_768c = jax.random.dirichlet(jax.random.fold_in(_rk, 511), 0.3 * jnp.ones((16,), jnp.float32), (8, 1024))
        _ctx_768t = jnp.einsum('bsk,bkd->bsd', _ctx_768c, _ctx_768P)
        _ctx_768t = _ctx_768t * jax.lax.rsqrt(jnp.mean(jnp.square(_ctx_768t)) + 1e-12) * 0.953939
        ctx_768 = -7.36909e-05 + 0.999899 * (_ctx_768t + 0.3 * jax.random.normal(jax.random.fold_in(_rk, 611), (8, 1024, 192), jnp.float32))
        return (x, ctx_768)
    x, ctx_768 = _rec_inputs()

    def _L0_xattn_setup():
        import jax, jax.numpy as jnp
        import numpy as np
        IMG_DIM, TXT_DIM, HID = (256, 192, 256)
        B, LQ, LK = (8, 512, 512)
        key = jax.random.key(seed)
        ks = jax.random.split(key, 8)
        s_img = 1.0 / np.sqrt(IMG_DIM)
        s_txt = 1.0 / np.sqrt(TXT_DIM)
        return {'image_features': jax.random.normal(ks[0], (B, LQ, IMG_DIM), jnp.float32), 'text_features': jax.random.normal(ks[1], (B, LK, TXT_DIM), jnp.float32), 'Wq': jax.random.uniform(ks[2], (IMG_DIM, HID), jnp.float32, -s_img, s_img), 'bq': jax.random.uniform(ks[3], (HID,), jnp.float32, -s_img, s_img), 'Wk': jax.random.uniform(ks[4], (TXT_DIM, HID), jnp.float32, -s_txt, s_txt), 'bk': jax.random.uniform(ks[5], (HID,), jnp.float32, -s_txt, s_txt), 'Wv': jax.random.uniform(ks[6], (TXT_DIM, HID), jnp.float32, -s_txt, s_txt), 'bv': jax.random.uniform(ks[7], (HID,), jnp.float32, -s_txt, s_txt)}
    _L0_xattn_all = _L0_xattn_setup()
    _L0_xattn_in = {k: v for k, v in _L0_xattn_all.items() if k in ('Wq', 'bq', 'Wk', 'bk', 'Wv', 'bv')}
    del _L0_xattn_all

    def _L0_attn_setup():
        import jax, jax.numpy as jnp
        import numpy as np
        N_EMBD = 256
        N_HEAD = 16
        HEAD_DIM = N_EMBD // N_HEAD
        LATENT_DIM = N_EMBD // 2
        B, T = (4, 512)
        key = jax.random.key(seed)
        ks = jax.random.split(key, 5)

        def init(k, fan_in, fan_out):
            bound = 1.0 / np.sqrt(fan_in)
            return jax.random.uniform(k, (fan_in, fan_out), jnp.float32, -bound, bound)
        return {'x': jax.random.normal(ks[0], (B, T, N_EMBD), jnp.float32), 'Wc_down': init(ks[1], N_EMBD, LATENT_DIM), 'Wq_up': init(ks[2], LATENT_DIM, N_EMBD), 'Wkv_up': init(ks[3], LATENT_DIM, 2 * HEAD_DIM), 'Wc_proj': init(ks[4], N_EMBD, N_EMBD)}
    _L0_attn_all = _L0_attn_setup()
    _L0_attn_in = {k: v for k, v in _L0_attn_all.items() if k in ('Wc_down', 'Wq_up', 'Wkv_up', 'Wc_proj')}
    del _L0_attn_all

    def _L0_ffn_setup():
        import jax, jax.numpy as jnp
        import numpy as np
        N, T, D = (4, 1024, 256)
        NUM_EXPERTS = 8
        EXPERT_CAP = 2.0
        MLP_RATIO = 4
        HIDDEN = MLP_RATIO * D
        key = jax.random.key(seed)
        k1, k2, k3, k4 = jax.random.split(key, 4)
        x = jax.random.normal(k1, (N, T, D), dtype=jnp.float32)
        gate_w = jax.random.truncated_normal(k2, -2.0, 2.0, (D, NUM_EXPERTS), dtype=jnp.float32) * 0.02
        w1 = jax.random.normal(k3, (NUM_EXPERTS, D, HIDDEN), dtype=jnp.float32) * 0.02
        w2 = jax.random.normal(k4, (NUM_EXPERTS, HIDDEN, D), dtype=jnp.float32) * 0.02
        return {'x': x, 'gate_w': gate_w, 'w1': w1, 'w2': w2}
    _L0_ffn_all = _L0_ffn_setup()
    _L0_ffn_in = {k: v for k, v in _L0_ffn_all.items() if k in ('gate_w', 'w1', 'w2')}
    del _L0_ffn_all

    def _L1_xattn_setup():
        import jax, jax.numpy as jnp
        import numpy as np
        HEADS = 16
        DIM_HEAD = 64
        key = jax.random.key(seed)
        ks = jax.random.split(key, 8)
        B, S, D = (16, 1024, 256)
        K, DE = (77, 192)
        inner = HEADS * DIM_HEAD
        hidden_states = jax.random.normal(ks[0], (B, S, D), dtype=jnp.float32)
        encoder_hidden_states = jax.random.normal(ks[1], (B, K, DE), dtype=jnp.float32)
        sc_q = 1.0 / np.sqrt(D)
        sc_kv = 1.0 / np.sqrt(DE)
        sc_o = 1.0 / np.sqrt(inner)
        Wq = jax.random.normal(ks[2], (D, inner), dtype=jnp.float32) * sc_q
        Wk = jax.random.normal(ks[3], (DE, inner), dtype=jnp.float32) * sc_kv
        Wv = jax.random.normal(ks[4], (DE, inner), dtype=jnp.float32) * sc_kv
        Wo = jax.random.normal(ks[5], (inner, D), dtype=jnp.float32) * sc_o
        bo = jax.random.normal(ks[6], (D,), dtype=jnp.float32) * 0.01
        return {'hidden_states': hidden_states, 'encoder_hidden_states': encoder_hidden_states, 'Wq': Wq, 'Wk': Wk, 'Wv': Wv, 'Wo': Wo, 'bo': bo}
    _L1_xattn_all = _L1_xattn_setup()
    _L1_xattn_in = {k: v for k, v in _L1_xattn_all.items() if k in ('Wq', 'Wk', 'Wv', 'Wo', 'bo')}
    del _L1_xattn_all

    def _L1_attn_setup():
        import jax, jax.numpy as jnp
        import numpy as np
        import math
        D_MODEL = 256
        N_HEADS = 16
        HEAD_DIM = D_MODEL // N_HEADS
        ROT_DIM = min(32, D_MODEL // 4)

        def _xavier(key, fan_in, fan_out):
            lim = math.sqrt(6.0 / (fan_in + fan_out))
            return jax.random.uniform(key, (fan_in, fan_out), jnp.float32, -lim, lim)
        key = jax.random.key(seed)
        ks = jax.random.split(key, 6)
        x = jax.random.normal(ks[0], (2, 512, D_MODEL), jnp.float32)
        Wq = _xavier(ks[1], D_MODEL, D_MODEL)
        Wk = _xavier(ks[2], D_MODEL, D_MODEL)
        Wv = _xavier(ks[3], D_MODEL, D_MODEL)
        Wr = _xavier(ks[4], D_MODEL, N_HEADS * ROT_DIM)
        Wo = _xavier(ks[5], D_MODEL, D_MODEL)
        z = jnp.zeros((D_MODEL,), jnp.float32)
        zr = jnp.zeros((N_HEADS * ROT_DIM,), jnp.float32)
        return {'x': x, 'Wq': Wq, 'bq': z, 'Wk': Wk, 'bk': z, 'Wv': Wv, 'bv': z, 'Wr': Wr, 'br': zr, 'Wo': Wo, 'bo': z}
    _L1_attn_all = _L1_attn_setup()
    _L1_attn_in = {k: v for k, v in _L1_attn_all.items() if k in ('Wq', 'bq', 'Wk', 'bk', 'Wv', 'bv', 'Wr', 'br', 'Wo', 'bo')}
    del _L1_attn_all

    def _L1_ffn_setup():
        import jax, jax.numpy as jnp
        import numpy as np
        E = 16
        K = 2
        LOAD = 1.0

        def _dispatch(xb, pb, cap):
            T, C = xb.shape
            top_k_probs, ei = jax.lax.top_k(pb, K)
            flat = ei.swapaxes(0, 1).ravel()
            one_hot = jax.nn.one_hot(flat, E, dtype=jnp.int32)
            pos = jnp.cumsum(one_hot, axis=0) * one_hot
            pos = pos.reshape(K, T, E).swapaxes(0, 1)
            pos = jnp.max(pos, axis=-1) - 1
            ei2 = flat.reshape(K, T).swapaxes(0, 1)
            xr = jnp.repeat(xb, K, axis=0)
            buf = jnp.zeros((E, cap, C), xb.dtype)
            buf = buf.at[ei2.ravel(), pos.ravel()].set(xr, mode='drop')
            return (top_k_probs, pos, ei2, buf)

        def _collect(eo_b, ei_b, pos_b, tk_b):
            out = eo_b[ei_b, pos_b]
            return jnp.sum(tk_b[..., None] * out, axis=1)
        key = jax.random.key(seed)
        k1, k2, k3, k4, k5 = jax.random.split(key, 5)
        B, T, C, H = (8, 1024, 256, 128)
        n_layer = 12
        x = jax.random.normal(k1, (B, T, C), dtype=jnp.float32)
        w_router = jax.random.normal(k2, (C, E), dtype=jnp.float32) * 0.02
        w_fc = jax.random.normal(k3, (E, C, H), dtype=jnp.float32) * 0.02
        w_gate = jax.random.normal(k4, (E, C, H), dtype=jnp.float32) * 0.02
        w_proj = jax.random.normal(k5, (E, H, C), dtype=jnp.float32) * (0.02 * (2 * n_layer) ** (-0.5))
        return {'x': x, 'w_router': w_router, 'w_fc': w_fc, 'w_gate': w_gate, 'w_proj': w_proj}
    _L1_ffn_all = _L1_ffn_setup()
    _L1_ffn_in = {k: v for k, v in _L1_ffn_all.items() if k in ('w_router', 'w_fc', 'w_gate', 'w_proj')}
    del _L1_ffn_all

    def _L2_xattn_setup():
        import jax, jax.numpy as jnp
        import numpy as np
        HEADS = 16
        DIM_HEAD = 64
        key = jax.random.key(seed)
        ks = jax.random.split(key, 7)
        b, n, m = (2, 512, 256)
        query_dim, context_dim = (256, 192)
        inner = HEADS * DIM_HEAD
        s_q = 1.0 / np.sqrt(query_dim)
        s_c = 1.0 / np.sqrt(context_dim)
        s_i = 1.0 / np.sqrt(inner)
        return {'x': jax.random.normal(ks[0], (b, n, query_dim), jnp.float32), 'context': jax.random.normal(ks[1], (b, m, context_dim), jnp.float32), 'Wq': jax.random.normal(ks[2], (query_dim, inner), jnp.float32) * s_q, 'Wk': jax.random.normal(ks[3], (context_dim, inner), jnp.float32) * s_c, 'Wv': jax.random.normal(ks[4], (context_dim, inner), jnp.float32) * s_c, 'Wo': jax.random.normal(ks[5], (inner, query_dim), jnp.float32) * s_i, 'bo': jax.random.normal(ks[6], (query_dim,), jnp.float32) * 0.01}
    _L2_xattn_all = _L2_xattn_setup()
    _L2_xattn_in = {k: v for k, v in _L2_xattn_all.items() if k in ('Wq', 'Wk', 'Wv', 'Wo', 'bo')}
    del _L2_xattn_all

    def _L2_attn_setup():
        import jax, jax.numpy as jnp
        import numpy as np
        SEQ_LEN = 512
        DIM_EMB = 256
        DIM_K = 256
        DIM_V = 256
        BATCH = 4
        key = jax.random.key(seed)
        kx, kq, kk, kv, ko = jax.random.split(key, 5)
        s = DIM_EMB ** (-0.5)
        return {'x': jax.random.normal(kx, (BATCH, SEQ_LEN, DIM_EMB), dtype=jnp.float32), 'Wq': jax.random.normal(kq, (DIM_EMB, DIM_K), dtype=jnp.float32) * s, 'Wk': jax.random.normal(kk, (DIM_EMB, DIM_K), dtype=jnp.float32) * s, 'Wv': jax.random.normal(kv, (DIM_EMB, DIM_V), dtype=jnp.float32) * s, 'Wo': jax.random.normal(ko, (DIM_V, DIM_V), dtype=jnp.float32) * DIM_V ** (-0.5)}
    _L2_attn_all = _L2_attn_setup()
    _L2_attn_in = {k: v for k, v in _L2_attn_all.items() if k in ('Wq', 'Wk', 'Wv', 'Wo')}
    del _L2_attn_all

    def _L2_ffn_setup():
        import jax, jax.numpy as jnp
        import numpy as np
        B, S, D, E, F = (4, 512, 256, 8, 1024)
        MIN_CAPACITY = 4

        def _make_waff():
            g = D // E
            scale = E / D
            w = np.zeros((E, D), np.float32)
            for i in range(E):
                w[i, i * g:(i + 1) * g] = scale
            return jnp.asarray(w)
        key = jax.random.key(seed)
        ks = jax.random.split(key, 6)
        inputs = jax.random.normal(ks[0], (B, S, D), dtype=jnp.float32)
        W1 = jax.random.normal(ks[1], (E, D, F), dtype=jnp.float32) * (1.0 / np.sqrt(D))
        b1 = jnp.zeros((E, F), dtype=jnp.float32)
        W2 = jax.random.normal(ks[2], (E, F, D), dtype=jnp.float32) * (1.0 / np.sqrt(F))
        b2 = jnp.zeros((E, D), dtype=jnp.float32)
        return {'inputs': inputs, 'waff': _make_waff(), 'W1': W1, 'b1': b1, 'W2': W2, 'b2': b2, 'affinity_threshold': jnp.float32(0.5)}
    _L2_ffn_all = _L2_ffn_setup()
    _L2_ffn_in = {k: v for k, v in _L2_ffn_all.items() if k in ('waff', 'W1', 'b1', 'W2', 'b2', 'affinity_threshold')}
    del _L2_ffn_all

    def _L3_xattn_setup():
        import jax, jax.numpy as jnp
        import numpy as np
        EPS = 1e-05

        def layernorm(x, g, b):
            mu = jnp.mean(x, axis=-1, keepdims=True)
            var = jnp.mean(jnp.square(x - mu), axis=-1, keepdims=True)
            return (x - mu) * jax.lax.rsqrt(var + EPS) * g + b
        key = jax.random.key(seed)
        ks = jax.random.split(key, 12)
        B, L1, L2 = (8, 512, 512)
        D1, D2, E = (256, 192, 256)
        s1, s2, se = (D1 ** (-0.5), D2 ** (-0.5), E ** (-0.5))
        return {'modality1': jax.random.normal(ks[0], (B, L1, D1), jnp.float32), 'modality2': jax.random.normal(ks[1], (B, L2, D2), jnp.float32), 'ln1_g': jnp.ones((D1,), jnp.float32), 'ln1_b': jnp.zeros((D1,), jnp.float32), 'ln2_g': jnp.ones((D2,), jnp.float32), 'ln2_b': jnp.zeros((D2,), jnp.float32), 'Wq': jax.random.normal(ks[2], (D1, E), jnp.float32) * s1, 'bq': jax.random.normal(ks[3], (E,), jnp.float32) * 0.01, 'Wk': jax.random.normal(ks[4], (D2, E), jnp.float32) * s2, 'bk': jax.random.normal(ks[5], (E,), jnp.float32) * 0.01, 'Wv': jax.random.normal(ks[6], (D2, E), jnp.float32) * s2, 'bv': jax.random.normal(ks[7], (E,), jnp.float32) * 0.01, 'Wo': jax.random.normal(ks[8], (E, D1), jnp.float32) * se, 'bo': jax.random.normal(ks[9], (D1,), jnp.float32) * 0.01}
    _L3_xattn_all = _L3_xattn_setup()
    _L3_xattn_in = {k: v for k, v in _L3_xattn_all.items() if k in ('ln1_g', 'ln1_b', 'ln2_g', 'ln2_b', 'Wq', 'bq', 'Wk', 'bk', 'Wv', 'bv', 'Wo', 'bo')}
    del _L3_xattn_all

    def _L3_attn_setup():
        import jax, jax.numpy as jnp
        import numpy as np
        B, S, H = (8, 512, 256)
        key = jax.random.key(seed)
        k1, k2, k3 = jax.random.split(key, 3)
        x = jax.random.normal(k1, (B, S, H), dtype=jnp.float32)
        W_qkv = jax.random.normal(k2, (3 * H, H), dtype=jnp.float32) / np.sqrt(H)
        W_out = jax.random.normal(k3, (H, H), dtype=jnp.float32) / np.sqrt(H)
        return {'x': x, 'W_qkv': W_qkv, 'W_out': W_out}
    _L3_attn_all = _L3_attn_setup()
    _L3_attn_in = {k: v for k, v in _L3_attn_all.items() if k in ('W_qkv', 'W_out')}
    del _L3_attn_all

    def _L3_ffn_setup():
        import jax, jax.numpy as jnp
        import numpy as np
        D_MODEL = 256
        M = 64
        INNER = 16
        key = jax.random.key(seed)
        ks = jax.random.split(key, 9)

        def init(k, shape, fan_in):
            bound = 1.0 / np.sqrt(fan_in)
            return jax.random.uniform(k, shape, jnp.float32, -bound, bound)
        x = jax.random.normal(ks[0], (16, 1024, D_MODEL), dtype=jnp.float32)
        Win = init(ks[1], (D_MODEL, M), D_MODEL)
        bin_ = init(ks[2], (M,), D_MODEL)
        W1 = init(ks[3], (M, INNER), 1)
        b1 = init(ks[4], (M, INNER), 1)
        W2 = init(ks[5], (M, INNER), INNER)
        b2 = init(ks[6], (M,), INNER)
        Wout = init(ks[7], (M, D_MODEL), M)
        bout = init(ks[8], (D_MODEL,), M)
        return {'x': x, 'Win': Win, 'bin_': bin_, 'W1': W1, 'b1': b1, 'W2': W2, 'b2': b2, 'Wout': Wout, 'bout': bout}
    _L3_ffn_all = _L3_ffn_setup()
    _L3_ffn_in = {k: v for k, v in _L3_ffn_all.items() if k in ('Win', 'bin_', 'W1', 'b1', 'W2', 'b2', 'Wout', 'bout')}
    del _L3_ffn_all
    return {'x': x, 'ctx_768': ctx_768, 'L0_xattn_Wq': _L0_xattn_in['Wq'], 'L0_xattn_bq': _L0_xattn_in['bq'], 'L0_xattn_Wk': _L0_xattn_in['Wk'], 'L0_xattn_bk': _L0_xattn_in['bk'], 'L0_xattn_Wv': _L0_xattn_in['Wv'], 'L0_xattn_bv': _L0_xattn_in['bv'], 'L0_attn_Wc_down': _L0_attn_in['Wc_down'], 'L0_attn_Wq_up': _L0_attn_in['Wq_up'], 'L0_attn_Wkv_up': _L0_attn_in['Wkv_up'], 'L0_attn_Wc_proj': _L0_attn_in['Wc_proj'], 'L0_ffn_gate_w': _L0_ffn_in['gate_w'], 'L0_ffn_w1': _L0_ffn_in['w1'], 'L0_ffn_w2': _L0_ffn_in['w2'], 'L1_xattn_Wq': _L1_xattn_in['Wq'], 'L1_xattn_Wk': _L1_xattn_in['Wk'], 'L1_xattn_Wv': _L1_xattn_in['Wv'], 'L1_xattn_Wo': _L1_xattn_in['Wo'], 'L1_xattn_bo': _L1_xattn_in['bo'], 'L1_attn_Wq': _L1_attn_in['Wq'], 'L1_attn_bq': _L1_attn_in['bq'], 'L1_attn_Wk': _L1_attn_in['Wk'], 'L1_attn_bk': _L1_attn_in['bk'], 'L1_attn_Wv': _L1_attn_in['Wv'], 'L1_attn_bv': _L1_attn_in['bv'], 'L1_attn_Wr': _L1_attn_in['Wr'], 'L1_attn_br': _L1_attn_in['br'], 'L1_attn_Wo': _L1_attn_in['Wo'], 'L1_attn_bo': _L1_attn_in['bo'], 'L1_ffn_w_router': _L1_ffn_in['w_router'], 'L1_ffn_w_fc': _L1_ffn_in['w_fc'], 'L1_ffn_w_gate': _L1_ffn_in['w_gate'], 'L1_ffn_w_proj': _L1_ffn_in['w_proj'], 'L2_xattn_Wq': _L2_xattn_in['Wq'], 'L2_xattn_Wk': _L2_xattn_in['Wk'], 'L2_xattn_Wv': _L2_xattn_in['Wv'], 'L2_xattn_Wo': _L2_xattn_in['Wo'], 'L2_xattn_bo': _L2_xattn_in['bo'], 'L2_attn_Wq': _L2_attn_in['Wq'], 'L2_attn_Wk': _L2_attn_in['Wk'], 'L2_attn_Wv': _L2_attn_in['Wv'], 'L2_attn_Wo': _L2_attn_in['Wo'], 'L2_ffn_waff': _L2_ffn_in['waff'], 'L2_ffn_W1': _L2_ffn_in['W1'], 'L2_ffn_b1': _L2_ffn_in['b1'], 'L2_ffn_W2': _L2_ffn_in['W2'], 'L2_ffn_b2': _L2_ffn_in['b2'], 'L2_ffn_affinity_threshold': _L2_ffn_in['affinity_threshold'], 'L3_xattn_ln1_g': _L3_xattn_in['ln1_g'], 'L3_xattn_ln1_b': _L3_xattn_in['ln1_b'], 'L3_xattn_ln2_g': _L3_xattn_in['ln2_g'], 'L3_xattn_ln2_b': _L3_xattn_in['ln2_b'], 'L3_xattn_Wq': _L3_xattn_in['Wq'], 'L3_xattn_bq': _L3_xattn_in['bq'], 'L3_xattn_Wk': _L3_xattn_in['Wk'], 'L3_xattn_bk': _L3_xattn_in['bk'], 'L3_xattn_Wv': _L3_xattn_in['Wv'], 'L3_xattn_bv': _L3_xattn_in['bv'], 'L3_xattn_Wo': _L3_xattn_in['Wo'], 'L3_xattn_bo': _L3_xattn_in['bo'], 'L3_attn_W_qkv': _L3_attn_in['W_qkv'], 'L3_attn_W_out': _L3_attn_in['W_out'], 'L3_ffn_Win': _L3_ffn_in['Win'], 'L3_ffn_bin_': _L3_ffn_in['bin_'], 'L3_ffn_W1': _L3_ffn_in['W1'], 'L3_ffn_b1': _L3_ffn_in['b1'], 'L3_ffn_W2': _L3_ffn_in['W2'], 'L3_ffn_b2': _L3_ffn_in['b2'], 'L3_ffn_Wout': _L3_ffn_in['Wout'], 'L3_ffn_bout': _L3_ffn_in['bout']}

def reference(x, ctx_768, L0_xattn_Wq, L0_xattn_bq, L0_xattn_Wk, L0_xattn_bk, L0_xattn_Wv, L0_xattn_bv, L0_attn_Wc_down, L0_attn_Wq_up, L0_attn_Wkv_up, L0_attn_Wc_proj, L0_ffn_gate_w, L0_ffn_w1, L0_ffn_w2, L1_xattn_Wq, L1_xattn_Wk, L1_xattn_Wv, L1_xattn_Wo, L1_xattn_bo, L1_attn_Wq, L1_attn_bq, L1_attn_Wk, L1_attn_bk, L1_attn_Wv, L1_attn_bv, L1_attn_Wr, L1_attn_br, L1_attn_Wo, L1_attn_bo, L1_ffn_w_router, L1_ffn_w_fc, L1_ffn_w_gate, L1_ffn_w_proj, L2_xattn_Wq, L2_xattn_Wk, L2_xattn_Wv, L2_xattn_Wo, L2_xattn_bo, L2_attn_Wq, L2_attn_Wk, L2_attn_Wv, L2_attn_Wo, L2_ffn_waff, L2_ffn_W1, L2_ffn_b1, L2_ffn_W2, L2_ffn_b2, L2_ffn_affinity_threshold, L3_xattn_ln1_g, L3_xattn_ln1_b, L3_xattn_ln2_g, L3_xattn_ln2_b, L3_xattn_Wq, L3_xattn_bq, L3_xattn_Wk, L3_xattn_bk, L3_xattn_Wv, L3_xattn_bv, L3_xattn_Wo, L3_xattn_bo, L3_attn_W_qkv, L3_attn_W_out, L3_ffn_Win, L3_ffn_bin_, L3_ffn_W1, L3_ffn_b1, L3_ffn_W2, L3_ffn_b2, L3_ffn_Wout, L3_ffn_bout):
    import jax
    import jax.numpy as jnp

    def _L0_xattn_ref(image_features, text_features, Wq, bq, Wk, bk, Wv, bv):
        import jax, jax.numpy as jnp
        import numpy as np
        IMG_DIM, TXT_DIM, HID = (256, 192, 256)
        B, LQ, LK = (8, 512, 512)
        query = jnp.einsum('bqi,ih->bqh', image_features, Wq) + bq
        key = jnp.einsum('bkt,th->bkh', text_features, Wk) + bk
        value = jnp.einsum('bkt,th->bkh', text_features, Wv) + bv
        scale = 1.0 / jnp.sqrt(jnp.asarray(HID, query.dtype))
        scores = jnp.einsum('bqh,bkh->bqk', query, key) * scale
        weights = jax.nn.softmax(scores, axis=-1)
        attended = jnp.einsum('bqk,bkh->bqh', weights, value)
        return attended

    def _L0_attn_ref(x, Wc_down, Wq_up, Wkv_up, Wc_proj):
        import jax, jax.numpy as jnp
        import numpy as np
        N_EMBD = 256
        N_HEAD = 16
        HEAD_DIM = N_EMBD // N_HEAD
        LATENT_DIM = N_EMBD // 2
        B, T = (4, 512)
        Bsz, Tlen, C = x.shape
        latent = x @ Wc_down
        q = (latent @ Wq_up).reshape(Bsz, Tlen, N_HEAD, HEAD_DIM)
        kv = latent @ Wkv_up
        k, v = (kv[..., :HEAD_DIM], kv[..., HEAD_DIM:])
        scale = 1.0 / np.sqrt(HEAD_DIM)
        att = jnp.einsum('bthd,bsd->bhts', q, k) * scale
        causal = jnp.tril(jnp.ones((Tlen, Tlen), dtype=bool))
        att = jnp.where(causal[None, None], att, -jnp.inf)
        att = jax.nn.softmax(att, axis=-1)
        y = jnp.einsum('bhts,bsd->bthd', att, v).reshape(Bsz, Tlen, C)
        return y @ Wc_proj

    def _L0_ffn_ref(x, gate_w, w1, w2):
        import jax, jax.numpy as jnp
        import numpy as np
        N, T, D = (4, 1024, 256)
        NUM_EXPERTS = 8
        EXPERT_CAP = 2.0
        MLP_RATIO = 4
        HIDDEN = MLP_RATIO * D
        x = x.astype(jnp.float32)
        n, t, d = x.shape
        k = int(EXPERT_CAP * t / NUM_EXPERTS)
        scores = jnp.einsum('ntd,de->nte', x, gate_w)
        probs = jax.nn.softmax(scores, axis=-1)
        probs = jnp.transpose(probs, (0, 2, 1))
        g, m = jax.lax.top_k(probs, k)
        xin = jax.vmap(lambda xb, mb: xb[mb])(x, m)
        h = jax.nn.gelu(jnp.einsum('nekd,edf->nekf', xin, w1))
        h = jnp.einsum('nekf,efd->nekd', h, w2)
        weighted = g[..., None] * h
        flat_idx = (m + jnp.arange(n, dtype=m.dtype)[:, None, None] * t).reshape(-1)
        out = jnp.zeros((n * t, d), dtype=jnp.float32).at[flat_idx].add(weighted.reshape(-1, d))
        out = out.reshape(n, t, d)
        return out.astype(jnp.bfloat16)

    def _L1_xattn_ref(hidden_states, encoder_hidden_states, Wq, Wk, Wv, Wo, bo):
        import jax, jax.numpy as jnp
        import numpy as np
        HEADS = 16
        DIM_HEAD = 64
        B, S, D = hidden_states.shape
        K = encoder_hidden_states.shape[1]
        H, Dh = (HEADS, DIM_HEAD)
        scale = 1.0 / np.sqrt(Dh)
        q = hidden_states @ Wq
        k = encoder_hidden_states @ Wk
        v = encoder_hidden_states @ Wv
        q = q.reshape(B, S, H, Dh).transpose(0, 2, 1, 3)
        k = k.reshape(B, K, H, Dh).transpose(0, 2, 1, 3)
        v = v.reshape(B, K, H, Dh).transpose(0, 2, 1, 3)
        scores = jnp.einsum('bhsd,bhkd->bhsk', q, k) * scale
        probs = jax.nn.softmax(scores, axis=-1)
        out = jnp.einsum('bhsk,bhkd->bhsd', probs, v)
        out = out.transpose(0, 2, 1, 3).reshape(B, S, H * Dh)
        out = out @ Wo + bo
        return out

    def _L1_attn_ref(x, Wq, bq, Wk, bk, Wv, bv, Wr, br, Wo, bo):
        import jax, jax.numpy as jnp
        import numpy as np
        import math
        D_MODEL = 256
        N_HEADS = 16
        HEAD_DIM = D_MODEL // N_HEADS
        ROT_DIM = min(32, D_MODEL // 4)

        def _xavier(key, fan_in, fan_out):
            lim = math.sqrt(6.0 / (fan_in + fan_out))
            return jax.random.uniform(key, (fan_in, fan_out), jnp.float32, -lim, lim)
        B, S, _ = x.shape
        H, Dh, Dr = (N_HEADS, HEAD_DIM, ROT_DIM)
        q = (x @ Wq + bq).reshape(B, S, H, Dh)
        k = (x @ Wk + bk).reshape(B, S, H, Dh)
        v = (x @ Wv + bv).reshape(B, S, H, Dh)
        r = (x @ Wr + br).reshape(B, S, H, Dr)
        q = jnp.concatenate([q, r], axis=-1)
        k = jnp.concatenate([k, r], axis=-1)
        scale = 1.0 / math.sqrt(Dh + Dr)
        scores = jnp.einsum('bqhd,bkhd->bhqk', q * scale, k)
        attn = jax.nn.softmax(scores, axis=-1)
        out = jnp.einsum('bhqk,bkhd->bqhd', attn, v).reshape(B, S, H * Dh)
        return out @ Wo + bo

    def _L1_ffn_ref(x, w_router, w_fc, w_gate, w_proj):
        import jax, jax.numpy as jnp
        import numpy as np
        E = 16
        K = 2
        LOAD = 1.0

        def _dispatch(xb, pb, cap):
            T, C = xb.shape
            top_k_probs, ei = jax.lax.top_k(pb, K)
            flat = ei.swapaxes(0, 1).ravel()
            one_hot = jax.nn.one_hot(flat, E, dtype=jnp.int32)
            pos = jnp.cumsum(one_hot, axis=0) * one_hot
            pos = pos.reshape(K, T, E).swapaxes(0, 1)
            pos = jnp.max(pos, axis=-1) - 1
            ei2 = flat.reshape(K, T).swapaxes(0, 1)
            xr = jnp.repeat(xb, K, axis=0)
            buf = jnp.zeros((E, cap, C), xb.dtype)
            buf = buf.at[ei2.ravel(), pos.ravel()].set(xr, mode='drop')
            return (top_k_probs, pos, ei2, buf)

        def _collect(eo_b, ei_b, pos_b, tk_b):
            out = eo_b[ei_b, pos_b]
            return jnp.sum(tk_b[..., None] * out, axis=1)
        B, T, C = x.shape
        cap = int(LOAD * K * max(1, T / E))
        g = jnp.einsum('btc,ce->bte', x, w_router)
        gate_probs = jax.nn.softmax(g, axis=-1)
        top_k_probs, positions, indices, expert_inputs = jax.vmap(lambda xb, pb: _dispatch(xb, pb, cap))(x, gate_probs)
        expert_inputs = jnp.swapaxes(expert_inputs, 0, 1).reshape(E, B * cap, C)
        gg = jnp.einsum('enc,ech->enh', expert_inputs, w_gate)
        h = jnp.einsum('enc,ech->enh', expert_inputs, w_fc)
        h = jax.nn.silu(gg) * h
        o = jnp.einsum('enh,ehc->enc', h, w_proj)
        expert_outputs = jnp.swapaxes(o.reshape(E, B, cap, C), 0, 1)
        y = jax.vmap(_collect)(expert_outputs, indices, positions, top_k_probs)
        return y

    def _L2_xattn_ref(x, context, Wq, Wk, Wv, Wo, bo):
        import jax, jax.numpy as jnp
        import numpy as np
        HEADS = 16
        DIM_HEAD = 64
        b, n, _ = x.shape
        h, d = (HEADS, DIM_HEAD)
        scale = d ** (-0.5)
        q = (x @ Wq).reshape(b, n, h, d).transpose(0, 2, 1, 3)
        k = (context @ Wk).reshape(b, -1, h, d).transpose(0, 2, 1, 3)
        v = (context @ Wv).reshape(b, -1, h, d).transpose(0, 2, 1, 3)
        sim = jnp.einsum('bhid,bhjd->bhij', q, k) * scale
        attn = jax.nn.softmax(sim, axis=-1)
        out = jnp.einsum('bhij,bhjd->bhid', attn, v)
        out = out.transpose(0, 2, 1, 3).reshape(b, n, h * d)
        return out @ Wo + bo

    def _L2_attn_ref(x, Wq, Wk, Wv, Wo):
        import jax, jax.numpy as jnp
        import numpy as np
        SEQ_LEN = 512
        DIM_EMB = 256
        DIM_K = 256
        DIM_V = 256
        BATCH = 4
        q = jnp.einsum('bse,ek->bsk', x, Wq)
        k = jnp.einsum('bse,ek->bsk', x, Wk)
        v = jnp.einsum('bse,ev->bsv', x, Wv)
        scores = jnp.einsum('bqk,bsk->bqs', q, k)
        S = scores.shape[-1]
        causal_mask = jnp.triu(jnp.ones((S, S), dtype=bool), k=1)
        scores = jnp.where(causal_mask[None], -jnp.inf, scores)
        attn = jax.nn.softmax(scores * Wq.shape[1] ** (-0.5), axis=-1)
        out = jnp.einsum('bqs,bsv->bqv', attn, v)
        return jnp.einsum('bqv,vo->bqo', out, Wo)

    def _L2_ffn_ref(inputs, waff, W1, b1, W2, b2, affinity_threshold):
        import jax, jax.numpy as jnp
        import numpy as np
        B, S, D, E, F = (4, 512, 256, 8, 1024)
        MIN_CAPACITY = 4

        def _make_waff():
            g = D // E
            scale = E / D
            w = np.zeros((E, D), np.float32)
            for i in range(E):
                w[i, i * g:(i + 1) * g] = scale
            return jnp.asarray(w)
        num = jnp.einsum('bsd,ed->bse', inputs, waff)
        x_norm = jnp.linalg.norm(inputs, axis=-1, keepdims=True)
        w_norm = jnp.linalg.norm(waff, axis=-1)
        aff = num / (x_norm * w_norm[None, None, :] + 1e-09)
        router_probs = jax.nn.softmax(aff, axis=-1)
        cap = jnp.floor(S * jax.nn.sigmoid(aff.mean() - affinity_threshold)).astype(jnp.int32)
        cap = jnp.minimum(jnp.maximum(cap, MIN_CAPACITY), S)
        tcr = jax.nn.one_hot(jnp.argmax(router_probs, axis=-1), E, dtype=inputs.dtype)
        order = jnp.argsort(-aff, axis=1)
        ranks = jnp.argsort(order, axis=1)
        ecr = (ranks < cap).astype(inputs.dtype)
        dispatch = tcr * ecr
        masks = jnp.moveaxis(dispatch, -1, 0)

        def body(acc, expert):
            W1e, b1e, W2e, b2e, me = expert
            xi = inputs * me[..., None]
            h = jax.nn.gelu(xi @ W1e + b1e, approximate=False)
            return (acc + (h @ W2e + b2e), None)
        out, _ = jax.lax.scan(body, jnp.zeros_like(inputs), (W1, b1, W2, b2, masks))
        return out

    def _L3_xattn_ref(modality1, modality2, ln1_g, ln1_b, ln2_g, ln2_b, Wq, bq, Wk, bk, Wv, bv, Wo, bo):
        import jax, jax.numpy as jnp
        import numpy as np
        EPS = 1e-05

        def layernorm(x, g, b):
            mu = jnp.mean(x, axis=-1, keepdims=True)
            var = jnp.mean(jnp.square(x - mu), axis=-1, keepdims=True)
            return (x - mu) * jax.lax.rsqrt(var + EPS) * g + b
        E = Wq.shape[1]
        scaling = E ** (-0.5)
        x1 = layernorm(modality1, ln1_g, ln1_b)
        x2 = layernorm(modality2, ln2_g, ln2_b)
        q = x1 @ Wq + bq
        k = x2 @ Wk + bk
        v = x2 @ Wv + bv
        scores = jnp.einsum('bqe,bke->bqk', q, k) * scaling
        attn = jax.nn.softmax(scores, axis=-1)
        ctx = jnp.einsum('bqk,bke->bqe', attn, v)
        return ctx @ Wo + bo

    def _L3_attn_ref(x, W_qkv, W_out):
        import jax, jax.numpy as jnp
        import numpy as np
        B, S, H = (8, 512, 256)
        h = x.shape[-1]
        scale = 1.0 / np.sqrt(h).astype(np.float32)
        y = jnp.einsum('bsh,oh->bso', x, W_qkv).reshape(*x.shape, 3)
        q, k, v = (y[..., 0], y[..., 1], y[..., 2])
        scores = jnp.einsum('bqh,bkh->bqk', q, k) * scale
        attn = jax.nn.softmax(scores, axis=-1)
        ctx = jnp.einsum('bqk,bkh->bqh', attn, v)
        out = jnp.einsum('bsh,oh->bso', ctx, W_out)
        return out

    def _L3_ffn_ref(x, Win, bin_, W1, b1, W2, b2, Wout, bout):
        import jax, jax.numpy as jnp
        import numpy as np
        D_MODEL = 256
        M = 64
        INNER = 16
        s = jnp.einsum('btd,dm->btm', x, Win) + bin_
        h = jax.nn.relu(s[..., None] * W1 + b1)
        g = jnp.einsum('btmh,mh->btm', h, W2) + b2
        out = jnp.einsum('btm,md->btd', g, Wout) + bout
        return out
    x = x + _L0_xattn_ref(_layernorm(x, axis=-1), ctx_768, L0_xattn_Wq, L0_xattn_bq, L0_xattn_Wk, L0_xattn_bk, L0_xattn_Wv, L0_xattn_bv)
    x = x + _L0_attn_ref(_layernorm(x, axis=-1), L0_attn_Wc_down, L0_attn_Wq_up, L0_attn_Wkv_up, L0_attn_Wc_proj)
    x = x + _L0_ffn_ref(_layernorm(x, axis=-1), L0_ffn_gate_w, L0_ffn_w1, L0_ffn_w2)
    x = x + _L1_xattn_ref(_layernorm(x, axis=-1), ctx_768, L1_xattn_Wq, L1_xattn_Wk, L1_xattn_Wv, L1_xattn_Wo, L1_xattn_bo)
    x = x + _L1_attn_ref(_layernorm(x, axis=-1), L1_attn_Wq, L1_attn_bq, L1_attn_Wk, L1_attn_bk, L1_attn_Wv, L1_attn_bv, L1_attn_Wr, L1_attn_br, L1_attn_Wo, L1_attn_bo)
    x = x + _L1_ffn_ref(_layernorm(x, axis=-1), L1_ffn_w_router, L1_ffn_w_fc, L1_ffn_w_gate, L1_ffn_w_proj)
    x = x + _L2_xattn_ref(_layernorm(x, axis=-1), ctx_768, L2_xattn_Wq, L2_xattn_Wk, L2_xattn_Wv, L2_xattn_Wo, L2_xattn_bo)
    x = x + _L2_attn_ref(_layernorm(x, axis=-1), L2_attn_Wq, L2_attn_Wk, L2_attn_Wv, L2_attn_Wo)
    x = x + _L2_ffn_ref(_layernorm(x, axis=-1), L2_ffn_waff, L2_ffn_W1, L2_ffn_b1, L2_ffn_W2, L2_ffn_b2, L2_ffn_affinity_threshold)
    x = x + _L3_xattn_ref(_layernorm(x, axis=-1), ctx_768, L3_xattn_ln1_g, L3_xattn_ln1_b, L3_xattn_ln2_g, L3_xattn_ln2_b, L3_xattn_Wq, L3_xattn_bq, L3_xattn_Wk, L3_xattn_bk, L3_xattn_Wv, L3_xattn_bv, L3_xattn_Wo, L3_xattn_bo)
    x = x + _L3_attn_ref(_layernorm(x, axis=-1), L3_attn_W_qkv, L3_attn_W_out)
    x = x + _L3_ffn_ref(_layernorm(x, axis=-1), L3_ffn_Win, L3_ffn_bin_, L3_ffn_W1, L3_ffn_b1, L3_ffn_W2, L3_ffn_b2, L3_ffn_Wout, L3_ffn_bout)
    return x

_drawn_inputs = setup_inputs


def setup_inputs(seed=0):
    import zlib

    import numpy as np

    out = dict(_drawn_inputs(seed))
    spreads = {'L1_attn_bq': (0.0, 0.8),
     'L1_attn_bk': (0.0, 2.0),
     'L1_attn_bv': (0.0, 0.1),
     'L1_attn_br': (0.0, 0.319),
     'L1_attn_bo': (0.0, 0.1),
     'L2_ffn_b1': (0.0, 0.1),
     'L2_ffn_b2': (0.0, 0.1),
     'L3_xattn_ln1_g': (1.0, 0.6),
     'L3_xattn_ln1_b': (0.0, 0.796),
     'L3_xattn_ln2_g': (1.0, 0.2),
     'L3_xattn_ln2_b': (0.0, 0.1)}
    factors = {'L0_xattn_bq': 2.812,
     'L0_xattn_bk': 64.0,
     'L1_ffn_w_router': 8.0,
     'L1_ffn_w_fc': 8.0,
     'L1_ffn_w_gate': 8.0,
     'L1_ffn_w_proj': 8.0,
     'L3_xattn_bq': 64.0,
     'L3_xattn_bk': 64.0,
     'L3_xattn_bv': 8.0,
     'L3_xattn_bo': 8.0,
     'L3_ffn_bin_': 31.017}
    for name, (base, spread) in spreads.items():
        noise = np.random.default_rng([zlib.crc32(name.encode()), seed]).standard_normal(out[name].shape)
        drawn = base * np.exp(spread * noise) if base else spread * noise
        out[name] = jnp.asarray(drawn.astype(out[name].dtype))
    for name, factor in factors.items():
        out[name] = (out[name] * factor).astype(out[name].dtype)
    return out
```

```python
import numpy as np
import concourse.bass as bass
from concourse import mybir
from contextlib import ExitStack

F32 = mybir.dt.float32
BF16 = mybir.dt.bfloat16
ALU = mybir.AluOpType
ACT = mybir.ActivationFunctionType
X = mybir.AxisListType.X

B, S, D = 8, 64, 256
LK, DC = 1024, 192
TOK = B * S
NT = TOK // 128
KT = LK // 128
D2 = DC - 128
HB, DHB = 16, 64
NPAIR = HB // 2
LAYERS = 12
CAP = 512

SLOT = 2048
NSLOT = 5

UNITS = ["L0x_a", "L0x_b", "L0a_a", "L0a_b"]
UNITS += [f"L0f_{e}_{w}" for e in range(8) for w in ("w1", "w2")]
UNITS += ["L1x_q", "L1x_k0", "L1x_k1", "L1x_v", "L1x_o", "L1a_q", "L1a_k", "L1a_v"]
UNITS += [f"L1f_g{g}" for g in range(4)] + [f"L1f_p{g}" for g in range(2)]
UNITS += ["L2x_q", "L2x_k0", "L2x_k1", "L2x_v", "L2x_o", "L2a", "L2f_b2"]
UNITS += [f"L2f_{e}_{w}" for e in range(8) for w in ("w1", "w2")]
UNITS += ["L3x_a", "L3x_b", "L3a", "L3f"]
UIDX = {u: n for n, u in enumerate(UNITS)}

CW = {}
_at = 0
for _name, _width in (
    ("ident", 128), ("ones", 128), ("same", 128), ("tri", 128), ("delta", 64), ("causal", 64),
    ("bcausal", 128), ("bfull", 128), ("before", 64), ("slot32", 32), ("slot16", 16), ("rev8", 8),
    ("rev16", 16), ("nhalf", 64), ("half", 8),
    ("L0x_bq", 2), ("L1a_bq", 8), ("L1a_bk", 8), ("L2f_b1", 64), ("L2f_waff", 16), ("L2f_thr", 1),
    ("L0f_gate", 16), ("L1f_router", 32),
    ("L3x_g1", 2), ("L3x_b1", 2), ("L3x_g2", 2), ("L3x_b2", 2), ("L3x_bq", 2), ("L3x_bk", 2),
    ("L3f_bin", 1), ("L3f_W1", 16), ("L3f_b1", 16), ("L3f_W2", 16), ("L3f_b2", 1),
):
    CW[_name] = (_at, _width)
    _at += _width
NCONST = _at


def build(nc, widths, units_d, const_d, ctxT1_d, ctxT2_d, ctxN_d, x_d, out_d):
    ctx = ExitStack()
    with ctx:
        sem = lambda name: ctx.enter_context(nc.semaphore(name))
        consts_loaded, out_stored, x_final, x_loaded = sem("consts_loaded"), sem("out_stored"), sem("x_final"), sem("x_loaded")
        units_used = sem("units_used")
        dve_step, pool_step = sem("dve_step"), sem("pool_step")
        ln_T, ln_rstd, ln_stats, ln_xn = sem("ln_T"), sem("ln_rstd"), sem("ln_stats"), sem("ln_xn")
        ln_xnT_act, ln_xnT_dve = sem("ln_xnT_act"), sem("ln_xnT_dve")
        layer_out = sem("layer_out")
        xa_A, xa_As, xa_O, xa_OT = sem("xa_A"), sem("xa_As"), sem("xa_O"), sem("xa_OT")
        xa_P, xa_PT_act, xa_PT_dve, xa_S = sem("xa_P"), sem("xa_PT_act"), sem("xa_PT_dve"), sem("xa_S")
        xa_T, xa_Z, xa_ZT, xa_ZTs = sem("xa_T"), sem("xa_Z"), sem("xa_ZT"), sem("xa_ZTs")
        xa_Zs, xa_max, xa_q, xa_qs_act = sem("xa_Zs"), sem("xa_max"), sem("xa_q"), sem("xa_qs_act")
        xa_qs_dve, xa_recip = sem("xa_qs_dve"), sem("xa_recip")
        na_A, na_A1_scaled, na_As_act, na_As_dve = sem("na_A"), sem("na_A1_scaled"), sem("na_As_act"), sem("na_As_dve")
        na_P, na_PT_act, na_PT_dve, na_S = sem("na_P"), sem("na_PT_act"), sem("na_PT_dve"), sem("na_S")
        na_T, na_Z, na_ZT, na_ZTs = sem("na_T"), sem("na_Z"), sem("na_ZT"), sem("na_ZTs")
        na_Zs, na_kb, na_kbs, na_max = sem("na_Zs"), sem("na_kb"), sem("na_kbs"), sem("na_max")
        na_ones, na_q, na_qs_act, na_qs_dve = sem("na_ones"), sem("na_q"), sem("na_qs_act"), sem("na_qs_dve")
        na_v, na_vs_act, na_vs_dve = sem("na_v"), sem("na_vs_act"), sem("na_vs_dve")
        sa_P, sa_PT, sa_S, sa_T = sem("sa_P"), sem("sa_PT"), sem("sa_S"), sem("sa_T")
        sa_d, sa_exp, sa_k, sa_k0 = sem("sa_d"), sem("sa_exp"), sem("sa_k"), sem("sa_k0")
        sa_ks0, sa_ks_act, sa_ks_dve, sa_lat = sem("sa_ks0"), sem("sa_ks_act"), sem("sa_ks_dve"), sem("sa_lat")
        sa_lats, sa_q, sa_qs_act, sa_qs_dve = sem("sa_lats"), sem("sa_q"), sem("sa_qs_act"), sem("sa_qs_dve")
        sa_v, sa_vs, sa_y, sa_ys_act = sem("sa_v"), sem("sa_vs"), sem("sa_y"), sem("sa_ys_act")
        sa_ys_dve = sem("sa_ys_dve")
        s1_P, s1_PT, s1_S, s1_T = sem("s1_P"), sem("s1_PT"), sem("s1_S"), sem("s1_T")
        s1_d, s1_exp, s1_k, s1_ks = sem("s1_d"), sem("s1_exp"), sem("s1_k"), sem("s1_ks")
        s1_o, s1_os_act, s1_os_dve, s1_q = sem("s1_o"), sem("s1_os_act"), sem("s1_os_dve"), sem("s1_q")
        s1_qs, s1_v, s1_vs, s1_vs_dve = sem("s1_qs"), sem("s1_v"), sem("s1_vs"), sem("s1_vs_dve")
        comb_T, comb_Ts, gathered, rk_diag = sem("comb_T"), sem("comb_Ts"), sem("gathered"), sem("rk_diag")
        rk_spread, router_d = sem("rk_spread"), sem("router_d")
        router_exp, router_logits = sem("router_exp"), sem("router_logits")
        xin_act, xin_dve = sem("xin_act"), sem("xin_dve")
        L0f_h, L0f_hs, L0f_sel, L0f_y = sem("L0f_h"), sem("L0f_hs"), sem("L0f_sel"), sem("L0f_y")
        L0f_ys = sem("L0f_ys")
        L1f_comb, L1f_cum, L1f_disp, L1f_gate = sem("L1f_comb"), sem("L1f_cum"), sem("L1f_disp"), sem("L1f_gate")
        L1f_hot, L1f_hs, L1f_o, L1f_oT = sem("L1f_hot"), sem("L1f_hs"), sem("L1f_o"), sem("L1f_oT")
        L1f_ons_act, L1f_ons_dve = sem("L1f_ons_act"), sem("L1f_ons_dve")
        L1f_os_act, L1f_os_dve = sem("L1f_os_act"), sem("L1f_os_dve")
        L1f_silu, L1f_up = sem("L1f_silu"), sem("L1f_up")
        L2f_diag, L2f_h, L2f_hs, L2f_mean = sem("L2f_diag"), sem("L2f_h"), sem("L2f_hs"), sem("L2f_mean")
        L2f_norms, L2f_norms2, L2f_rowsum, L2f_sig = sem("L2f_norms"), sem("L2f_norms2"), sem("L2f_rowsum"), sem("L2f_sig")
        L2f_total, L2f_w2, L2f_wn, L2f_xi = sem("L2f_total"), sem("L2f_w2"), sem("L2f_wn"), sem("L2f_xi")
        L2f_xis_act, L2f_xis_dve, L2f_y = sem("L2f_xis_act"), sem("L2f_xis_dve"), sem("L2f_y")
        ctx_T, ctx_Ts_act, ctx_Ts_dve, ctx_n = sem("ctx_T"), sem("ctx_Ts_act"), sem("ctx_Ts_dve"), sem("ctx_n")
        L3f_acc, L3f_relu, L3f_s, L3f_ss = sem("L3f_acc"), sem("L3f_relu"), sem("L3f_s"), sem("L3f_ss")
        slot_loaded = [sem(f"slot{n}_loaded") for n in range(NSLOT)]
        ctx_loaded = [sem(f"ctx{i}_loaded") for i in range(NT)]

        sb = lambda name, shape, dt=F32: ctx.enter_context(nc.sbuf_tensor(name, shape, dt))
        ctxT1 = sb("ctxT1_sb", [128, B * LK])
        ctxT2 = sb("ctxT2_sb", [D2 + 1, B * LK])
        ctxN = sb("ctxN_sb", [128, B * KT, DC])
        ring = sb("ring", [128, NSLOT, SLOT])
        cst = sb("cst", [128, NCONST])
        x = sb("x", [128, NT, D])
        xn = sb("xn", [128, NT, D])
        xnT = sb("xnT", [128, 2, TOK])
        WORK = 9800
        wk = sb("wk", [128, WORK])
        ps = ctx.enter_context(nc.psum_tensor("ps", [128, 8, 512], F32))

        PE, DVE, ACTE, POOL = nc.tensor, nc.vector, nc.scalar, nc.gpsimd

        def C(name, rows=slice(0, 128)):
            at, width = CW[name]
            return cst[rows, at:at + width]

        def wv(at, *dims, rows=slice(0, 128)):
            n = int(np.prod(dims))
            assert at + n <= WORK
            ap = wk[rows, at:at + n]
            if len(dims) == 2:
                ap = ap.rearrange("p (a b) -> p a b", b=dims[1])
            if len(dims) == 3:
                ap = ap.rearrange("p (a b c) -> p a b c", b=dims[1], c=dims[2])
            if len(dims) == 4:
                ap = ap.rearrange("p (a b c d) -> p a b c d", b=dims[1], c=dims[2], d=dims[3])
            return ap

        def unit(name, at, *dims, rows=slice(0, 128)):
            n = int(np.prod(dims))
            assert at + n <= widths[name], (name, at, dims)
            ap = ring[rows, UIDX[name] % NSLOT, at:at + n]
            if len(dims) == 2:
                ap = ap.rearrange("p (a b) -> p a b", b=dims[1])
            if len(dims) == 3:
                ap = ap.rearrange("p (a b c) -> p a b c", b=dims[1], c=dims[2])
            return ap

        def bank(n, *dims, rows=slice(0, 128), at=0):
            m = int(np.prod(dims))
            nb = max(1, (at + m + 511) // 512)
            ap = ps[rows, n:n + nb, :].rearrange("p a b -> p (a b)")[:, at:at + m]
            if len(dims) == 2:
                ap = ap.rearrange("p (a b) -> p a b", b=dims[1])
            if len(dims) == 3:
                ap = ap.rearrange("p (a b c) -> p a b c", b=dims[1], c=dims[2])
            if len(dims) == 4:
                ap = ap.rearrange("p (a b c d) -> p a b c d", b=dims[1], c=dims[2], d=dims[3])
            return ap

        def half(par):
            return slice(64 * par, 64 * par + 64)

        def mm(out, lhsT, rhs, start=True, stop=True):
            return PE.matmul(out, lhsT, rhs, start=start, stop=stop)

        ident = C("ident")

        st6 = sb("st6", [128, NT, 6])
        mv = sb("mv", [128, NT, 2])
        rstd = sb("rstd", [128, 2 * NT])
        XQ = wv(0, NPAIR, TOK)
        XP = wv(4096, 2, 1024)
        XPT = wv(6144, 2, KT, 128)
        XA = wv(8192, 2, 256)
        XZ = wv(8704, 2, DC)
        XZT = wv(9088, 2, 256)
        XNM, XRS, XRI = wv(9600, 4), wv(9604, 4), wv(9608, 4)
        NA1, NA2 = wv(0, TOK), wv(512, TOK)
        NQ = wv(1024, 2, TOK)
        NZT1, NZT2 = wv(2048, TOK), wv(2560, TOK)
        NV = wv(3072, 2, TOK)
        QC, KC = wv(0, 8, 256), wv(2048, 8, 256)
        VB = wv(4096, 4, 8, 32)
        LAT = wv(5120, TOK)
        SC = wv(5632, 2, 512)
        PT = wv(6656, 2, 512)
        YT = wv(7680, 2, TOK)
        AMX, ASM, ARC = wv(8704, 2, 8), wv(8720, 2, 8), wv(8736, 2, 8)
        SQ, SK = wv(0, 2, TOK), wv(1024, 2, TOK)
        SV = wv(2048, NT, D)
        SS = wv(3072, NT, 128)
        SPT = wv(3584, NT, 128)
        SO = wv(4096, 2, TOK)
        SMX, SSM, SRC = wv(5120, NT), wv(5124, NT), wv(5128, NT)
        RP = wv(9616, NT, 8)
        RK = wv(9648, NT, 8)
        RA, RB_, RC_ = wv(9680, 4), wv(9684, 4), wv(9688, 4)
        RL = wv(9692, NT, 8)
        ROH = wv(9724, NT, 8)
        RT = wv(9756, NT, 8)
        RS1 = wv(9788, 8)
        RDL = wv(7232, 8, 64)
        RG, RE = wv(5184, 8, 64), wv(5696, 8, 64)
        SEL = wv(64, NT, 8, 32)
        SELG = wv(1088, 8, NT, 32)
        SGT = wv(2112, 8, 128)
        XIN = wv(3136, 2, 8, NT, 32)
        HT0 = wv(5184, 2, 8, 128)
        YS = wv(7232, 8, D)
        TP = wv(0, NT, 16)
        TOH1, TOH2, TQ1, TQ2 = wv(64, NT, 16), wv(128, NT, 16), wv(192, NT, 16), wv(256, NT, 16)
        TT, TU = wv(320, NT, 16), wv(384, NT, 16)
        TM1, TM2, TV = wv(448, NT), wv(452, NT), wv(456, NT)
        TD = wv(1024, NT, 16, 16)
        TC = wv(2048, NT, 16, 16)
        TX_ = wv(6144, NT, 16, 16)
        TCT = wv(3072, NT, 2, 128)
        TXIN = wv(4096, 2, 16, NT, 16)
        TSG = wv(6144, 2, 512)
        THT = wv(7168, 16, 64)
        TOT = wv(4096, 2, NT, 16, 16)
        TON = wv(6144, NT, 2, D)
        EXI = wv(0, 2, 2, TOK)
        EDG = wv(2048, 2, NT, 128)
        EH = wv(3072, 4, TOK)
        FS, FT, FG_ = wv(0, 256), wv(256, 4, 256), wv(1280, 256)

        CST6 = wv(4096, B * KT, 6)
        CMV = wv(4096 + 6 * B * KT, B * KT, 2)
        CRS = wv(4096 + 8 * B * KT, B * KT)
        LN = {l: l for l in range(9)} | {"c": 9, 9: 10, "9b": 11, 10: 12, 11: 13}
        LNX = {l: l for l in range(10)} | {"9b": 10, 10: 11, 11: 12}
        LNT = {l: l for l in range(9)} | {"9b": 9, 10: 10, 11: 11}

        block = ctx.enter_context(nc.Block())

        @block.sync
        def _(sp):
            sp.dma_start(x[:, :, :], x_d).then_inc(x_loaded, 16)
            sp.dma_start(cst[:, :], const_d).then_inc(consts_loaded, 16)
            at = 0

            def load(n):
                nonlocal at
                name = UNITS[n]
                if n >= NSLOT:
                    sp.wait_ge(units_used, n - NSLOT + 1)
                w = widths[name]
                sp.dma_start(ring[:, n % NSLOT, 0:w], units_d[at:at + 128 * w].rearrange("(p w) -> p w", p=128)) \
                    .then_inc(slot_loaded[n % NSLOT], 16)
                at += 128 * w

            load(0)
            load(1)
            for i in range(NT):
                k = slice(2 * i * LK, (2 * i + 2) * LK)
                t = slice(2 * i * KT, (2 * i + 2) * KT)
                sp.dma_start(ctxT1[:, k], ctxT1_d[:, k]).then_inc(ctx_loaded[i], 16)
                sp.dma_start(ctxT2[:, k], ctxT2_d[:, k]).then_inc(ctx_loaded[i], 16)
                sp.dma_start(ctxN[:, t, :], ctxN_d[:, t, :]).then_inc(ctx_loaded[i], 16)
            for n in range(2, len(UNITS)):
                load(n)
            sp.wait_ge(x_final, NT)
            sp.dma_start(out_d, x[:, :, :]).then_inc(out_stored, 16)
            sp.wait_ge(out_stored, 16)

        @block.gpsimd
        def _(pool):
            pool.wait_ge(consts_loaded, 16)

            def rsqrt(n, src, dst, cols, eps):
                pool.wait_ge(ln_stats, n + 1)
                POOL.tensor_scalar(dst, src, float(eps), None, ALU.add).then_inc(pool_step, 1)
                pool.wait_ge(pool_step, n + 1)
                POOL.tensor_tensor(dst, dst, C("nhalf")[:, 0:cols], ALU.pow).then_inc(ln_rstd, 1)

            n = 0
            for l in range(LAYERS):
                if l == 9:
                    rsqrt(n, CMV[:, :, 1], CRS, B * KT, 1e-5)
                    n += 1
                rsqrt(n, mv[:, :, 1], rstd[:, 0:NT], NT, 1e-5)
                n += 1
                if l == 9:
                    rsqrt(n, mv[:, :, 1], rstd[:, 0:NT], NT, 1e-5)
                    n += 1
                if l == 8:
                    pool.wait_ge(L2f_norms2, 2)
                    POOL.tensor_tensor(RA, RA, C("half")[:, 0:NT], ALU.pow).then_inc(L2f_norms, 1)
                    POOL.tensor_tensor(RS1, RS1, C("half")[:, 0:8], ALU.pow).then_inc(L2f_norms, 1)

        @block.scalar
        def _(act):
            act.wait_ge(consts_loaded, 16)

            def layernorm(key, affine=None):
                act.wait_ge(ln_T, LNT[key] + 1)
                if affine is None:
                    ACTE.copy(xnT[:, 0, :], ps[:, 0, :]).then_inc(ln_xnT_act, 1)
                else:
                    g, b = affine
                    ACTE.activation(xnT[:, 0, :], ps[:, 0, :], ACT.Identity, scale=C(g)[:, 0:1],
                                    bias=C(b)[:, 0:1]).then_inc(ln_xnT_act, 1)

            def wide(k):
                for r in range(0, NPAIR, 2):
                    act.wait_ge(xa_q, 8 * k + r + 1)
                    ACTE.mul(XQ[:, r, :], ps[:, r, :], DHB ** -0.5).then_inc(xa_qs_act, 1)

                def queries(t, p):
                    act.wait_ge(xa_A, t + 1)
                    ACTE.copy(XA[:, p, 0:128], bank(7, 128)).then_inc(xa_As, 1)
                    ACTE.copy(XA[0:D2, p, 128:256], bank(7, 128, rows=slice(0, D2), at=128)).then_inc(xa_As, 1)

                def exp(t, r):
                    act.wait_ge(xa_max, t + 1)
                    if not (isinstance(t, int) and t - 64 * k < 2):
                        act.wait_ge(xa_T, 2 * t - 2)
                    ACTE.activation(XP[:, r % 2, :], bank(2 * (r % 2), 1024), ACT.Exp, bias=XNM[:, r % 4:r % 4 + 1],
                                    accum_out=XRS[:, r % 4:r % 4 + 1]).then_inc(xa_P, 1)

                def spread(t, r, first):
                    act.wait_ge(xa_T, 2 * t + 1)
                    if not first:
                        act.wait_ge(xa_Z, t - 1)
                    ACTE.copy(XPT[:, r % 2, 0:4, :], bank(4, 4, 128)).then_inc(xa_PT_act, 1)

                def heads(t, r, b):
                    act.wait_ge(xa_O, t + 1)
                    ACTE.copy(XQ[:, r, bass.ds(b * 64, 64)], bank(7, 64, at=256)).then_inc(xa_OT, 1)

                def batch(b, first):
                    t0 = 64 * k + 8 * b if first else b * 8 + 64 * k
                    for r in range(NPAIR):
                        if r == 0:
                            queries(t0, 0)
                            if not first:
                                spread(t0 - 1, 7, False)
                                heads(t0 - 3, 5, b - 1)
                            queries(t0 + 1, 1)
                            exp(t0, 0)
                        else:
                            if r < NPAIR - 1:
                                queries(t0 + r + 1, (r + 1) % 2)
                            exp(t0 + r, r)
                            spread(t0 + r - 1, r - 1, first and r < 3)
                            if r >= 3:
                                heads(t0 + r - 3, r - 3, b)
                            elif not first:
                                heads(t0 + r - 3, r + 5, b - 1)

                batch(0, True)
                with act.Fori(1, B) as b:
                    batch(b, False)
                t1 = 64 * (k + 1)
                spread(t1 - 1, 7, False)
                for r in (5, 6, 7):
                    heads(t1 - 8 + r, r, B - 1)

            def narrow(k):
                act.wait_ge(na_q, 2 * k + 1)
                ACTE.activation(NQ[:, 0, :], ps[:, 2, :], ACT.Identity,
                                bias=C("L0x_bq" if k == 0 else "L3x_bq")[:, 0:1]).then_inc(na_qs_act, 1)
                act.wait_ge(na_A, 2 * k + 1)
                ACTE.mul(NA1, ps[:, 4, :], D ** -0.5).then_inc(na_As_act, 1)
                if k == 1:
                    act.wait_ge(na_A1_scaled, 1)
                for i in range(NT):
                    t = 4 * k + i
                    act.wait_ge(na_max, t + 1)
                    if i >= 2:
                        act.wait_ge(na_T, 2 * t - 2)
                    ACTE.activation(XP[:, i % 2, :], bank(2 * (i % 2), 1024), ACT.Exp, bias=XNM[:, i:i + 1],
                                    accum_out=XRS[:, i:i + 1]).then_inc(na_P, 1)
                    if i >= 1:
                        u = t - 1
                        act.wait_ge(na_T, 2 * u + 1)
                        if i >= 3:
                            act.wait_ge(na_Z, u - 1)
                        ACTE.copy(XPT[:, (i - 1) % 2, 0:4, :], bank(4, 4, 128)).then_inc(na_PT_act, 1)
                act.wait_ge(na_T, 2 * (4 * k + 3) + 1)
                act.wait_ge(na_Z, 4 * k + 2)
                ACTE.copy(XPT[:, 1, 0:4, :], bank(4, 4, 128)).then_inc(na_PT_act, 1)

            def self16(k):
                scale = 0.25 if k == 0 else 48 ** -0.5
                for h in range(2):
                    for r in (0, 1, 4, 5):
                        act.wait_ge(sa_q, 8 * k + 4 * h + r // 2 + 1)
                        src = bank(r // 2, 256, at=256 * (r % 2))
                        if k == 0:
                            ACTE.copy(QC[:, r, :], src).then_inc(sa_qs_act, 1)
                        else:
                            ACTE.activation(QC[:, r, :], src, ACT.Identity,
                                            bias=C("L1a_bq")[:, r:r + 1]).then_inc(sa_qs_act, 1)
                    for r in (0, 1, 4, 5):
                        if k == 1:
                            act.wait_ge(sa_k, 4 * h + r // 2 + 1)
                            ACTE.activation(KC[:, r, :], bank(4 + r // 2, 256, at=256 * (r % 2)), ACT.Identity,
                                            bias=C("L1a_bk")[:, r:r + 1]).then_inc(sa_ks_act, 1)
                    for u in range(4):
                        t = 8 * k + 4 * h + u
                        act.wait_ge(sa_d, t + 1)
                        ACTE.activation(SC[:, u % 2, :], SC[:, u % 2, :], ACT.Exp, scale=scale).then_inc(sa_exp, 1)
                        if u >= 1:
                            act.wait_ge(sa_T, t)
                            ACTE.copy(PT[:, (u - 1) % 2, :], ps[:, 2 + (u - 1) % 2, :]).then_inc(sa_PT, 1)
                    act.wait_ge(sa_T, 8 * k + 4 * h + 4)
                    ACTE.copy(PT[:, 1, :], ps[:, 3, :]).then_inc(sa_PT, 1)
                    act.wait_ge(sa_y, 2 * k + h + 1)
                    ACTE.copy(YT[:, 0, 256 * h:256 * h + 256], ps[:, 4, 256 * h:256 * h + 256]).then_inc(sa_ys_act, 1)

            def self1(k):
                act.wait_ge(s1_q, 1 + k)
                ACTE.copy(SQ, bank(2, 2, TOK)).then_inc(s1_qs, 1)
                act.wait_ge(s1_v, 1 + k)
                ACTE.copy(SV[:, 0:2, :], bank(6, 2, D)).then_inc(s1_vs, 1)
                act.wait_ge(s1_d, 1 + k)
                ACTE.activation(SS, SS, ACT.Exp, scale=D ** -0.5).then_inc(s1_exp, 1)
                act.wait_ge(s1_T, 1 + k)
                ACTE.copy(SPT, bank(1, NT, 128)).then_inc(s1_PT, 1)
                act.wait_ge(s1_o, 1 + k)
                ACTE.copy(SO[:, 0, :], ps[:, 2, :]).then_inc(s1_os_act, 1)

            layernorm(0)
            narrow(0)
            layernorm(1)
            act.wait_ge(sa_lat, 1)
            ACTE.copy(LAT, ps[:, 2, :]).then_inc(sa_lats, 1)
            self16(0)
            layernorm(2)
            act.wait_ge(router_d, 1)
            ACTE.activation(RP, RP, ACT.Exp).then_inc(router_exp, 1)
            act.wait_ge(comb_T, 1)
            ACTE.copy(SGT, bank(6, 8, 128)).then_inc(comb_Ts, 1)
            for i in range(0, NT, 2):
                act.wait_ge(gathered, i + 1)
                ACTE.copy(XIN[:, :, :, i, :], bank(i, 2, 8, 32)).then_inc(xin_act, 1)
            for e in range(8):
                for g in range(2):
                    act.wait_ge(L0f_h, 2 * e + g + 1)
                    if e >= 2:
                        act.wait_ge(L0f_y, e - 1)
                    ACTE.activation(HT0[:, e % 2, 4 * g:4 * g + 4, :], bank(4 + g, 4, 128),
                                    ACT.Gelu_apprx_tanh).then_inc(L0f_hs, 1)
            layernorm(3)
            wide(0)
            layernorm(4)
            self16(1)
            layernorm(5)
            act.wait_ge(router_d, 2)
            ACTE.activation(TP, TP, ACT.Exp).then_inc(router_exp, 1)
            for i in range(0, NT, 2):
                act.wait_ge(gathered, i + 5)
                ACTE.copy(TXIN[:, :, :, i, :], bank(i, 2, 16, 16)).then_inc(xin_act, 1)
            act.wait_ge(comb_T, 2)
            ACTE.copy(TCT, bank(4, NT, 2, 128)).then_inc(comb_Ts, 1)
            for g in range(2):
                act.wait_ge(L1f_gate, g + 1)
                ACTE.activation(TSG[:, g, :], ps[:, 2 * g, :], ACT.Silu).then_inc(L1f_silu, 1)
            act.wait_ge(L1f_o, 1)
            for c in range(2):
                for g in range(2):
                    if g == 0:
                        ACTE.copy(TOT[:, c, :, 8 * g:8 * g + 8, :].rearrange("p i e s -> p e i s"),
                                  bank(4 + 2 * c + g, 8, NT, 16)).then_inc(L1f_os_act, 1)
            for i in range(0, NT, 2):
                act.wait_ge(L1f_oT, i + 1)
                ACTE.copy(TON[:, i, :, :], bank(i, 2, D)).then_inc(L1f_ons_act, 1)
            layernorm(6)
            wide(1)
            layernorm(7)
            self1(0)
            layernorm(8)
            act.wait_ge(router_d, 3)
            ACTE.activation(RL, RL, ACT.Exp).then_inc(router_exp, 1)
            act.wait_ge(L2f_mean, 1)
            ACTE.activation(RC_[:, 1:2], RC_[:, 0:1], ACT.Exp, scale=-1.0).then_inc(L2f_sig, 1)
            for e in range(8):
                act.wait_ge(L2f_xi, e + 1)
                if e >= 2:
                    act.wait_ge(L2f_h, 8 * (e - 1))
                ACTE.copy(EXI[:, e % 2, 0, :], ps[:, 6, :]).then_inc(L2f_xis_act, 1)
                for f in range(8):
                    n = 8 * e + f
                    act.wait_ge(L2f_h, n + 1)
                    if n >= 4:
                        act.wait_ge(L2f_y, n - 3)
                    ACTE.activation(EH[:, n % 4, :], ps[:, 4 + n % 2, :], ACT.Gelu,
                                    bias=C("L2f_b1")[:, n:n + 1]).then_inc(L2f_hs, 1)
            layernorm("9b", affine=("L3x_g1", "L3x_b1"))
            for b in range(16):
                act.wait_ge(ctx_T, b + 1)
                ACTE.copy(ctxT1[:, 512 * b:512 * b + 512], ps[:, 4 + 2 * (b % 2), :]).then_inc(ctx_Ts_act, 1)
            narrow(1)
            act.wait_ge(na_v, 1)
            ACTE.copy(NV[:, 0, :], ps[:, 0, :]).then_inc(na_vs_act, 1)
            layernorm(10)
            self1(1)
            layernorm(11)
            act.wait_ge(L3f_ss, 1)
            for h in range(16):
                if h >= 4:
                    act.wait_ge(L3f_acc, h - 3)
                ACTE.activation(FT[:, h % 4, :], FS, ACT.Relu, scale=C("L3f_W1")[:, h:h + 1],
                                bias=C("L3f_b1")[:, h:h + 1]).then_inc(L3f_relu, 1)

        @block.vector
        def _(dve):
            chain = [0]

            def link(ins):
                chain[0] += 1
                ins.then_inc(dve_step, 1)
                dve.wait_ge(dve_step, chain[0])

            dve.wait_ge(consts_loaded, 16)
            dve.wait_ge(x_loaded, 16)

            def layernorm(key, affine=None):
                n = LN[key]
                src = xn if key == "9b" else x
                for i in range(NT):
                    ins = DVE.bn_stats(st6[:, i, :], src[:, i, :])
                link(ins)
                for i in range(NT):
                    ins = DVE.bn_aggr(mv[:, i, :], st6[:, i, :])
                ins.then_inc(ln_stats, 1)
                dve.wait_ge(ln_rstd, n + 1)
                for i in range(NT):
                    DVE.tensor_scalar(xn[:, i, :], src[:, i, :], mv[:, i, 0:1], rstd[:, i:i + 1], ALU.subtract,
                                      ALU.mult).then_inc(ln_xn, 1)
                if key == 9:
                    dve.wait_ge(ln_xn, 4 * (LNX[9] + 1))
                    return
                dve.wait_ge(ln_T, LNT[key] + 1)
                if affine is None:
                    DVE.tensor_copy(xnT[:, 1, :], ps[:, 1, :]).then_inc(ln_xnT_dve, 1)
                else:
                    g, b = affine
                    DVE.tensor_scalar(xnT[:, 1, :], ps[:, 1, :], C(g)[:, 1:2], C(b)[:, 1:2], ALU.mult,
                                      ALU.add).then_inc(ln_xnT_dve, 1)

            def add_x(l, banks):
                for i in range(NT):
                    dve.wait_ge(layer_out, 4 * l + i + 1)
                    ins = DVE.tensor_tensor(x[:, i, :], x[:, i, :], ps[:, banks[i], 0:D], ALU.add)
                    if l == LAYERS - 1:
                        ins.then_inc(x_final, 1)
                    elif i == NT - 1:
                        link(ins)

            def wide(k):
                for r in range(1, NPAIR, 2):
                    dve.wait_ge(xa_q, 8 * k + r + 1)
                    DVE.tensor_scalar(XQ[:, r, :], ps[:, r, :], DHB ** -0.5, None, ALU.mult).then_inc(xa_qs_dve, 1)

                def rowmax(t, r):
                    dve.wait_ge(xa_S, t + 1)
                    DVE.tensor_reduce(XNM[:, r % 4:r % 4 + 1], bank(2 * (r % 2), 1024), X, ALU.max,
                                      negate=True).then_inc(xa_max, 1)

                def spread(t, r, first):
                    dve.wait_ge(xa_T, 2 * t + 2)
                    if not first:
                        dve.wait_ge(xa_Z, t - 1)
                    DVE.tensor_copy(XPT[:, r % 2, 4:8, :], bank(5, 4, 128)).then_inc(xa_PT_dve, 1)

                def normalise(t, r):
                    dve.wait_ge(xa_P, t + 1)
                    DVE.reciprocal(XRI[:, r % 4:r % 4 + 1], XRS[:, r % 4:r % 4 + 1]).then_inc(xa_recip, 1)
                    dve.wait_ge(xa_recip, t + 1)
                    dve.wait_ge(xa_Z, t + 1)
                    DVE.tensor_scalar(XZ[:, r % 2, :], bank(6, DC), XRI[:, r % 4:r % 4 + 1], None,
                                      ALU.mult).then_inc(xa_Zs, 1)

                def ztrans(t, r):
                    dve.wait_ge(xa_ZT, t + 1)
                    DVE.tensor_copy(XZT[:, r % 2, 0:128], bank(6, 128, at=DC)).then_inc(xa_ZTs, 1)
                    DVE.tensor_copy(XZT[0:D2, r % 2, 128:256], bank(6, 128, rows=slice(0, D2), at=DC + 128)) \
                        .then_inc(xa_ZTs, 1)

                def batch(b, first):
                    t0 = 64 * k + 8 * b if first else b * 8 + 64 * k
                    for r in range(NPAIR):
                        if r == 0:
                            if not first:
                                ztrans(t0 - 3, 5)
                                spread(t0 - 1, 7, False)
                                normalise(t0 - 2, 6)
                            rowmax(t0, 0)
                            continue
                        rowmax(t0 + r, r)
                        if r >= 3:
                            ztrans(t0 + r - 3, r - 3)
                        elif not first:
                            ztrans(t0 + r - 3, r + 5)
                        spread(t0 + r - 1, r - 1, first and r < 3)
                        if r >= 2:
                            normalise(t0 + r - 2, r - 2)
                        elif not first:
                            normalise(t0 + r - 2, r + 6)

                batch(0, True)
                with dve.Fori(1, B) as b:
                    batch(b, False)
                t1 = 64 * (k + 1)
                ztrans(t1 - 3, 5)
                spread(t1 - 1, 7, False)
                normalise(t1 - 2, 6)
                ztrans(t1 - 2, 6)
                normalise(t1 - 1, 7)
                ztrans(t1 - 1, 7)

            def narrow(k):
                dve.wait_ge(na_q, 2 * k + 2)
                DVE.tensor_scalar(NQ[:, 1, :], ps[:, 3, :], C("L0x_bq" if k == 0 else "L3x_bq")[:, 1:2], None,
                                  ALU.add).then_inc(na_qs_dve, 1)
                dve.wait_ge(na_A, 2 * k + 2)
                R = slice(0, D2 + 1)
                if k == 0:
                    DVE.tensor_scalar(NA2[R], bank(5, TOK, rows=R), D ** -0.5, None, ALU.mult).then_inc(na_As_dve, 1)
                else:
                    DVE.tensor_scalar(NA2[D2:D2 + 1], bank(5, TOK, rows=slice(D2, D2 + 1)), D ** -0.5, None, ALU.mult)
                    DVE.tensor_scalar(NA2[0:D2], bank(5, TOK, rows=slice(0, D2)), C("L3x_g2")[0:D2, 1:2], D ** -0.5,
                                      ALU.mult, ALU.mult).then_inc(na_As_dve, 1)
                    dve.wait_ge(na_As_act, 2)
                    DVE.tensor_scalar(NA1, NA1, C("L3x_g2")[:, 0:1], None, ALU.mult).then_inc(na_A1_scaled, 1)
                DVE.memset(NZT2[D2:D2 + 1], 1.0).then_inc(na_ones, 1)

                def norm(i):
                    t = 4 * k + i
                    dve.wait_ge(na_P, t + 1)
                    link(DVE.reciprocal(XRI[:, i:i + 1], XRS[:, i:i + 1]))
                    dve.wait_ge(na_Z, t + 1)
                    DVE.tensor_scalar(XZ[:, i % 2, :], bank(6, DC), XRI[:, i:i + 1], None, ALU.mult).then_inc(na_Zs, 1)
                    dve.wait_ge(na_ZT, t + 1)
                    c = slice(128 * i, 128 * i + 128)
                    if k == 0:
                        DVE.tensor_copy(NZT1[:, c], bank(6, 128, at=DC)).then_inc(na_ZTs, 1)
                        DVE.tensor_copy(NZT2[0:D2, c], bank(6, 128, rows=slice(0, D2), at=DC + 128)).then_inc(na_ZTs, 1)
                    else:
                        DVE.tensor_scalar(NZT1[:, c], bank(6, 128, at=DC), C("L3x_g2")[:, 0:1], C("L3x_b2")[:, 0:1],
                                          ALU.mult, ALU.add).then_inc(na_ZTs, 1)
                        DVE.tensor_scalar(NZT2[0:D2, c], bank(6, 128, rows=slice(0, D2), at=DC + 128),
                                          C("L3x_g2")[0:D2, 1:2], C("L3x_b2")[0:D2, 1:2],
                                          ALU.mult, ALU.add).then_inc(na_ZTs, 1)

                for i in range(NT):
                    t = 4 * k + i
                    dve.wait_ge(na_S, t + 1)
                    DVE.tensor_reduce(XNM[:, i:i + 1], bank(2 * (i % 2), 1024), X, ALU.max, negate=True) \
                        .then_inc(na_max, 1)
                    if i >= 1:
                        dve.wait_ge(na_T, 2 * t)
                        if i >= 3:
                            dve.wait_ge(na_Z, t - 2)
                        DVE.tensor_copy(XPT[:, (i - 1) % 2, 4:8, :], bank(5, 4, 128)).then_inc(na_PT_dve, 1)
                        norm(i - 1)
                dve.wait_ge(na_T, 8 * k + 8)
                dve.wait_ge(na_Z, 4 * k + 2)
                DVE.tensor_copy(XPT[:, 1, 4:8, :], bank(5, 4, 128)).then_inc(na_PT_dve, 1)
                norm(3)

            def self16(k):
                for h in range(2):
                    for r in (2, 3, 6, 7):
                        dve.wait_ge(sa_q, 8 * k + 4 * h + r // 2 + 1)
                        src = bank(r // 2, 256, at=256 * (r % 2))
                        if k == 0:
                            DVE.tensor_copy(QC[:, r, :], src).then_inc(sa_qs_dve, 1)
                        else:
                            DVE.tensor_scalar(QC[:, r, :], src, C("L1a_bq")[:, r:r + 1], None,
                                              ALU.add).then_inc(sa_qs_dve, 1)
                    if k == 0:
                        dve.wait_ge(sa_k0, h + 1)
                        DVE.tensor_copy(KC[:, 0, :], bank(4, 256)).then_inc(sa_ks0, 1)
                    else:
                        for r in (2, 3, 6, 7):
                            dve.wait_ge(sa_k, 4 * h + r // 2 + 1)
                            DVE.tensor_scalar(KC[:, r, :], bank(4 + r // 2, 256, at=256 * (r % 2)),
                                              C("L1a_bk")[:, r:r + 1], None, ALU.add).then_inc(sa_ks_dve, 1)
                    if h == 0:
                        link(DVE.memset(VB, 0.0))
                    dve.wait_ge(sa_v, 2 * k + h + 1)
                    for b in range(4):
                        for e in range(2):
                            R = half(e)
                            if k == 0:
                                src = bank(6, 4, 16, rows=R)[:, b:b + 1, :].to_broadcast([64, 8, 16])
                            else:
                                src = bank(6 + b // 2, 2, 8, 32, rows=R)[:, b % 2, :, 16 * e:16 * e + 16]
                            ins = DVE.tensor_copy(VB[R, b, :, 16 * e:16 * e + 16], src)
                    ins.then_inc(sa_vs, 1)

                    def soft(u):
                        t = 8 * k + 4 * h + u
                        p = u % 2
                        sc = SC[:, p, :].rearrange("p (a b) -> p a b", b=64)
                        raw = ps[:, p, :].rearrange("p (a b) -> p a b", b=64)
                        mx = AMX[:, p, :]
                        dve.wait_ge(sa_S, t + 1)
                        if u >= 2:
                            dve.wait_ge(sa_T, t - 1)
                        if k == 0:
                            link(DVE.tensor_tensor(sc, raw, C("causal").unsqueeze(1).to_broadcast([128, 8, 64]), ALU.add))
                            raw = sc
                        link(DVE.tensor_reduce(mx, raw, X, ALU.max))
                        DVE.tensor_tensor(sc, raw, mx.unsqueeze(2).to_broadcast([128, 8, 64]), ALU.subtract) \
                            .then_inc(sa_d, 1)

                    def norm(u):
                        t = 8 * k + 4 * h + u
                        p = u % 2
                        sc = SC[:, p, :].rearrange("p (a b) -> p a b", b=64)
                        dve.wait_ge(sa_exp, t + 1)
                        link(DVE.tensor_reduce(ASM[:, p, :], sc, X, ALU.add))
                        link(DVE.reciprocal(ARC[:, p, :], ASM[:, p, :]))
                        DVE.tensor_tensor(sc, sc, ARC[:, p, :].unsqueeze(2).to_broadcast([128, 8, 64]), ALU.mult) \
                            .then_inc(sa_P, 1)

                    soft(0)
                    for u in range(1, 4):
                        soft(u)
                        norm(u - 1)
                    norm(3)
                    dve.wait_ge(sa_y, 2 * k + h + 1)
                    DVE.tensor_copy(YT[:, 1, 256 * h:256 * h + 256], ps[:, 5, 256 * h:256 * h + 256]) \
                        .then_inc(sa_ys_dve, 1)

            def self1(k):
                dve.wait_ge(s1_k, 1 + k)
                DVE.tensor_copy(SK, bank(4, 2, TOK)).then_inc(s1_ks, 1)
                dve.wait_ge(s1_v, 1 + k)
                DVE.tensor_copy(SV[:, 2:4, :], bank(7, 2, D)).then_inc(s1_vs_dve, 1)
                dve.wait_ge(s1_S, 1 + k)
                mask = C("bcausal" if k == 0 else "bfull").unsqueeze(1).to_broadcast([128, NT, 128])
                link(DVE.tensor_tensor(SS, bank(0, NT, 128), mask, ALU.add))
                link(DVE.tensor_reduce(SMX, SS, X, ALU.max))
                DVE.tensor_tensor(SS, SS, SMX.unsqueeze(2).to_broadcast([128, NT, 128]), ALU.subtract) \
                    .then_inc(s1_d, 1)
                dve.wait_ge(s1_exp, 1 + k)
                link(DVE.tensor_reduce(SSM, SS, X, ALU.add))
                link(DVE.reciprocal(SRC, SSM))
                DVE.tensor_tensor(SS, SS, SRC.unsqueeze(2).to_broadcast([128, NT, 128]), ALU.mult) \
                    .then_inc(s1_P, 1)
                dve.wait_ge(s1_o, 1 + k)
                DVE.tensor_copy(SO[:, 1, :], ps[:, 3, :]).then_inc(s1_os_dve, 1)

            def ranks(k):
                for i in range(NT):
                    if i >= 1:
                        dve.wait_ge(rk_spread, 4 * k + i)
                    DVE.tensor_tensor(RDL, RP[:, i, :].unsqueeze(2).to_broadcast([128, 8, 64]),
                                      C("delta").unsqueeze(1).to_broadcast([128, 8, 64]), ALU.mult) \
                        .then_inc(rk_diag, 1)
                for i in range(NT):
                    dve.wait_ge(rk_spread, 4 * k + i + 1)
                    other = bank(2 + i, 8, 64)
                    mine = RP[:, i, :].unsqueeze(2).to_broadcast([128, 8, 64])
                    DVE.tensor_tensor(RG, other, mine, ALU.is_gt)
                    link(DVE.tensor_tensor(RE, other, mine, ALU.is_equal))
                    link(DVE.tensor_tensor(RE, RE, C("before").unsqueeze(1).to_broadcast([128, 8, 64]), ALU.mult))
                    link(DVE.tensor_tensor(RG, RG, RE, ALU.add))
                    link(DVE.tensor_reduce(RK[:, i, :], RG, X, ALU.add))

            def first_hot(out, p, mx, tmp, vmx, rev, n):
                bc = lambda a: a.unsqueeze(2).to_broadcast([128, NT, n])
                link(DVE.tensor_reduce(mx, p, X, ALU.max))
                link(DVE.tensor_tensor(tmp, p, bc(mx), ALU.is_equal))
                link(DVE.tensor_tensor(tmp, tmp, C(rev).unsqueeze(1).to_broadcast([128, NT, n]), ALU.mult))
                link(DVE.tensor_reduce(vmx, tmp, X, ALU.max))
                link(DVE.tensor_tensor(out, tmp, bc(vmx), ALU.is_equal))

            layernorm(0)
            narrow(0)
            add_x(0, (0, 1, 2, 3))
            layernorm(1)
            self16(0)
            add_x(1, (0, 1, 2, 3))
            layernorm(2)
            bc8 = lambda a: a.unsqueeze(2).to_broadcast([128, NT, 8])
            dve.wait_ge(router_logits, 1)
            link(DVE.tensor_reduce(RA, bank(2, NT, 8), X, ALU.max))
            DVE.tensor_tensor(RP, bank(2, NT, 8), bc8(RA), ALU.subtract).then_inc(router_d, 1)
            dve.wait_ge(router_exp, 1)
            link(DVE.tensor_reduce(RA, RP, X, ALU.add))
            link(DVE.reciprocal(RB_, RA))
            link(DVE.tensor_tensor(RP, RP, bc8(RB_), ALU.mult))
            ranks(0)
            for i in range(NT):
                ins = DVE.tensor_tensor(SEL[:, i], RK[:, i, :].unsqueeze(2).to_broadcast([128, 8, 32]),
                                        C("slot32").unsqueeze(1).to_broadcast([128, 8, 32]), ALU.is_equal)
            chain[0] += 1
            ins.then_inc(dve_step, 1)
            dve.wait_ge(dve_step, chain[0])
            for i in range(NT):
                ins = DVE.tensor_tensor(SELG[:, :, i], SEL[:, i], RP[:, i, :].unsqueeze(2).to_broadcast([128, 8, 32]),
                                        ALU.mult)
            ins.then_inc(L0f_sel, 1)
            for i in range(1, NT, 2):
                dve.wait_ge(gathered, i + 1)
                DVE.tensor_copy(XIN[:, :, :, i, :], bank(i, 2, 8, 32)).then_inc(xin_dve, 1)
            for e in range(8):
                dve.wait_ge(L0f_y, e + 1)
                DVE.tensor_copy(YS[:, e, :], bank(6 + e % 2, D)).then_inc(L0f_ys, 1)
            rb = wv(5184, D).bitcast(BF16)
            for i in range(NT):
                dve.wait_ge(layer_out, 4 * 2 + i + 1)
                o = rb[:, 256 * (i % 2):256 * (i % 2) + 256]
                link(DVE.tensor_copy(o, ps[:, i, 0:D]))
                ins = DVE.tensor_tensor(x[:, i, :], x[:, i, :], o, ALU.add)
                link(ins)
            layernorm(3)
            wide(0)
            add_x(3, (0, 1, 2, 3))
            layernorm(4)
            self16(1)
            add_x(4, (0, 1, 2, 3))
            layernorm(5)
            bc16 = lambda a: a.unsqueeze(2).to_broadcast([128, NT, 16])
            dve.wait_ge(router_logits, 2)
            link(DVE.tensor_reduce(TM1, bank(2, NT, 16), X, ALU.max))
            DVE.tensor_tensor(TP, bank(2, NT, 16), bc16(TM1), ALU.subtract).then_inc(router_d, 1)
            dve.wait_ge(router_exp, 2)
            link(DVE.tensor_reduce(TM1, TP, X, ALU.add))
            link(DVE.reciprocal(TM2, TM1))
            link(DVE.tensor_tensor(TP, TP, bc16(TM2), ALU.mult))
            first_hot(TOH1, TP, TM1, TT, TV, "rev16", 16)
            link(DVE.scalar_tensor_tensor(TP, TOH1, -2.0, TP, ALU.mult, ALU.add))
            first_hot(TOH2, TP, TM2, TT, TV, "rev16", 16)
            DVE.tensor_copy(TU, TOH1).then_inc(L1f_hot, 1)
            dve.wait_ge(L1f_cum, 1)
            DVE.tensor_tensor(TQ1, bank(3, NT, 16), TOH1, ALU.mult)
            link(DVE.tensor_tensor(TQ2, bank(3, NT, 16, at=64), TOH2, ALU.mult))
            bs = lambda a, i: a[:, i, :].unsqueeze(2).to_broadcast([128, 16, 16])
            slots = C("slot16").unsqueeze(1).to_broadcast([128, 16, 16])
            for i in range(NT):
                DVE.tensor_tensor(TD[:, i], bs(TQ1, i), slots, ALU.is_equal)
                ins = DVE.tensor_tensor(TX_[:, i], bs(TQ2, i), slots, ALU.is_equal)
            link(ins)
            for i in range(NT):
                ins = DVE.tensor_tensor(TD[:, i], TD[:, i], TX_[:, i], ALU.add)
            ins.then_inc(L1f_disp, 1)
            DVE.tensor_scalar(TQ1, TQ1, 8.0, None, ALU.min)
            link(DVE.tensor_scalar(TQ2, TQ2, 8.0, None, ALU.min))
            dve.wait_ge(L1f_disp, 1)
            for i in range(NT):
                DVE.tensor_tensor(TC[:, i], bs(TQ1, i), slots, ALU.is_equal)
                ins = DVE.tensor_tensor(TX_[:, i], bs(TQ2, i), slots, ALU.is_equal)
            link(ins)
            for i in range(NT):
                ins = DVE.tensor_scalar(TC[:, i], TC[:, i], TM1[:, i:i + 1], None, ALU.mult)
            link(ins)
            for i in range(NT):
                ins = DVE.scalar_tensor_tensor(TC[:, i], TX_[:, i], TM2[:, i:i + 1], TC[:, i], ALU.mult, ALU.add)
            ins.then_inc(L1f_comb, 1)
            for i in range(1, NT, 2):
                dve.wait_ge(gathered, i + 5)
                DVE.tensor_copy(TXIN[:, :, :, i, :], bank(i, 2, 16, 16)).then_inc(xin_dve, 1)
            for g in range(2):
                dve.wait_ge(L1f_silu, g + 1)
                dve.wait_ge(L1f_up, g + 1)
                DVE.tensor_tensor(THT[:, 8 * g:8 * g + 8, :], TSG[:, g, :].rearrange("p (a b) -> p a b", b=64),
                                  bank(2 * g + 1, 8, 64), ALU.mult).then_inc(L1f_hs, 1)
            dve.wait_ge(L1f_o, 1)
            for c in range(2):
                DVE.tensor_copy(TOT[:, c, :, 8:16, :].rearrange("p i e s -> p e i s"),
                                bank(4 + 2 * c + 1, 8, NT, 16)).then_inc(L1f_os_dve, 1)
            for i in range(1, NT, 2):
                dve.wait_ge(L1f_oT, i + 1)
                DVE.tensor_copy(TON[:, i, :, :], bank(i, 2, D)).then_inc(L1f_ons_dve, 1)
            add_x(5, (4, 5, 6, 7))
            layernorm(6)
            wide(1)
            add_x(6, (0, 1, 2, 3))
            layernorm(7)
            self1(0)
            add_x(7, (4, 5, 6, 7))
            layernorm(8)
            bc8 = lambda a: a.unsqueeze(2).to_broadcast([128, NT, 8])
            sq = wv(5184, D)
            for i in range(NT):
                link(DVE.tensor_tensor(sq, xn[:, i, :], xn[:, i, :], ALU.mult))
                link(DVE.tensor_reduce(RA[:, i:i + 1], sq, X, ALU.add))
            wf2 = wv(5696, 16)
            DVE.tensor_tensor(wf2, C("L2f_waff"), C("L2f_waff"), ALU.mult).then_inc(L2f_w2, 1)
            dve.wait_ge(L2f_wn, 1)
            DVE.tensor_copy(RS1, bank(3, 8)).then_inc(L2f_norms2, 2)
            dve.wait_ge(L2f_norms, 2)
            for i in range(NT):
                ins = DVE.tensor_scalar(RT[:, i, :], RS1, RA[:, i:i + 1], 1e-9, ALU.mult, ALU.add)
            link(ins)
            link(DVE.reciprocal(RL, RT))
            dve.wait_ge(router_logits, 3)
            link(DVE.tensor_tensor(RP, bank(2, NT, 8), RL, ALU.mult))
            link(DVE.tensor_reduce(RB_[:, 0:1], RP, mybir.AxisListType.XY, ALU.add))
            link(DVE.tensor_copy(RB_[:, 1:2], RB_[:, 0:1]))
            DVE.tensor_copy(RB_[:, 2:3], RB_[:, 0:1]).then_inc(L2f_rowsum, 1)
            link(DVE.tensor_reduce(RA, RP, X, ALU.max))
            DVE.tensor_tensor(RL, RP, bc8(RA), ALU.subtract).then_inc(router_d, 1)
            dve.wait_ge(L2f_total, 1)
            DVE.tensor_scalar(RC_[:, 0:1], bank(3, 1, at=8), 1.0 / (TOK * 8), C("L2f_thr"), ALU.mult,
                              ALU.subtract).then_inc(L2f_mean, 1)
            dve.wait_ge(router_exp, 3)
            link(DVE.tensor_reduce(RA, RL, X, ALU.add))
            link(DVE.reciprocal(RB_, RA))
            link(DVE.tensor_tensor(RL, RL, bc8(RB_), ALU.mult))
            first_hot(ROH, RL, RA, RT, RB_, "rev8", 8)
            dve.wait_ge(L2f_sig, 1)
            link(DVE.tensor_scalar(RC_[:, 2:3], RC_[:, 1:2], 1.0, None, ALU.add))
            link(DVE.reciprocal(RC_[:, 3:4], RC_[:, 2:3]))
            link(DVE.tensor_scalar(RC_[:, 2:3], RC_[:, 3:4], float(CAP), 4.0, ALU.mult, ALU.max))
            ranks(1)
            link(DVE.tensor_scalar(RK, RK, 1.0, RC_[:, 2:3], ALU.add, ALU.is_le))
            link(DVE.tensor_tensor(ROH, ROH, RK, ALU.mult))
            for e in range(8):
                if e >= 2:
                    dve.wait_ge(L2f_xi, e - 1)
                DVE.tensor_tensor(EDG[:, e % 2], ident.unsqueeze(1).to_broadcast([128, NT, 128]),
                                  ROH[:, :, e:e + 1].to_broadcast([128, NT, 128]), ALU.mult) \
                    .then_inc(L2f_diag, 1)
                dve.wait_ge(L2f_xi, e + 1)
                if e >= 2:
                    dve.wait_ge(L2f_h, 8 * (e - 1))
                DVE.tensor_copy(EXI[:, e % 2, 1, :], ps[:, 7, :]).then_inc(L2f_xis_dve, 1)
            add_x(8, (0, 1, 2, 3))
            for t in range(B * KT):
                ins = DVE.bn_stats(CST6[:, t, :], ctxN[:, t, :])
            link(ins)
            for t in range(B * KT):
                ins = DVE.bn_aggr(CMV[:, t, :], CST6[:, t, :])
            ins.then_inc(ln_stats, 1)
            dve.wait_ge(ln_rstd, LN["c"] + 1)
            for t in range(B * KT):
                ins = DVE.tensor_scalar(ctxN[:, t, :], ctxN[:, t, :], CMV[:, t, 0:1], CRS[:, t:t + 1],
                                        ALU.subtract, ALU.mult)
                if t % 4 == 3:
                    ins.then_inc(ctx_n, 1)
            layernorm(9)
            layernorm("9b", affine=("L3x_g1", "L3x_b1"))
            for b in range(16):
                dve.wait_ge(ctx_T, b + 1)
                DVE.tensor_copy(ctxT2[0:D2, 512 * b:512 * b + 512], ps[0:D2, 5 + 2 * (b % 2), :]) \
                    .then_inc(ctx_Ts_dve, 1)
            dve.wait_ge(na_kb, 1)
            for c in range(2):
                DVE.tensor_scalar(wv(4090 + c, 1), ps[:, 0, c:c + 1], C("L3x_bk")[:, c:c + 1], None,
                                  ALU.add).then_inc(na_kbs, 1)
            narrow(1)
            dve.wait_ge(na_v, 2)
            DVE.tensor_copy(NV[:, 1, :], ps[:, 1, :]).then_inc(na_vs_dve, 1)
            add_x(9, (2, 3, 4, 5))
            layernorm(10)
            self1(1)
            add_x(10, (4, 5, 6, 7))
            layernorm(11)
            dve.wait_ge(L3f_s, 1)
            DVE.tensor_scalar(FS, ps[:, 2, 0:256], C("L3f_bin"), None, ALU.add).then_inc(L3f_ss, 1)
            for h in range(16):
                dve.wait_ge(L3f_relu, h + 1)
                if h == 0:
                    ins = DVE.tensor_scalar(FG_, FT[:, 0, :], C("L3f_W2")[:, 0:1], C("L3f_b2"), ALU.mult, ALU.add)
                else:
                    ins = DVE.scalar_tensor_tensor(FG_, FT[:, h % 4, :], C("L3f_W2")[:, h:h + 1], FG_,
                                                   ALU.mult, ALU.add)
                ins.then_inc(L3f_acc, 1)
                dve.wait_ge(L3f_acc, h + 1)
            add_x(11, (3, 4, 5, 6))

        @block.tensor
        def _(pe):

            def loaded(name):
                n = UIDX[name]
                pe.wait_ge(slot_loaded[n % NSLOT], 16 * (n // NSLOT + 1))

            pe.wait_ge(consts_loaded, 16)

            def layernorm(key):
                for i in range(NT):
                    pe.wait_ge(ln_xn, 4 * LNX[key] + i + 1)
                    for c in range(2):
                        ins = PE.transpose(ps[:, c, 128 * i:128 * i + 128], xn[:, i, 128 * c:128 * c + 128], ident)
                ins.then_inc(ln_T, 1)
                pe.wait_ge(ln_xnT_act, LNT[key] + 1)
                pe.wait_ge(ln_xnT_dve, LNT[key] + 1)

            tile = lambda i: slice(128 * i, 128 * i + 128)

            def project_out(l, banks, lhs, rhs, n, bias=None, used=1):
                for i in range(NT):
                    o = ps[:, banks[i], 0:D]
                    if bias is not None:
                        mm(o, C("ones", slice(0, 1)), bias, True, False)
                    for c in range(n):
                        ins = mm(o, lhs(c, i), rhs(c), start=(c == 0 and bias is None), stop=(c == n - 1))
                    ins.then_inc(layer_out, 1)
                    if i == NT - 1 and used:
                        pe.wait_ge(layer_out, 4 * l + 4)
                        pe.sem_inc(units_used, used)

            def release(n):
                pe.sem_inc(units_used, n)

            def wide(k):
                L = "L1x" if k == 0 else "L2x"
                l = 3 if k == 0 else 6
                loaded(f"{L}_q")
                wq = unit(f"{L}_q", 0, 2, 1024)
                for r in range(NPAIR):
                    for c in range(2):
                        ins = mm(ps[:, r, :], wq[:, c, 128 * r:128 * r + 128], xnT[:, c, :], c == 0, c == 1)
                    ins.then_inc(xa_q, 1)
                pe.wait_ge(xa_q, 8 * k + 8)
                release(1)
                pe.wait_ge(xa_qs_act, 4 * k + 4)
                pe.wait_ge(xa_qs_dve, 4 * k + 4)
                loaded(f"{L}_k0")
                loaded(f"{L}_k1")
                loaded(f"{L}_v")
                wkt = [unit(f"{L}_k{h}", 0, 4, 2, DC) for h in range(2)]
                wvv = unit(f"{L}_v", 0, 2, 1024)

                def queries(b, t, r, before=None):
                    if before is not None:
                        pe.wait_ge(xa_OT, before + 1)
                    for e in range(2):
                        wkr = wkt[r // 4][:, r % 4, e, :]
                        rhs = XQ[:, r, bass.ds(b * 64, 64)]
                        mm(bank(7, 64, at=64 * e), wkr[:, 0:128], rhs)
                        ins = mm(bank(7, 64, rows=slice(0, D2), at=128 + 64 * e), wkr[:, 128:DC], rhs)
                    ins.then_inc(xa_A, 1)

                def scores(b, t, r, first):
                    pe.wait_ge(xa_As, 2 * t + 2)
                    if not first:
                        pe.wait_ge(xa_P, t - 1)
                    for n in range(2):
                        o = ps[:, 2 * (r % 2) + n, :]
                        mm(o, XA[:, r % 2, 0:128], ctxT1[:, bass.ds(b * LK + 512 * n, 512)], True, False)
                        ins = mm(o, XA[0:D2, r % 2, 128:256], ctxT2[0:D2, bass.ds(b * LK + 512 * n, 512)], False, True)
                    ins.then_inc(xa_S, 1)

                def transposes(t, r, first):
                    pe.wait_ge(xa_P, t + 1)
                    for g in range(2):
                        if not first:
                            pe.wait_ge(xa_PT_act if g == 0 else xa_PT_dve, t)
                        for m in range(4):
                            n = 4 * g + m
                            ins = PE.transpose(bank(4 + g, 128, at=128 * m), XP[:, r % 2, 128 * n:128 * n + 128], ident)
                        ins.then_inc(xa_T, 1)

                def attend(b, t, r, first):
                    pe.wait_ge(xa_PT_act, t + 1)
                    pe.wait_ge(xa_PT_dve, t + 1)
                    if not first:
                        pe.wait_ge(xa_Zs, t)
                    for n in range(KT):
                        ins = mm(bank(6, DC), XPT[:, r % 2, n, :],
                                 ctxN[:, bass.ds(b * KT + n, 1), :].rearrange("p a d -> p (a d)"), n == 0, n == KT - 1)
                    ins.then_inc(xa_Z, 1)

                def ztrans(t, r, first):
                    pe.wait_ge(xa_Zs, t + 1)
                    if not first:
                        pe.wait_ge(xa_ZTs, 2 * t)
                    PE.transpose(bank(6, 128, at=DC), XZ[:, r % 2, 0:128], ident)
                    PE.transpose(bank(6, 128, rows=slice(0, D2), at=DC + 128), XZ[:, r % 2, 128:DC], ident) \
                        .then_inc(xa_ZT, 1)

                def heads(t, r, before, first=False):
                    pe.wait_ge(xa_ZTs, 2 * t + 2)
                    if not first:
                        pe.wait_ge(xa_OT, t)
                    pe.wait_ge(xa_As, 2 * before + 2)
                    for e in range(2):
                        o = bank(7, 64, rows=half(e), at=256)
                        h = 2 * r + e
                        c = slice(64 * e, 64 * e + 64)
                        mm(o, wvv[:, 0, 64 * h:64 * h + 64], XZT[:, r % 2, 64 * e:64 * e + 64], True, False)
                        ins = mm(o, wvv[0:D2, 1, 64 * h:64 * h + 64], XZT[0:D2, r % 2, 128 + 64 * e:192 + 64 * e],
                                 False, True)
                    ins.then_inc(xa_O, 1)

                def behind(b, t0, r, first):
                    prev = lambda lag: (b - 1, r - lag + 8) if r < lag else (b, r - lag)
                    for lag, what in ((3, "zt"), (1, "t"), (3, "o"), (2, "z")):
                        if first and r < lag:
                            continue
                        bb, rr = prev(lag)
                        t = t0 + r - lag
                        f = first and r - lag == 0
                        if what == "zt":
                            ztrans(t, rr, f)
                        elif what == "t":
                            transposes(t, rr, f)
                        elif what == "o":
                            heads(t, rr, t + 3 if r in (0, NPAIR - 1) else t + 4, f)
                        else:
                            attend(bb, t, rr, f)

                def batch(b, first):
                    t0 = 64 * k + 8 * b if first else b * 8 + 64 * k
                    for r in range(NPAIR):
                        t = t0 + r
                        if r == 0:
                            queries(b, t, 0, None if first else t - 4)
                            behind(b, t0, 0, first)
                        scores(b, t, r, first and r < 2)
                        if r < NPAIR - 1:
                            if first and r < 4:
                                queries(b, t + 1, r + 1)
                            else:
                                queries(b, t + 1, r + 1, t - 3 if r == 0 else t - 4)
                        if r > 0:
                            behind(b, t0, r, first)

                batch(0, True)
                with pe.Fori(1, B) as b:
                    batch(b, False)
                t1 = 64 * (k + 1)
                ztrans(t1 - 3, 5, False)
                transposes(t1 - 1, 7, False)
                heads(t1 - 3, 5, t1 - 1)
                attend(B - 1, t1 - 2, 6, False)
                ztrans(t1 - 2, 6, False)
                heads(t1 - 2, 6, t1 - 1)
                attend(B - 1, t1 - 1, 7, False)
                ztrans(t1 - 1, 7, False)
                heads(t1 - 1, 7, t1 - 1)
                loaded(f"{L}_o")
                pe.wait_ge(xa_OT, t1)
                wo = unit(f"{L}_o", 0, 8, D)
                project_out(l, (0, 1, 2, 3), lambda c, i: XQ[:, c, tile(i)], lambda c: wo[:, c, :], 8,
                            bias=unit(f"{L}_k0", 1536, D, rows=slice(0, 1)), used=4)

            def narrow(k):
                ua, ub = ("L0x_a", "L0x_b") if k == 0 else ("L3x_a", "L3x_b")
                wq, wkt = unit(ua, 0, 2, D), unit(ua, 512, 2, DC + 1)
                wvv = unit(ub, 0, 2, D)
                loaded(ua)
                for c in range(2):
                    for d in range(2):
                        ins = mm(ps[:, 2 + c, :], wq[:, d, 128 * c:128 * c + 128], xnT[:, d, :], d == 0, d == 1)
                    ins.then_inc(na_q, 1)
                pe.wait_ge(na_qs_act, k + 1)
                pe.wait_ge(na_qs_dve, k + 1)
                for c in range(2):
                    ins = mm(ps[:, 4, :], wkt[:, c, 0:128], NQ[:, c, :], c == 0, c == 1)
                ins.then_inc(na_A, 1)
                for c in range(2):
                    lhs = wkt[:, c, 128:DC + 1] if k == 0 else wkt[:, c, 128:DC]
                    mmx = D2 + 1 if k == 0 else D2
                    ins = mm(bank(5, TOK, rows=slice(0, mmx)), lhs, NQ[:, c, :], c == 0, c == 1)
                if k == 1:
                    pe.wait_ge(na_kbs, 2)
                    for c in range(2):
                        ins = mm(bank(5, TOK, rows=slice(D2, D2 + 1)), wv(4090 + c, 1), NQ[:, c, :], c == 0, c == 1)
                ins.then_inc(na_A, 1)
                pe.wait_ge(na_As_act, k + 1)
                pe.wait_ge(na_As_dve, k + 1)
                if k == 1:
                    pe.wait_ge(na_A1_scaled, 1)
                R = slice(0, D2 + 1)

                def scores(i):
                    t = 4 * k + i
                    if k == 0:
                        pe.wait_ge(ctx_loaded[i], 48)
                    if i >= 2:
                        pe.wait_ge(na_P, t - 1)
                    for par in range(2):
                        b = 2 * i + par
                        q = slice(64 * b, 64 * b + 64)
                        for n in range(2):
                            o = ps[half(par), 2 * (i % 2) + n, :]
                            kk = slice(b * LK + 512 * n, b * LK + 512 * n + 512)
                            mm(o, NA1[:, q], ctxT1[:, kk], True, False)
                            ins = mm(o, NA2[R, q], ctxT2[R, kk], False, True)
                    ins.then_inc(na_S, 1)

                def rest(i):
                    t = 4 * k + i
                    pe.wait_ge(na_P, t + 1)
                    for g in range(2):
                        if i >= 1:
                            pe.wait_ge(na_PT_act if g == 0 else na_PT_dve, t)
                        for m in range(4):
                            n = 4 * g + m
                            ins = PE.transpose(bank(4 + g, 128, at=128 * m), XP[:, i % 2, 128 * n:128 * n + 128], ident)
                        ins.then_inc(na_T, 1)
                    pe.wait_ge(na_PT_act, t + 1)
                    pe.wait_ge(na_PT_dve, t + 1)
                    if i >= 1:
                        pe.wait_ge(na_Zs, t)
                    for par in range(2):
                        for n in range(KT):
                            ins = mm(bank(6, DC, rows=half(par)), XPT[:, i % 2, n, 64 * par:64 * par + 64],
                                     ctxN[:, (2 * i + par) * KT + n, :], n == 0, n == KT - 1)
                    ins.then_inc(na_Z, 1)
                    pe.wait_ge(na_Zs, t + 1)
                    if i >= 1:
                        pe.wait_ge(na_ZTs, 2 * t)
                    PE.transpose(bank(6, 128, at=DC), XZ[:, i % 2, 0:128], ident)
                    PE.transpose(bank(6, 128, rows=slice(0, D2), at=DC + 128), XZ[:, i % 2, 128:DC], ident) \
                        .then_inc(na_ZT, 1)

                scores(0)
                for i in range(1, NT):
                    scores(i)
                    rest(i - 1)
                rest(NT - 1)
                pe.wait_ge(na_ZTs, 8 * k + 8)
                pe.wait_ge(na_ones, k + 1)
                loaded(ub)
                if k == 0:
                    project_out(0, (0, 1, 2, 3), lambda c, i: NZT1[:, tile(i)] if c == 0 else NZT2[R, tile(i)],
                                lambda c: wvv[:, 0, :] if c == 0 else wvv[R, 1, :], 2, used=2)
                else:
                    for c in range(2):
                        o = ps[:, c, :]
                        mm(o, wvv[:, 0, 128 * c:128 * c + 128], NZT1, True, False)
                        mm(o, wvv[R, 1, 128 * c:128 * c + 128], NZT2[R], False, True).then_inc(na_v, 1)
                    pe.wait_ge(na_vs_act, 1)
                    pe.wait_ge(na_vs_dve, 1)
                    wo = unit(ub, 512, 2, D)
                    project_out(9, (2, 3, 4, 5), lambda c, i: NV[:, c, tile(i)], lambda c: wo[:, c, :], 2,
                                bias=unit(ub, 1024, D, rows=slice(0, 1)), used=2)

            def self16(k):
                l = 1 if k == 0 else 4
                for h in range(2):
                    tok = slice(256 * h, 256 * h + 256)
                    if h == 1:
                        pe.wait_ge(sa_d, 8 * k + 4)
                        pe.wait_ge(sa_PT, 8 * k + 4)
                        pe.wait_ge(sa_ys_act, 2 * k + 1)
                        pe.wait_ge(sa_ys_dve, 2 * k + 1)
                        pe.wait_ge(sa_vs, 2 * k + 1)
                    if k == 0:
                        wq = unit("L0a_a", 256, 1024)
                        wkk = unit("L0a_a", 1280, 128)
                        wvv = unit("L0a_a", 1408, 16)
                        for r in range(8):
                            ins = mm(bank(r // 2, 256, at=256 * (r % 2)), wq[:, 128 * r:128 * r + 128], LAT[:, tok])
                            if r % 2:
                                ins.then_inc(sa_q, 1)
                        mm(bank(4, 256), wkk, LAT[:, tok]).then_inc(sa_k0, 1)
                    else:
                        wq, wkk = unit("L1a_q", 0, 2, 1024), unit("L1a_k", 0, 2, 1024)
                        wvv = unit("L1a_v", 0, 2, D)
                        for done, ww, b0 in ((sa_q, wq, 0), (sa_k, wkk, 4)):
                            for r in range(8):
                                for c in range(2):
                                    ins = mm(bank(b0 + r // 2, 256, at=256 * (r % 2)), ww[:, c, 128 * r:128 * r + 128],
                                             xnT[:, c, tok], c == 0, c == 1)
                                if r % 2:
                                    ins.then_inc(done, 1)
                    pe.wait_ge(sa_qs_act, 8 * k + 4 * h + 4)
                    pe.wait_ge(sa_qs_dve, 8 * k + 4 * h + 4)
                    if k == 0:
                        pe.wait_ge(sa_ks0, h + 1)
                    else:
                        pe.wait_ge(sa_ks_act, 4 * h + 4)
                        pe.wait_ge(sa_ks_dve, 4 * h + 4)
                    for b in range(4):
                        t = slice(256 * h + 64 * b, 256 * h + 64 * b + 64)
                        for e in range(2):
                            if k == 0:
                                ins = mm(bank(6, 16, rows=half(e), at=16 * b), LAT[:, t], wvv)
                            else:
                                o = bank(6 + b // 2, D, rows=half(e), at=256 * (b % 2))
                                mm(o, C("ones", slice(0, 1))[:, 0:64], unit("L1a_v", 1024, D, rows=slice(0, 1)),
                                   True, False)
                                for c in range(2):
                                    ins = mm(o, xnT[:, c, t], wvv[:, c, :], False, c == 1)
                    ins.then_inc(sa_v, 1)

                    def scores(u):
                        t = 8 * k + 4 * h + u
                        ii, j = u // 2, u % 2
                        if u >= 2:
                            pe.wait_ge(sa_d, t - 1)
                        for par in range(2):
                            c = slice(64 * (2 * ii + par), 64 * (2 * ii + par) + 64)
                            R = slice(64 * j, 64 * j + (16 if k == 0 else 48))
                            for p in range(8):
                                ins = mm(bank(u % 2, 64, rows=half(par), at=64 * p), QC[R, p, c],
                                         KC[R, 0 if k == 0 else p, c])
                        ins.then_inc(sa_S, 1)

                    def attend(u):
                        t = 8 * k + 4 * h + u
                        ii, j = u // 2, u % 2
                        pe.wait_ge(sa_P, t + 1)
                        if u >= 2:
                            pe.wait_ge(sa_PT, t - 1)
                        for m in range(4):
                            ins = PE.transpose(bank(2 + u % 2, 128, at=128 * m), SC[:, u % 2, 128 * m:128 * m + 128],
                                               ident)
                        ins.then_inc(sa_T, 1)
                        pe.wait_ge(sa_PT, t + 1)
                        if u == 0:
                            pe.wait_ge(sa_vs, 2 * k + h + 1)
                        for par in range(2):
                            b = 2 * ii + par
                            for m in range(4):
                                ins = mm(bank(4 + j, 64, rows=slice(32 * m, 32 * m + 32), at=256 * h + 64 * b),
                                         VB[:, b, 4 * j + m, :], PT[:, u % 2, 128 * m + 64 * par:128 * m + 64 * par + 64])
                        if u == 3:
                            ins.then_inc(sa_y, 1)

                    scores(0)
                    for u in range(1, 4):
                        scores(u)
                        attend(u - 1)
                    attend(3)
                pe.wait_ge(sa_ys_act, 2 * k + 2)
                pe.wait_ge(sa_ys_dve, 2 * k + 2)
                if k == 0:
                    loaded("L0a_b")
                    wo = unit("L0a_b", 0, 2, D)
                    project_out(1, (0, 1, 2, 3), lambda c, i: YT[:, c, tile(i)], lambda c: wo[:, c, :], 2, used=2)
                else:
                    wo = unit("L1a_v", 512, 2, D)
                    project_out(4, (0, 1, 2, 3), lambda c, i: YT[:, c, tile(i)], lambda c: wo[:, c, :], 2,
                                bias=unit("L1a_v", 1280, D, rows=slice(0, 1)), used=3)

            def self1(k):
                L, l = ("L2a", 7) if k == 0 else ("L3a", 10)
                loaded(L)
                wq, wkk, wvv, wo = (unit(L, 512 * n, 2, D) for n in range(4))
                for done, ww, b0 in ((s1_q, wq, 2), (s1_k, wkk, 4)):
                    for c in range(2):
                        for d in range(2):
                            ins = mm(ps[:, b0 + c, :], ww[:, d, 128 * c:128 * c + 128], xnT[:, d, :], d == 0, d == 1)
                    ins.then_inc(done, 1)
                for i in range(NT):
                    for d in range(2):
                        ins = mm(bank(6 + i // 2, D, at=256 * (i % 2)), xnT[:, d, tile(i)], wvv[:, d, :], d == 0, d == 1)
                ins.then_inc(s1_v, 1)
                pe.wait_ge(s1_qs, 1 + k)
                pe.wait_ge(s1_ks, 1 + k)
                for i in range(NT):
                    for c in range(2):
                        ins = mm(bank(0, 128, at=128 * i), SQ[:, c, tile(i)], SK[:, c, tile(i)], c == 0, c == 1)
                ins.then_inc(s1_S, 1)
                pe.wait_ge(s1_P, 1 + k)
                for i in range(NT):
                    ins = PE.transpose(bank(1, 128, at=128 * i), SS[:, i, :], ident)
                ins.then_inc(s1_T, 1)
                pe.wait_ge(s1_PT, 1 + k)
                pe.wait_ge(s1_vs, 1 + k)
                pe.wait_ge(s1_vs_dve, 1 + k)
                for c in range(2):
                    for i in range(NT):
                        ins = mm(ps[:, 2 + c, tile(i)], SV[:, i, 128 * c:128 * c + 128], SPT[:, i, :])
                ins.then_inc(s1_o, 1)
                pe.wait_ge(s1_os_act, 1 + k)
                pe.wait_ge(s1_os_dve, 1 + k)
                project_out(l, (4, 5, 6, 7), lambda c, i: SO[:, c, tile(i)], lambda c: wo[:, c, :], 2, used=1)

            def spread_scores(k):
                for i in range(NT):
                    pe.wait_ge(rk_diag, 4 * k + i + 1)
                    mm(bank(2 + i, 512), C("same"), RDL).then_inc(rk_spread, 1)

            layernorm(0)
            narrow(0)
            layernorm(1)
            loaded("L0a_a")
            wd = unit("L0a_a", 0, 2, 128)
            for c in range(2):
                ins = mm(ps[:, 2, :], wd[:, c, :], xnT[:, c, :], c == 0, c == 1)
            ins.then_inc(sa_lat, 1)
            pe.wait_ge(sa_lats, 1)
            self16(0)
            layernorm(2)
            gate = C("L0f_gate").rearrange("p (c e) -> p c e", c=2)
            for i in range(NT):
                for c in range(2):
                    ins = mm(bank(2, 8, at=8 * i), xnT[:, c, tile(i)], gate[:, c, :], c == 0, c == 1)
            ins.then_inc(router_logits, 1)
            pe.wait_ge(router_d, 1)
            spread_scores(0)
            pe.wait_ge(L0f_sel, 1)
            for i in range(NT):
                for c in range(2):
                    ins = mm(bank(i, 256, at=256 * c), xn[:, i, 128 * c:128 * c + 128], SEL[:, i])
                ins.then_inc(gathered, 1)
            for e in range(8):
                ins = PE.transpose(bank(6, 128, at=128 * e), SELG[:, e], ident)
            ins.then_inc(comb_T, 1)
            pe.wait_ge(xin_act, 2)
            pe.wait_ge(xin_dve, 2)
            pe.wait_ge(comb_Ts, 1)

            def up(e):
                loaded(f"L0f_{e}_w1")
                w1 = unit(f"L0f_{e}_w1", 0, 2, 1024)
                for g in range(2):
                    if e >= 1:
                        pe.wait_ge(L0f_hs, 2 * e - 1 + g)
                    for m in range(4):
                        f = 4 * g + m
                        for c in range(2):
                            ins = mm(bank(4 + g, 128, at=128 * m), w1[:, c, 128 * f:128 * f + 128], XIN[:, c, e],
                                     c == 0, c == 1)
                    ins.then_inc(L0f_h, 1)

            def down(e):
                loaded(f"L0f_{e}_w2")
                w2 = unit(f"L0f_{e}_w2", 0, 8, D)
                if e >= 2:
                    pe.wait_ge(L0f_ys, e - 1)
                pe.wait_ge(L0f_hs, 2 * e + 2)
                for f in range(8):
                    ins = mm(bank(6 + e % 2, D), HT0[:, e % 2, f, :], w2[:, f, :], f == 0, f == 7)
                ins.then_inc(L0f_y, 1)
                pe.wait_ge(L0f_y, e + 1)
                release(2)

            up(0)
            for e in range(8):
                if e < 7:
                    up(e + 1)
                down(e)
            pe.wait_ge(L0f_ys, 8)
            for i in range(NT):
                for e in range(8):
                    R = slice(32 * i, 32 * i + 32)
                    ins = PE.matmul(ps[:, i, 0:D], SGT[R, e, :], YS[R, e, :], start=(e == 0), stop=(e == 7),
                                    tile_position=(32 * i, 0))
                ins.then_inc(layer_out, 1)
            layernorm(3)
            wide(0)
            layernorm(4)
            loaded("L1a_q")
            loaded("L1a_k")
            loaded("L1a_v")
            self16(1)
            layernorm(5)
            router = C("L1f_router").rearrange("p (c e) -> p c e", c=2)
            for i in range(NT):
                for c in range(2):
                    ins = mm(bank(2, 16, at=16 * i), xnT[:, c, tile(i)], router[:, c, :], c == 0, c == 1)
            ins.then_inc(router_logits, 1)
            pe.wait_ge(L1f_hot, 1)
            mm(bank(3, 64), C("tri"), TOH1)
            mm(bank(3, 64, at=64), C("tri"), TOH2, True, False)
            mm(bank(3, 64, at=64), C("same"), TU, False, True).then_inc(L1f_cum, 1)
            pe.wait_ge(L1f_disp, 1)
            for i in range(NT):
                for c in range(2):
                    ins = mm(bank(i, 256, at=256 * c), xn[:, i, 128 * c:128 * c + 128], TD[:, i])
                ins.then_inc(gathered, 1)
            pe.wait_ge(L1f_comb, 1)
            for i in range(NT):
                for g in range(2):
                    ins = PE.transpose(bank(4, 128, at=256 * i + 128 * g), TC[:, i, 8 * g:8 * g + 8, :], ident)
            ins.then_inc(comb_T, 1)
            pe.wait_ge(xin_act, 4)
            pe.wait_ge(xin_dve, 4)
            for g in range(2):
                for which, done, bk in ((0, L1f_gate, 2 * g), (1, L1f_up, 2 * g + 1)):
                    for m in range(8):
                        e = 8 * g + m
                        u = f"L1f_g{e // 4}"
                        if which == 0 and m % 4 == 0:
                            loaded(u)
                        ww = unit(u, 0, 4, 2, 256)[:, e % 4, :, 128 * which:128 * which + 128]
                        for c in range(2):
                            ins = mm(bank(bk, 64, at=64 * m), ww[:, c, :], TXIN[:, c, e], c == 0, c == 1)
                    ins.then_inc(done, 1)
                pe.wait_ge(L1f_up, g + 1)
                release(2)
            pe.wait_ge(comb_Ts, 2)
            pe.wait_ge(L1f_hs, 2)
            for c in range(2):
                for e in range(16):
                    if c == 0 and e % 8 == 0:
                        loaded(f"L1f_p{e // 8}")
                    wp = unit(f"L1f_p{e // 8}", 0, 8, D)
                    ins = mm(bank(4 + 2 * c, 64, at=64 * e), wp[:, e % 8, 128 * c:128 * c + 128], THT[:, e, :])
            ins.then_inc(L1f_o, 1)
            pe.wait_ge(L1f_o, 1)
            release(2)
            pe.wait_ge(L1f_os_act, 2)
            pe.wait_ge(L1f_os_dve, 2)
            for i in range(NT):
                for g in range(2):
                    for c in range(2):
                        ins = PE.transpose(bank(i, 128, at=256 * g + 128 * c), TOT[:, c, i, 8 * g:8 * g + 8, :],
                                           ident)
                ins.then_inc(L1f_oT, 1)
            pe.wait_ge(L1f_ons_act, 2)
            pe.wait_ge(L1f_ons_dve, 2)
            for i in range(NT):
                for g in range(2):
                    ins = mm(ps[:, 4 + i, 0:D], TCT[:, i, g, :], TON[:, i, g, :], g == 0, g == 1)
                ins.then_inc(layer_out, 1)
            layernorm(6)
            wide(1)
            layernorm(7)
            self1(0)
            layernorm(8)
            waff = C("L2f_waff").rearrange("p (c e) -> p c e", c=2)
            for i in range(NT):
                for c in range(2):
                    ins = mm(bank(2, 8, at=8 * i), xnT[:, c, tile(i)], waff[:, c, :], c == 0, c == 1)
            ins.then_inc(router_logits, 1)
            pe.wait_ge(L2f_w2, 1)
            wf2 = wv(5696, 2, 8)
            for c in range(2):
                ins = mm(bank(3, 8), C("ones"), wf2[:, c, :], c == 0, c == 1)
            ins.then_inc(L2f_wn, 1)
            pe.wait_ge(L2f_rowsum, 1)
            mm(bank(3, 2, at=8), C("ones"), RB_[:, 0:2]).then_inc(L2f_total, 1)
            pe.wait_ge(L2f_mean, 1)
            spread_scores(1)
            loaded("L2f_b2")
            b2 = unit("L2f_b2", 0, D, rows=slice(0, 8))

            def gather(e):
                pe.wait_ge(L2f_diag, e + 1)
                if e >= 1:
                    pe.wait_ge(L2f_xis_act, e)
                    pe.wait_ge(L2f_xis_dve, e)
                for c in range(2):
                    for i in range(NT):
                        ins = mm(ps[:, 6 + c, tile(i)], xn[:, i, 128 * c:128 * c + 128], EDG[:, e % 2, i, :])
                ins.then_inc(L2f_xi, 1)

            def up(n):
                e, f = n // 8, n % 8
                w1 = unit(f"L2f_{e}_w1", 0, 2, 1024)
                if f == 0:
                    loaded(f"L2f_{e}_w1")
                    pe.wait_ge(L2f_xis_act, e + 1)
                    pe.wait_ge(L2f_xis_dve, e + 1)
                if n >= 2:
                    pe.wait_ge(L2f_hs, n - 1)
                for c in range(2):
                    ins = mm(ps[:, 4 + n % 2, :], w1[:, c, 128 * f:128 * f + 128], EXI[:, e % 2, c, :], c == 0, c == 1)
                ins.then_inc(L2f_h, 1)

            def down(n):
                e, f = n // 8, n % 8
                w2 = unit(f"L2f_{e}_w2", 0, 8, D)
                if f == 0:
                    loaded(f"L2f_{e}_w2")
                pe.wait_ge(L2f_hs, n + 1)
                for i in range(NT):
                    ins = mm(ps[:, i, 0:D], EH[:, n % 4, tile(i)], w2[:, f, :], False, n == 63)
                    if n == 63:
                        ins.then_inc(layer_out, 1)
                if n < 63:
                    ins.then_inc(L2f_y, 1)
                if f == 7 and e < 7:
                    pe.wait_ge(L2f_y, n + 1)
                    release(2)

            gather(0)
            pe.wait_ge(rk_spread, 8)
            pe.wait_ge(L2f_diag, 1)
            for i in range(NT):
                mm(ps[:, i, 0:D], C("ones", slice(0, 8)), b2, True, False)
            up(0)
            for n in range(64):
                if n % 8 == 4 and n // 8 < 7:
                    gather(n // 8 + 1)
                if n < 63:
                    up(n + 1)
                down(n)
            pe.wait_ge(layer_out, 36)
            release(3)
            for b in range(16):
                pe.wait_ge(ctx_n, b + 1)
                if b >= 2:
                    pe.wait_ge(ctx_Ts_act, b - 1)
                    pe.wait_ge(ctx_Ts_dve, b - 1)
                for m in range(4):
                    t = 4 * b + m
                    PE.transpose(bank(4 + 2 * (b % 2), 128, at=128 * m), ctxN[:, t, 0:128], ident)
                    ins = PE.transpose(bank(5 + 2 * (b % 2), 128, rows=slice(0, D2), at=128 * m),
                                       ctxN[:, t, 128:DC], ident)
                ins.then_inc(ctx_T, 1)
                if b == 1:
                    layernorm("9b")
            loaded("L3x_a")
            wkk = unit("L3x_a", 898, 2, D)
            for c in range(2):
                mm(ps[:, 0, c:c + 1], wkk[:, 0, 128 * c:128 * c + 128], C("L3x_b2")[:, 0:1], True, False)
                ins = mm(ps[:, 0, c:c + 1], wkk[0:D2, 1, 128 * c:128 * c + 128], C("L3x_b2")[0:D2, 1:2],
                         False, True)
            ins.then_inc(na_kb, 1)
            pe.wait_ge(ctx_Ts_act, 16)
            pe.wait_ge(ctx_Ts_dve, 16)
            narrow(1)
            layernorm(10)
            self1(1)
            layernorm(11)
            loaded("L3f")
            win = unit("L3f", 0, 2, 64)
            wout = unit("L3f", 128, D)
            for h in range(2):
                for c in range(2):
                    ins = mm(ps[half(h), 2, 0:256], win[:, c, :], xnT[:, c, 256 * h:256 * h + 256], c == 0, c == 1)
            ins.then_inc(L3f_s, 1)
            pe.wait_ge(L3f_acc, 16)
            for i in range(NT):
                h = i // 2
                mm(ps[:, 3 + i, 0:D], C("ones", slice(0, 1)), unit("L3f", 384, D, rows=slice(0, 1)), True, False)
                mm(ps[:, 3 + i, 0:D], FG_[half(h), tile(i % 2)], wout[half(h)], False, True) \
                    .then_inc(layer_out, 1)


def chunks(a, width=None):
    k, n = a.shape
    c = -(-k // 128)
    p = np.zeros((c * 128, n), np.float32)
    p[:k] = a
    return p.reshape(c, 128, n).transpose(1, 0, 2).reshape(128, c * n)


def column(v):
    return chunks(np.asarray(v).reshape(-1, 1))


def row(v, width=None):
    p = np.zeros((128, v.size), np.float32)
    p[0] = v
    return p


def packed(g):
    u = {}
    cat = lambda *a: np.concatenate(a, axis=1)

    def keys_transposed(wk, bk):
        return chunks(np.concatenate([wk.T, np.asarray(bk).reshape(-1, 1)], axis=1))

    def with_row(a, r):
        return np.concatenate([a, np.asarray(r).reshape(1, -1)], axis=0)

    u["L0x_a"] = cat(chunks(g["L0_xattn_Wq"]), keys_transposed(g["L0_xattn_Wk"], g["L0_xattn_bk"]))
    u["L0x_b"] = chunks(with_row(g["L0_xattn_Wv"], g["L0_xattn_bv"]))

    def slots16(a):
        p = np.zeros((a.shape[0], a.shape[1] // 16, 64), np.float32)
        p[:, :, 0:16] = a.reshape(a.shape[0], -1, 16)
        return p.reshape(a.shape[0], -1)

    order = lambda a: a.reshape(a.shape[0], 4, 2, 2, 16).transpose(0, 3, 1, 2, 4).reshape(a.shape[0], 256)
    kv = g["L0_attn_Wkv_up"]
    u["L0a_a"] = cat(chunks(g["L0_attn_Wc_down"]), slots16(g["L0_attn_Wq_up"]),
                     slots16(np.concatenate([kv[:, :16], kv[:, :16]], axis=1)), kv[:, 16:])
    u["L0a_b"] = chunks(order(g["L0_attn_Wc_proj"].T).T)
    for e in range(8):
        u[f"L0f_{e}_w1"] = chunks(g["L0_ffn_w1"][e])
        u[f"L0f_{e}_w2"] = chunks(g["L0_ffn_w2"][e])
        u[f"L2f_{e}_w1"] = chunks(g["L2_ffn_W1"][e])
        u[f"L2f_{e}_w2"] = chunks(g["L2_ffn_W2"][e])
    for L, n in (("L1x", "L1_xattn"), ("L2x", "L2_xattn")):
        u[f"{L}_q"] = chunks(g[n + "_Wq"])
        p = np.zeros((8, 2, 2, 64, DC), np.float32)
        wk = g[n + "_Wk"].T.reshape(8, 2, 64, DC)
        for e in range(2):
            p[:, e, e] = wk[:, e]
        p = p.reshape(8, 2, 128, DC).transpose(2, 0, 1, 3)
        bo = np.zeros((128, D), np.float32)
        bo[0] = g[n + "_bo"]
        u[f"{L}_k0"] = cat(p[:, 0:4].reshape(128, -1), bo)
        u[f"{L}_k1"] = p[:, 4:8].reshape(128, -1)
        u[f"{L}_v"] = chunks(g[n + "_Wv"])
        u[f"{L}_o"] = chunks(g[n + "_Wo"])

    def qr(q, r):
        p = np.zeros((q.shape[0], 16, 64), np.float32)
        p[:, :, 0:16] = q.reshape(-1, 16, 16)
        p[:, :, 16:48] = r.reshape(-1, 16, 32)
        return p.reshape(q.shape[0], 1024)

    u["L1a_q"] = chunks(qr(g["L1_attn_Wq"], g["L1_attn_Wr"]))
    u["L1a_k"] = chunks(qr(g["L1_attn_Wk"], g["L1_attn_Wr"]))
    u["L1a_v"] = cat(chunks(order(g["L1_attn_Wv"])), chunks(order(g["L1_attn_Wo"].T).T),
                     row(order(g["L1_attn_bv"].reshape(1, -1))[0]), row(g["L1_attn_bo"]))
    for q in range(4):
        u[f"L1f_g{q}"] = np.concatenate([chunks(np.concatenate([g["L1_ffn_w_gate"][e], g["L1_ffn_w_fc"][e]], axis=1))
                                         for e in range(4 * q, 4 * q + 4)], axis=1)
    for q in range(2):
        u[f"L1f_p{q}"] = np.concatenate([g["L1_ffn_w_proj"][e] for e in range(8 * q, 8 * q + 8)], axis=1)
    u["L2a"] = cat(*(chunks(g["L2_attn_" + n]) for n in ("Wq", "Wk", "Wv", "Wo")))
    b2 = np.zeros((128, D), np.float32)
    b2[:8] = g["L2_ffn_b2"]
    u["L2f_b2"] = b2
    u["L3x_a"] = cat(chunks(g["L3_xattn_Wq"]), keys_transposed(g["L3_xattn_Wk"], g["L3_xattn_bk"]),
                     chunks(g["L3_xattn_Wk"]))
    u["L3x_b"] = cat(chunks(with_row(g["L3_xattn_Wv"], g["L3_xattn_bv"])), chunks(g["L3_xattn_Wo"]),
                     row(g["L3_xattn_bo"]))
    w = g["L3_attn_W_qkv"]
    u["L3a"] = cat(*(chunks(w[n::3].T) for n in range(3)), chunks(g["L3_attn_W_out"].T))
    wout = g["L3_ffn_Wout"]
    u["L3f"] = cat(chunks(g["L3_ffn_Win"]), np.concatenate([wout, wout], axis=0), row(g["L3_ffn_bout"]))

    c = {}
    p = np.arange(128)
    par, t = p // 64, p % 64
    same = par[:, None] == par[None, :]
    c["ident"] = np.eye(128)
    c["ones"] = np.ones((128, 128))
    c["same"] = same
    c["tri"] = same & (t[:, None] <= t[None, :])
    s = np.arange(64)
    c["delta"] = t[:, None] == s[None, :]
    neg = -1e30
    c["causal"] = np.where(s[None, :] <= t[:, None], 0.0, neg)
    c["bfull"] = np.where(same, 0.0, neg)
    c["bcausal"] = np.where(same & (t[None, :] <= t[:, None]), 0.0, neg)
    c["before"] = s[None, :] < t[:, None]
    r = np.arange(32)
    c["slot32"] = np.where((r // 16)[None, :] == par[:, None], (r % 16)[None, :], -1)
    r = np.arange(16)
    c["slot16"] = np.where((r // 8)[None, :] == par[:, None], (r % 8)[None, :] + 1, -1)
    c["rev8"] = np.tile(8 - np.arange(8), (128, 1))
    c["rev16"] = np.tile(16 - np.arange(16), (128, 1))
    c["nhalf"] = np.full((128, 64), -0.5)
    c["half"] = np.full((128, 8), 0.5)
    c = {n: np.asarray(a, np.float32) for n, a in c.items()}
    c["L0x_bq"] = column(g["L0_xattn_bq"])
    c["L1a_bq"] = column(qr(g["L1_attn_bq"].reshape(1, -1), g["L1_attn_br"].reshape(1, -1))[0])
    c["L1a_bk"] = column(qr(g["L1_attn_bk"].reshape(1, -1), g["L1_attn_br"].reshape(1, -1))[0])
    c["L2f_b1"] = column(g["L2_ffn_b1"].reshape(-1))
    c["L2f_waff"] = chunks(g["L2_ffn_waff"].T)
    c["L2f_thr"] = np.broadcast_to(g["L2_ffn_affinity_threshold"].reshape(1, 1), (128, 1))
    c["L0f_gate"] = chunks(g["L0_ffn_gate_w"])
    c["L1f_router"] = chunks(g["L1_ffn_w_router"])
    for n, k in (("g1", "ln1_g"), ("b1", "ln1_b"), ("g2", "ln2_g"), ("b2", "ln2_b"), ("bq", "bq"), ("bk", "bk")):
        c["L3x_" + n] = column(g["L3_xattn_" + k])
    twice = lambda a: np.concatenate([a, a], axis=0)
    c["L3f_bin"] = twice(g["L3_ffn_bin_"].reshape(-1, 1))
    c["L3f_W1"], c["L3f_b1"], c["L3f_W2"] = (twice(g["L3_ffn_" + n]) for n in ("W1", "b1", "W2"))
    c["L3f_b2"] = twice(g["L3_ffn_b2"].reshape(-1, 1))
    const = np.concatenate([c[n].reshape(128, -1) for n in CW], axis=1)
    assert const.shape == (128, NCONST)
    widths = {n: u[n].shape[1] for n in UNITS}
    assert max(widths.values()) <= SLOT, widths
    units = np.concatenate([u[n].reshape(-1) for n in UNITS])
    return widths, np.ascontiguousarray(units), np.ascontiguousarray(const)


def kernel(**inputs):
    import concourse.bacc as _bacc
    from concourse.bass_utils import run_bass_kernel_spmd as _run

    g = {k: np.asarray(v) for k, v in inputs.items()}
    widths, units, const = packed(g)
    c = g["ctx_768"]
    cT = c.transpose(2, 0, 1).reshape(DC, B * LK)
    arrays = {
        "units": units, "consts": const,
        "ctxT1": np.ascontiguousarray(cT[0:128]),
        "ctxT2": np.concatenate([cT[128:DC], np.ones((1, B * LK), np.float32)], axis=0),
        "ctxN": np.ascontiguousarray(c.reshape(B * KT, 128, DC).transpose(1, 0, 2)),
        "x_in": np.ascontiguousarray(g["x"].reshape(NT, 128, D).transpose(1, 0, 2)),
    }
    nc = _bacc.Bacc("TRN2", target_bir_lowering=False, num_devices=1)
    aps = {n: nc.dram_tensor(n, a.shape, F32, kind="ExternalInput").ap() for n, a in arrays.items()}
    out = nc.dram_tensor("out", (128, NT, D), F32, kind="ExternalOutput").ap()
    build(nc, widths, aps["units"], aps["consts"], aps["ctxT1"], aps["ctxT2"], aps["ctxN"], aps["x_in"], out)
    r = _run(nc, [arrays], core_ids=[0])
    return r.results[0]["out"].transpose(1, 0, 2).reshape(B, S, D)
```

```python
import numpy as np
import concourse.bass as bass
from concourse import mybir
from contextlib import ExitStack

F32 = mybir.dt.float32
BF16 = mybir.dt.bfloat16
F16 = mybir.dt.float16
ALU = mybir.AluOpType
ACT = mybir.ActivationFunctionType
X = mybir.AxisListType.X

B, S, D = 8, 64, 256
LK, DC = 1024, 192
TOK = B * S
NT = TOK // 128
KT = LK // 128
D2 = DC - 128
HB, DHB = 16, 64
NPAIR = HB // 2
LAYERS = 12
CAP = 512

SLOT = 2048
NSLOT = 7

GROUP = 4
NGROUP = B * KT // GROUP
STAGES = 6
FIRST_STAGE_SLOT = NSLOT - STAGES // 2

UNITS = ["L0x_a", "L0x_b", "L0a_a", "L0a_b"]
UNITS += [f"L0f_{e}_{w}" for e in range(8) for w in ("w1", "w2")]
UNITS += ["L1x_q", "L1x_k0", "L1x_k1", "L1x_v", "L1x_o", "L1a_q", "L1a_k", "L1a_v"]
UNITS += [f"L1f_g{g}" for g in range(4)] + [f"L1f_p{g}" for g in range(2)]
UNITS += ["L2x_q", "L2x_k0", "L2x_k1", "L2x_v", "L2x_o", "L2a", "L2f_b2"]
UNITS += [f"L2f_{e}_{w}" for e in range(8) for w in ("w1", "w2")]
UNITS += ["L3x_a", "L3x_b", "L3a", "L3f"]
UIDX = {u: n for n, u in enumerate(UNITS)}

CW = {}
_at = 0
for _name, _width in (
    ("ident", 128), ("ones", 128), ("same", 128), ("tri", 128), ("delta", 64), ("causal", 64),
    ("bcausal", 128), ("bfull", 128), ("before", 64), ("slot32", 32), ("slot16", 16), ("rev8", 8),
    ("rev16", 16), ("nhalf", 64), ("half", 8),
    ("L0x_bq", 2), ("L1a_bq", 8), ("L1a_bk", 8), ("L2f_b1", 64), ("L2f_waff", 16), ("L2f_thr", 1),
    ("L0f_gate", 16), ("L1f_router", 32),
    ("L3x_g1", 2), ("L3x_b1", 2), ("L3x_g2", 2), ("L3x_b2", 2), ("L3x_bq", 2), ("L3x_bk", 2),
    ("L3f_bin", 1), ("L3f_W1", 16), ("L3f_b1", 16), ("L3f_W2", 16), ("L3f_b2", 1),
):
    CW[_name] = (_at, _width)
    _at += _width
NCONST = _at


def build(nc, widths, units_d, const_d, ctx_d, x_d, out_d):
    ctx = ExitStack()
    with ctx:
        sem = lambda name: ctx.enter_context(nc.semaphore(name))
        consts_loaded, out_stored, x_final, x_loaded = sem("consts_loaded"), sem("out_stored"), sem("x_final"), sem("x_loaded")
        units_used = sem("units_used")
        dve_step, pool_step = sem("dve_step"), sem("pool_step")
        ln_T, ln_rstd, ln_stats, ln_xn = sem("ln_T"), sem("ln_rstd"), sem("ln_stats"), sem("ln_xn")
        ln_xnT_act, ln_xnT_dve = sem("ln_xnT_act"), sem("ln_xnT_dve")
        layer_out = sem("layer_out")
        xa_A, xa_AH, xa_AL, xa_O, xa_OT = sem("xa_A"), sem("xa_AH"), sem("xa_AL"), sem("xa_O"), sem("xa_OT")
        xa_P, xa_PTH, xa_PTL, xa_S = sem("xa_P"), sem("xa_PTH"), sem("xa_PTL"), sem("xa_S")
        xa_T, xa_Z, xa_ZT, xa_ZTs = sem("xa_T"), sem("xa_Z"), sem("xa_ZT"), sem("xa_ZTs")
        xa_Zs, xa_max, xa_q, xa_qs = sem("xa_Zs"), sem("xa_max"), sem("xa_q"), sem("xa_qs")
        xa_recip = sem("xa_recip")
        na_A, na_AH, na_AL, na_P = sem("na_A"), sem("na_AH"), sem("na_AL"), sem("na_P")
        na_PTH, na_PTL, na_S = sem("na_PTH"), sem("na_PTL"), sem("na_S")
        na_T, na_Z, na_ZT, na_ZTs = sem("na_T"), sem("na_Z"), sem("na_ZT"), sem("na_ZTs")
        na_Zs, na_kb, na_kbs, na_max = sem("na_Zs"), sem("na_kb"), sem("na_kbs"), sem("na_max")
        na_ones, na_q, na_qs = sem("na_ones"), sem("na_q"), sem("na_qs")
        na_v, na_vs = sem("na_v"), sem("na_vs")
        sa_P, sa_PT, sa_S, sa_T = sem("sa_P"), sem("sa_PT"), sem("sa_S"), sem("sa_T")
        sa_d, sa_exp, sa_k, sa_k0 = sem("sa_d"), sem("sa_exp"), sem("sa_k"), sem("sa_k0")
        sa_ks0, sa_ks_act, sa_ks_dve, sa_lat = sem("sa_ks0"), sem("sa_ks_act"), sem("sa_ks_dve"), sem("sa_lat")
        sa_lats, sa_q, sa_qs_act, sa_qs_dve = sem("sa_lats"), sem("sa_q"), sem("sa_qs_act"), sem("sa_qs_dve")
        sa_v, sa_vs, sa_y, sa_ys = sem("sa_v"), sem("sa_vs"), sem("sa_y"), sem("sa_ys")
        s1_P, s1_PT, s1_S, s1_T = sem("s1_P"), sem("s1_PT"), sem("s1_S"), sem("s1_T")
        s1_d, s1_exp, s1_k, s1_ks = sem("s1_d"), sem("s1_exp"), sem("s1_k"), sem("s1_ks")
        s1_o, s1_os, s1_q = sem("s1_o"), sem("s1_os"), sem("s1_q")
        s1_qs, s1_v, s1_vs = sem("s1_qs"), sem("s1_v"), sem("s1_vs")
        comb_T, comb_Ts, gathered, rk_diag = sem("comb_T"), sem("comb_Ts"), sem("gathered"), sem("rk_diag")
        rk_spread, router_d = sem("rk_spread"), sem("router_d")
        router_exp, router_logits = sem("router_exp"), sem("router_logits")
        xin_copied = sem("xin_copied")
        L0f_h, L0f_hs, L0f_sel, L0f_y = sem("L0f_h"), sem("L0f_hs"), sem("L0f_sel"), sem("L0f_y")
        L0f_ys = sem("L0f_ys")
        L1f_comb, L1f_cum, L1f_disp, L1f_gate = sem("L1f_comb"), sem("L1f_cum"), sem("L1f_disp"), sem("L1f_gate")
        L1f_hot, L1f_hs, L1f_o, L1f_oT = sem("L1f_hot"), sem("L1f_hs"), sem("L1f_o"), sem("L1f_oT")
        L1f_ons = sem("L1f_ons")
        L1f_os = sem("L1f_os")
        L1f_silu, L1f_up = sem("L1f_silu"), sem("L1f_up")
        L2f_diag, L2f_h, L2f_hs, L2f_mean = sem("L2f_diag"), sem("L2f_h"), sem("L2f_hs"), sem("L2f_mean")
        L2f_norms, L2f_norms2, L2f_rowsum, L2f_sig = sem("L2f_norms"), sem("L2f_norms2"), sem("L2f_rowsum"), sem("L2f_sig")
        L2f_total, L2f_w2, L2f_wn, L2f_xi = sem("L2f_total"), sem("L2f_w2"), sem("L2f_wn"), sem("L2f_xi")
        L2f_xis_act, L2f_xis_dve, L2f_y = sem("L2f_xis_act"), sem("L2f_xis_dve"), sem("L2f_y")
        cx_stats, cx_rstd, cx_n, cx_hi, cx_lo = sem("cx_stats"), sem("cx_rstd"), sem("cx_n"), sem("cx_hi"), sem("cx_lo")
        cx_T, cx_Ts_act, cx_Ts_dve = sem("cx_T"), sem("cx_Ts_act"), sem("cx_Ts_dve")
        L3f_acc, L3f_relu, L3f_s, L3f_ss = sem("L3f_acc"), sem("L3f_relu"), sem("L3f_s"), sem("L3f_ss")
        slot_loaded = [sem(f"slot{n}_loaded") for n in range(NSLOT)]
        stage_loaded = [sem(f"stage{n}_loaded") for n in range(STAGES)]

        sb = lambda name, shape, dt=F32: ctx.enter_context(nc.sbuf_tensor(name, shape, dt))
        CN = sb("ctx_keys", [128, B * KT, 2 * DC], F16)
        CT = sb("ctx_T", [128, 3, B * LK], F16)
        ident16 = sb("ident16", [128, 128], F16)
        ring = sb("ring", [128, NSLOT, SLOT])
        cst = sb("cst", [128, NCONST])
        x = sb("x", [128, NT, D])
        xn = sb("xn", [128, NT, D])
        xnT = sb("xnT", [128, 2, TOK])
        WORK = 9800
        wk = sb("wk", [128, WORK])
        ps = ctx.enter_context(nc.psum_tensor("ps", [128, 8, 512], F32))

        PE, DVE, ACTE, POOL = nc.tensor, nc.vector, nc.scalar, nc.gpsimd

        def C(name, rows=slice(0, 128)):
            at, width = CW[name]
            return cst[rows, at:at + width]

        def wv(at, *dims, rows=slice(0, 128)):
            n = int(np.prod(dims))
            assert at + n <= WORK
            ap = wk[rows, at:at + n]
            if len(dims) == 2:
                ap = ap.rearrange("p (a b) -> p a b", b=dims[1])
            if len(dims) == 3:
                ap = ap.rearrange("p (a b c) -> p a b c", b=dims[1], c=dims[2])
            if len(dims) == 4:
                ap = ap.rearrange("p (a b c d) -> p a b c d", b=dims[1], c=dims[2], d=dims[3])
            return ap

        def wh(at, *dims, rows=slice(0, 128)):
            n = int(np.prod(dims))
            assert n % 2 == 0 and at + n // 2 <= WORK
            ap = wk[rows, at:at + n // 2].bitcast(F16)
            if len(dims) == 2:
                ap = ap.rearrange("p (a b) -> p a b", b=dims[1])
            if len(dims) == 3:
                ap = ap.rearrange("p (a b c) -> p a b c", b=dims[1], c=dims[2])
            return ap

        def unit(name, at, *dims, rows=slice(0, 128)):
            n = int(np.prod(dims))
            assert at + n <= widths[name], (name, at, dims)
            ap = ring[rows, UIDX[name] % NSLOT, at:at + n]
            if len(dims) == 2:
                ap = ap.rearrange("p (a b) -> p a b", b=dims[1])
            if len(dims) == 3:
                ap = ap.rearrange("p (a b c) -> p a b c", b=dims[1], c=dims[2])
            return ap

        def bank(n, *dims, rows=slice(0, 128), at=0):
            m = int(np.prod(dims))
            nb = max(1, (at + m + 511) // 512)
            ap = ps[rows, n:n + nb, :].rearrange("p a b -> p (a b)")[:, at:at + m]
            if len(dims) == 2:
                ap = ap.rearrange("p (a b) -> p a b", b=dims[1])
            if len(dims) == 3:
                ap = ap.rearrange("p (a b c) -> p a b c", b=dims[1], c=dims[2])
            if len(dims) == 4:
                ap = ap.rearrange("p (a b c d) -> p a b c d", b=dims[1], c=dims[2], d=dims[3])
            return ap

        def half(par):
            return slice(64 * par, 64 * par + 64)

        def mm(out, lhsT, rhs, start=True, stop=True):
            return PE.matmul(out, lhsT, rhs, start=start, stop=stop)

        ident = C("ident")

        st6 = sb("st6", [128, NT, 6])
        mv = sb("mv", [128, NT, 2])
        rstd = sb("rstd", [128, 2 * NT])
        XQ = wv(0, NPAIR, TOK)
        XP = wv(4096, 2, 1024)
        PTH = wh(6144, 2, KT, 128)
        PTL = wh(7168, 2, KT, 128)
        XAH = wh(8192, 2, 256)
        XAL = wh(8448, 2, 256)
        XZ = wv(8704, 2, DC)
        XZT = wv(9088, 2, 256)
        XNM, XRS, XRI = wv(9600, 4), wv(9604, 4), wv(9608, 4)
        NAH, NAL = wh(0, 2, TOK), wh(512, 2, TOK)
        NCR, ONES16 = wh(8192, TOK, rows=slice(0, 33)), wh(8448, TOK, rows=slice(0, 33))
        NKB = wv(9100, 2, 33)
        NQ = wv(1024, 2, TOK)
        NZT1, NZT2 = wv(2048, TOK), wv(2560, TOK)
        NV = wv(3072, 2, TOK)
        QC, KC = wv(0, 8, 256), wv(2048, 8, 256)
        VB = wv(4096, 4, 8, 32)
        LAT = wv(5120, TOK)
        SC = wv(5632, 2, 512)
        PT = wv(6656, 2, 512)
        YT = wv(7680, 2, TOK)
        AMX, ASM, ARC = wv(8704, 2, 8), wv(8720, 2, 8), wv(8736, 2, 8)
        SQ, SK = wv(0, 2, TOK), wv(1024, 2, TOK)
        SV = wv(2048, NT, D)
        SS = wv(3072, NT, 128)
        SPT = wv(3584, NT, 128)
        SO = wv(4096, 2, TOK)
        SMX, SSM, SRC = wv(5120, NT), wv(5124, NT), wv(5128, NT)
        RP = wv(9616, NT, 8)
        RK = wv(9648, NT, 8)
        RA, RB_, RC_ = wv(9680, 4), wv(9684, 4), wv(9688, 4)
        RL = wv(9692, NT, 8)
        ROH = wv(9724, NT, 8)
        RT = wv(9756, NT, 8)
        RS1 = wv(9788, 8)
        RDL = wv(7232, 8, 64)
        RG, RE = wv(5184, 8, 64), wv(5696, 8, 64)
        SEL = wv(64, NT, 8, 32)
        SELG = wv(1088, 8, NT, 32)
        SGT = wv(2112, 8, 128)
        XIN = wv(3136, 2, 8, NT, 32)
        HT0 = wv(5184, 2, 8, 128)
        YS = wv(7232, 8, D)
        TP = wv(0, NT, 16)
        TOH1, TOH2, TQ1, TQ2 = wv(64, NT, 16), wv(128, NT, 16), wv(192, NT, 16), wv(256, NT, 16)
        TT, TU = wv(320, NT, 16), wv(384, NT, 16)
        TM1, TM2, TV = wv(448, NT), wv(452, NT), wv(456, NT)
        TD = wv(1024, NT, 16, 16)
        TC = wv(2048, NT, 16, 16)
        TX_ = wv(6144, NT, 16, 16)
        TCT = wv(3072, NT, 2, 128)
        TXIN = wv(4096, 2, 16, NT, 16)
        TSG = wv(6144, 2, 512)
        THT = wv(7168, 16, 64)
        TOT = wv(4096, 2, NT, 16, 16)
        TON = wv(6144, NT, 2, D)
        EXI = wv(0, 2, 2, TOK)
        EDG = wv(2048, 2, NT, 128)
        EH = wv(3072, 4, TOK)
        FS, FT, FG_ = wv(0, 256), wv(256, 4, 256), wv(1280, 256)

        def stage(p, g):
            if p == 0:
                n = g % STAGES
                ap = ring[:, FIRST_STAGE_SLOT + n // 2, GROUP * DC * (n % 2):GROUP * DC * (n % 2 + 1)]
                return ap.rearrange("p (a b) -> p a b", b=DC)
            return wv(7744 + GROUP * DC * (g % 2), GROUP, DC)

        def stage_value(p, g):
            before = len(range(g % 2, NGROUP, STAGES))
            return 16 * (g // STAGES + 1) if p == 0 else 16 * (before + g // 2 + 1)

        PST6, PMV, PRS = wv(9280, 2, GROUP, 6), wv(9328, 2, GROUP, 2), wv(9344, 2, GROUP)

        def ctx_banks(p, g):
            return 2 + 2 * (g % 3) if p == 0 else 2

        LN = {l: l for l in range(10)} | {"9b": 10, 10: 11, 11: 12}
        LNT = {l: l for l in range(9)} | {"9b": 9, 10: 10, 11: 11}

        block = ctx.enter_context(nc.Block())

        @block.sync
        def _(sp):
            sp.dma_start(x[:, :, :], x_d).then_inc(x_loaded, 16)
            sp.dma_start(cst[:, :], const_d).then_inc(consts_loaded, 16)
            at = 0

            def load(n):
                nonlocal at
                name = UNITS[n]
                if n >= NSLOT:
                    sp.wait_ge(units_used, n - NSLOT + 1)
                w = widths[name]
                sp.dma_start(ring[:, n % NSLOT, 0:w], units_d[at:at + 128 * w].rearrange("(p w) -> p w", p=128)) \
                    .then_inc(slot_loaded[n % NSLOT], 16)
                at += 128 * w

            load(0)
            for g in range(NGROUP):
                if g >= STAGES:
                    sp.wait_ge(cx_lo, g - STAGES + 1)
                sp.dma_start(stage(0, g), ctx_d[:, GROUP * g:GROUP * g + GROUP, :]).then_inc(stage_loaded[g % STAGES], 16)
            for n in range(1, len(UNITS)):
                if n == FIRST_STAGE_SLOT:
                    sp.wait_ge(cx_lo, NGROUP)
                load(n)
                if UNITS[n][:4] == "L2f_" and UNITS[n][-2:] == "w2":
                    e = int(UNITS[n][4])
                    if e == 0:
                        sp.wait_ge(layer_out, 4 * 6 + 4)
                    for g in (2 * e, 2 * e + 1):
                        if g >= 2:
                            sp.wait_ge(cx_lo, NGROUP + g - 1)
                        sp.dma_start(stage(1, g), ctx_d[:, GROUP * g:GROUP * g + GROUP, :]).then_inc(stage_loaded[g % 2], 16)
            sp.wait_ge(x_final, NT)
            sp.dma_start(out_d, x[:, :, :]).then_inc(out_stored, 16)
            sp.wait_ge(out_stored, 16)

        @block.gpsimd
        def _(pool):
            pool.wait_ge(consts_loaded, 16)

            def rsqrt(n, src, dst, cols, eps):
                pool.wait_ge(ln_stats, n + 1)
                POOL.tensor_scalar(dst, src, float(eps), None, ALU.add).then_inc(pool_step, 1)
                pool.wait_ge(pool_step, n + 1 if n <= 8 else n + 1 + NGROUP)
                POOL.tensor_tensor(dst, dst, C("nhalf")[:, 0:cols], ALU.pow).then_inc(ln_rstd, 1)

            n = 0
            for l in range(LAYERS):
                rsqrt(n, mv[:, :, 1], rstd[:, 0:NT], NT, 1e-5)
                n += 1
                if l == 9:
                    rsqrt(n, mv[:, :, 1], rstd[:, 0:NT], NT, 1e-5)
                    n += 1
                if l == 8:
                    pool.wait_ge(L2f_norms2, 2)
                    POOL.tensor_tensor(RA, RA, C("half")[:, 0:NT], ALU.pow).then_inc(L2f_norms, 1)
                    POOL.tensor_tensor(RS1, RS1, C("half")[:, 0:8], ALU.pow).then_inc(L2f_norms, 1)
                    for g in range(NGROUP):
                        pool.wait_ge(cx_stats, g + 1)
                        r = PRS[:, g % 2, :]
                        POOL.tensor_scalar(r, PMV[:, g % 2, :, 1], 1e-5, None, ALU.add).then_inc(pool_step, 1)
                        pool.wait_ge(pool_step, n + g + 1)
                        POOL.tensor_tensor(r, r, C("nhalf")[:, 0:GROUP], ALU.pow).then_inc(cx_rstd, 1)

        @block.scalar
        def _(act):
            act.wait_ge(consts_loaded, 16)

            def layernorm(key, affine=None):
                act.wait_ge(ln_T, LNT[key] + 1)
                if affine is None:
                    ACTE.copy(xnT[:, 0, :], ps[:, 0, :]).then_inc(ln_xnT_act, 1)
                else:
                    g, b = affine
                    ACTE.activation(xnT[:, 0, :], ps[:, 0, :], ACT.Identity, scale=C(g)[:, 0:1],
                                    bias=C(b)[:, 0:1]).then_inc(ln_xnT_act, 1)

            def wide(k):
                for r in range(0, NPAIR, 2):
                    act.wait_ge(xa_q, 8 * k + r + 1)
                    ACTE.mul(XQ[:, r, :], ps[:, r, :], DHB ** -0.5).then_inc(xa_qs, 1)

                def queries(t, r):
                    act.wait_ge(xa_A, t + 1)
                    ACTE.copy(XAH[:, r % 2, :], bank(7, 256)).then_inc(xa_AH, 1)

                def exp(t, r, first):
                    act.wait_ge(xa_max, t + 1)
                    if not first:
                        act.wait_ge(xa_T, 2 * t - 2)
                    ACTE.activation(XP[:, r % 2, :], bank(2 * (r % 2), 1024), ACT.Exp, bias=XNM[:, r % 4:r % 4 + 1],
                                    accum_out=XRS[:, r % 4:r % 4 + 1]).then_inc(xa_P, 1)

                def spread(t, r, first):
                    if not first:
                        act.wait_ge(xa_Z, t - 1)
                    for g in range(2):
                        act.wait_ge(xa_T, 2 * t + g + 1)
                        ACTE.copy(PTH[:, r % 2, 4 * g:4 * g + 4, :], bank(4 + g, 4, 128)).then_inc(xa_PTH, 1)

                def heads(t, r, b):
                    act.wait_ge(xa_O, t + 1)
                    ACTE.copy(XQ[:, r, bass.ds(b * 64, 64)], bank(7, 64, at=256)).then_inc(xa_OT, 1)

                def batch(b, first, last):
                    t0 = 64 * k + 8 * b if isinstance(b, int) else b * 8 + 64 * k
                    for r in range(NPAIR):
                        t = t0 + r
                        if not (last and r == NPAIR - 1):
                            queries(t + 1, r + 1)
                        if not (first and r < 1):
                            spread(t - 1, (r - 1) % NPAIR, first and r < 3)
                        if not (first and r < 3):
                            heads(t - 3, (r - 3) % NPAIR, b if r >= 3 else b - 1)
                        exp(t, r, first and r < 2)

                queries(64 * k, 0)
                batch(0, True, False)
                with act.Fori(1, B - 1) as b:
                    batch(b, False, False)
                batch(B - 1, False, True)
                t1 = 64 * (k + 1)
                spread(t1 - 1, 7, False)
                for r in (5, 6, 7):
                    heads(t1 - 8 + r, r, B - 1)

            def split_high(p, g):
                if p == 0:
                    act.wait_ge(stage_loaded[g % STAGES], stage_value(0, g))
                else:
                    act.wait_ge(cx_n, g + 1)
                ACTE.copy(CN[:, GROUP * g:GROUP * g + GROUP, 0:DC], stage(p, g)).then_inc(cx_hi, 1)

            def spread_high(p, g):
                act.wait_ge(cx_T, NGROUP * p + g + 1)
                ACTE.copy(CT[:, 0:2, 512 * g:512 * g + 512],
                          bank(ctx_banks(p, g), 512).bitcast(F16).rearrange("p (a b) -> p a b", b=512)) \
                    .then_inc(cx_Ts_act, 1)

            def narrow(k):
                for c in range(3):
                    act.wait_ge(na_A, 3 * k + c + 1)
                    if c == 2:
                        ACTE.copy(NCR, bank(6, TOK, rows=slice(0, 33))).then_inc(na_AH, 1)
                    elif k == 0:
                        ACTE.copy(NAH[:, c, :], ps[:, 4 + c, :]).then_inc(na_AH, 1)
                    else:
                        ACTE.activation(NAH[:, c, :], ps[:, 4 + c, :], ACT.Identity,
                                        scale=C("L3x_g2")[:, c:c + 1]).then_inc(na_AH, 1)

                def spread(i):
                    t = 4 * k + i
                    if i >= 2:
                        act.wait_ge(na_Z, t - 1)
                    for g in range(2):
                        act.wait_ge(na_T, 2 * t + g + 1)
                        ACTE.copy(PTH[:, i % 2, 4 * g:4 * g + 4, :], bank(4 + g, 4, 128)).then_inc(na_PTH, 1)

                for i in range(NT):
                    t = 4 * k + i
                    act.wait_ge(na_max, t + 1)
                    if i >= 2:
                        act.wait_ge(na_T, 2 * t - 2)
                    ACTE.activation(XP[:, i % 2, :], bank(2 * (i % 2), 1024), ACT.Exp, bias=XNM[:, i:i + 1],
                                    accum_out=XRS[:, i:i + 1]).then_inc(na_P, 1)
                    if i >= 1:
                        spread(i - 1)
                spread(NT - 1)

            def self16(k):
                scale = 0.25 if k == 0 else 48 ** -0.5
                for h in range(2):
                    for r in (0, 1, 4, 5):
                        act.wait_ge(sa_q, 8 * k + 4 * h + r // 2 + 1)
                        src = bank(r // 2, 256, at=256 * (r % 2))
                        if k == 0:
                            ACTE.copy(QC[:, r, :], src).then_inc(sa_qs_act, 1)
                        else:
                            ACTE.activation(QC[:, r, :], src, ACT.Identity,
                                            bias=C("L1a_bq")[:, r:r + 1]).then_inc(sa_qs_act, 1)
                    for r in (0, 1, 4, 5):
                        if k == 1:
                            act.wait_ge(sa_k, 4 * h + r // 2 + 1)
                            ACTE.activation(KC[:, r, :], bank(4 + r // 2, 256, at=256 * (r % 2)), ACT.Identity,
                                            bias=C("L1a_bk")[:, r:r + 1]).then_inc(sa_ks_act, 1)
                    for u in range(4):
                        t = 8 * k + 4 * h + u
                        act.wait_ge(sa_d, t + 1)
                        ACTE.activation(SC[:, u % 2, :], SC[:, u % 2, :], ACT.Exp, scale=scale).then_inc(sa_exp, 1)
                        if u >= 1:
                            act.wait_ge(sa_T, t)
                            ACTE.copy(PT[:, (u - 1) % 2, :], ps[:, 2 + (u - 1) % 2, :]).then_inc(sa_PT, 1)
                    act.wait_ge(sa_T, 8 * k + 4 * h + 4)
                    ACTE.copy(PT[:, 1, :], ps[:, 3, :]).then_inc(sa_PT, 1)
                    act.wait_ge(sa_y, 2 * k + h + 1)
                    ACTE.copy(YT[:, 0, 256 * h:256 * h + 256], ps[:, 4, 256 * h:256 * h + 256]).then_inc(sa_ys, 1)

            def self1(k):
                act.wait_ge(s1_q, 1 + k)
                ACTE.copy(SQ, bank(2, 2, TOK)).then_inc(s1_qs, 1)
                act.wait_ge(s1_v, 1 + k)
                ACTE.copy(SV[:, 0:2, :], bank(6, 2, D)).then_inc(s1_vs, 1)
                act.wait_ge(s1_d, 1 + k)
                ACTE.activation(SS, SS, ACT.Exp, scale=D ** -0.5).then_inc(s1_exp, 1)
                act.wait_ge(s1_T, 1 + k)
                ACTE.copy(SPT, bank(1, NT, 128)).then_inc(s1_PT, 1)
                act.wait_ge(s1_o, 1 + k)
                ACTE.copy(SO[:, 0, :], ps[:, 2, :]).then_inc(s1_os, 1)

            layernorm(0)
            for g in range(NGROUP):
                split_high(0, g)
                if g >= 2:
                    spread_high(0, g - 2)
            spread_high(0, NGROUP - 2)
            spread_high(0, NGROUP - 1)
            narrow(0)
            layernorm(1)
            act.wait_ge(sa_lat, 1)
            ACTE.copy(LAT, ps[:, 2, :]).then_inc(sa_lats, 1)
            self16(0)
            layernorm(2)
            act.wait_ge(router_d, 1)
            ACTE.activation(RP, RP, ACT.Exp).then_inc(router_exp, 1)
            act.wait_ge(comb_T, 1)
            ACTE.copy(SGT, bank(6, 8, 128)).then_inc(comb_Ts, 1)
            for i in range(0, NT, 2):
                act.wait_ge(gathered, i + 1)
                ACTE.copy(XIN[:, :, :, i, :], bank(i, 2, 8, 32)).then_inc(xin_copied, 1)
            for e in range(8):
                for g in range(2):
                    act.wait_ge(L0f_h, 2 * e + g + 1)
                    if e >= 2:
                        act.wait_ge(L0f_y, e - 1)
                    ACTE.activation(HT0[:, e % 2, 4 * g:4 * g + 4, :], bank(4 + g, 4, 128),
                                    ACT.Gelu_apprx_tanh).then_inc(L0f_hs, 1)
            layernorm(3)
            wide(0)
            layernorm(4)
            self16(1)
            layernorm(5)
            act.wait_ge(router_d, 2)
            ACTE.activation(TP, TP, ACT.Exp).then_inc(router_exp, 1)
            for i in range(0, NT, 2):
                act.wait_ge(gathered, i + 5)
                ACTE.copy(TXIN[:, :, :, i, :], bank(i, 2, 16, 16)).then_inc(xin_copied, 1)
            act.wait_ge(comb_T, 2)
            ACTE.copy(TCT, bank(4, NT, 2, 128)).then_inc(comb_Ts, 1)
            for g in range(2):
                act.wait_ge(L1f_gate, g + 1)
                ACTE.activation(TSG[:, g, :], ps[:, 2 * g, :], ACT.Silu).then_inc(L1f_silu, 1)
            act.wait_ge(L1f_o, 1)
            for c in range(2):
                for g in range(2):
                    if g == 0:
                        ACTE.copy(TOT[:, c, :, 8 * g:8 * g + 8, :].rearrange("p i e s -> p e i s"),
                                  bank(4 + 2 * c + g, 8, NT, 16)).then_inc(L1f_os, 1)
            for i in range(0, NT, 2):
                act.wait_ge(L1f_oT, i + 1)
                ACTE.copy(TON[:, i, :, :], bank(i, 2, D)).then_inc(L1f_ons, 1)
            layernorm(6)
            wide(1)
            layernorm(7)
            self1(0)
            layernorm(8)
            act.wait_ge(router_d, 3)
            ACTE.activation(RL, RL, ACT.Exp).then_inc(router_exp, 1)
            act.wait_ge(L2f_mean, 1)
            ACTE.activation(RC_[:, 1:2], RC_[:, 0:1], ACT.Exp, scale=-1.0).then_inc(L2f_sig, 1)

            def copy_inputs(e):
                act.wait_ge(L2f_xi, e + 1)
                if e >= 2:
                    act.wait_ge(L2f_h, 8 * (e - 1))
                ACTE.copy(EXI[:, e % 2, 0, :], ps[:, 6, :]).then_inc(L2f_xis_act, 1)

            copy_inputs(0)
            for e in range(8):
                for f in range(8):
                    n = 8 * e + f
                    if f == 0 and e > 0:
                        spread_high(1, 2 * e - 1)
                    if f == 2:
                        split_high(1, 2 * e)
                    if f == 4:
                        split_high(1, 2 * e + 1)
                    if f == 6:
                        if e < 7:
                            copy_inputs(e + 1)
                        spread_high(1, 2 * e)
                    act.wait_ge(L2f_h, n + 1)
                    if n >= 4:
                        act.wait_ge(L2f_y, n - 3)
                    ACTE.activation(EH[:, n % 4, :], ps[:, 4 + n % 2, :], ACT.Gelu,
                                    bias=C("L2f_b1")[:, n:n + 1]).then_inc(L2f_hs, 1)
            spread_high(1, NGROUP - 1)
            layernorm("9b", affine=("L3x_g1", "L3x_b1"))
            narrow(1)
            act.wait_ge(na_v, 1)
            ACTE.copy(NV[:, 0, :], ps[:, 0, :]).then_inc(na_vs, 1)
            layernorm(10)
            self1(1)
            layernorm(11)
            act.wait_ge(L3f_ss, 1)
            for h in range(16):
                if h >= 4:
                    act.wait_ge(L3f_acc, h - 3)
                ACTE.activation(FT[:, h % 4, :], FS, ACT.Relu, scale=C("L3f_W1")[:, h:h + 1],
                                bias=C("L3f_b1")[:, h:h + 1]).then_inc(L3f_relu, 1)

        @block.vector
        def _(dve):
            chain = [0]

            def link(ins):
                chain[0] += 1
                ins.then_inc(dve_step, 1)
                dve.wait_ge(dve_step, chain[0])

            dve.wait_ge(consts_loaded, 16)
            link(DVE.tensor_copy(ident16[:, :], ident))
            dve.wait_ge(x_loaded, 16)

            def layernorm(key, affine=None):
                n = LN[key]
                src = xn if key == "9b" else x
                for i in range(NT):
                    ins = DVE.bn_stats(st6[:, i, :], src[:, i, :])
                link(ins)
                for i in range(NT):
                    ins = DVE.bn_aggr(mv[:, i, :], st6[:, i, :])
                ins.then_inc(ln_stats, 1)
                dve.wait_ge(ln_rstd, n + 1)
                for i in range(NT):
                    DVE.tensor_scalar(xn[:, i, :], src[:, i, :], mv[:, i, 0:1], rstd[:, i:i + 1], ALU.subtract,
                                      ALU.mult).then_inc(ln_xn, 1)
                if key == 9:
                    dve.wait_ge(ln_xn, 4 * (LN[9] + 1))
                    return
                dve.wait_ge(ln_T, LNT[key] + 1)
                if affine is None:
                    DVE.tensor_copy(xnT[:, 1, :], ps[:, 1, :]).then_inc(ln_xnT_dve, 1)
                else:
                    g, b = affine
                    DVE.tensor_scalar(xnT[:, 1, :], ps[:, 1, :], C(g)[:, 1:2], C(b)[:, 1:2], ALU.mult,
                                      ALU.add).then_inc(ln_xnT_dve, 1)

            def add_x(l, banks):
                for i in range(NT):
                    dve.wait_ge(layer_out, 4 * l + i + 1)
                    ins = DVE.tensor_tensor(x[:, i, :], x[:, i, :], ps[:, banks[i], 0:D], ALU.add)
                    if l == LAYERS - 1:
                        ins.then_inc(x_final, 1)
                    elif i == NT - 1:
                        link(ins)

            def wide(k):
                for r in range(1, NPAIR, 2):
                    dve.wait_ge(xa_q, 8 * k + r + 1)
                    DVE.tensor_scalar(XQ[:, r, :], ps[:, r, :], DHB ** -0.5, None, ALU.mult).then_inc(xa_qs, 1)

                def rowmax(t, r):
                    dve.wait_ge(xa_S, t + 1)
                    DVE.tensor_reduce(XNM[:, r % 4:r % 4 + 1], bank(2 * (r % 2), 1024), X, ALU.max,
                                      negate=True).then_inc(xa_max, 1)

                def queries(t, r):
                    dve.wait_ge(xa_AH, t + 1)
                    DVE.tensor_tensor(XAL[:, r % 2, :], bank(7, 256), XAH[:, r % 2, :], ALU.subtract).then_inc(xa_AL, 1)

                def spread(t, r):
                    for g in range(2):
                        dve.wait_ge(xa_PTH, 2 * t + g + 1)
                        c = slice(4 * g, 4 * g + 4)
                        DVE.tensor_tensor(PTL[:, r % 2, c, :], bank(4 + g, 4, 128), PTH[:, r % 2, c, :],
                                          ALU.subtract).then_inc(xa_PTL, 1)

                def normalise(t, r):
                    dve.wait_ge(xa_P, t + 1)
                    DVE.reciprocal(XRI[:, r % 4:r % 4 + 1], XRS[:, r % 4:r % 4 + 1]).then_inc(xa_recip, 1)
                    dve.wait_ge(xa_recip, t + 1)
                    dve.wait_ge(xa_Z, t + 1)
                    DVE.tensor_scalar(XZ[:, r % 2, :], bank(6, DC), XRI[:, r % 4:r % 4 + 1], None,
                                      ALU.mult).then_inc(xa_Zs, 1)

                def ztrans(t, r):
                    dve.wait_ge(xa_ZT, t + 1)
                    DVE.tensor_copy(XZT[:, r % 2, 0:128], bank(6, 128, at=DC)).then_inc(xa_ZTs, 1)
                    DVE.tensor_copy(XZT[0:D2, r % 2, 128:256], bank(6, 128, rows=slice(0, D2), at=DC + 128)) \
                        .then_inc(xa_ZTs, 1)

                def batch(b, first, last):
                    t0 = 64 * k + 8 * b if isinstance(b, int) else b * 8 + 64 * k
                    for r in range(NPAIR):
                        t = t0 + r
                        if not (first and r < 3):
                            ztrans(t - 3, (r - 3) % NPAIR)
                        if not (last and r == NPAIR - 1):
                            queries(t + 1, r + 1)
                        rowmax(t, r)
                        if not (first and r < 1):
                            spread(t - 1, (r - 1) % NPAIR)
                        if not (first and r < 2):
                            normalise(t - 2, (r - 2) % NPAIR)

                queries(64 * k, 0)
                batch(0, True, False)
                with dve.Fori(1, B - 1) as b:
                    batch(b, False, False)
                batch(B - 1, False, True)
                t1 = 64 * (k + 1)
                ztrans(t1 - 3, 5)
                spread(t1 - 1, 7)
                normalise(t1 - 2, 6)
                ztrans(t1 - 2, 6)
                normalise(t1 - 1, 7)
                ztrans(t1 - 1, 7)

            def context_stats(g):
                dve.wait_ge(stage_loaded[g % 2], stage_value(1, g))
                for m in range(GROUP):
                    ins = DVE.bn_stats(PST6[:, g % 2, m, :], stage(1, g)[:, m, :])
                link(ins)
                for m in range(GROUP):
                    ins = DVE.bn_aggr(PMV[:, g % 2, m, :], PST6[:, g % 2, m, :])
                ins.then_inc(cx_stats, 1)

            def context_norm(g):
                dve.wait_ge(cx_rstd, g + 1)
                for m in range(GROUP):
                    c = stage(1, g)[:, m, :]
                    ins = DVE.tensor_scalar(c, c, PMV[:, g % 2, m, 0:1], PRS[:, g % 2, m:m + 1], ALU.subtract, ALU.mult)
                ins.then_inc(cx_n, 1)

            def split_low(p, g):
                dve.wait_ge(cx_hi, NGROUP * p + g + 1)
                c = slice(GROUP * g, GROUP * g + GROUP)
                src = stage(p, g)
                DVE.tensor_tensor(CN[:, c, DC:DC + D2], src[:, :, 128:DC], CN[:, c, 128:DC], ALU.subtract)
                DVE.tensor_tensor(CN[:, c, DC + D2:], src[:, :, 0:128], CN[:, c, 0:128], ALU.subtract) \
                    .then_inc(cx_lo, 1)

            def spread_low(p, g):
                dve.wait_ge(cx_T, NGROUP * p + g + 1)
                DVE.tensor_copy(CT[:, 2, 512 * g:512 * g + 512], bank(ctx_banks(p, g) + 1, 256).bitcast(F16)) \
                    .then_inc(cx_Ts_dve, 1)

            def narrow(k):
                DVE.memset(ONES16, 1.0)
                for c in range(2):
                    dve.wait_ge(na_q, 2 * k + c + 1)
                    DVE.tensor_scalar(NQ[:, c, :], ps[:, 2 + c, :], C("L0x_bq" if k == 0 else "L3x_bq")[:, c:c + 1],
                                      D ** -0.5, ALU.add, ALU.mult).then_inc(na_qs, 1)
                for c in range(3):
                    dve.wait_ge(na_AH, 3 * k + c + 1)
                    if c == 2:
                        R = slice(32, 33)
                        DVE.tensor_tensor(NCR[R], bank(6, TOK, rows=R), NCR[R], ALU.subtract).then_inc(na_AL, 1)
                    elif k == 0:
                        DVE.tensor_tensor(NAL[:, c, :], ps[:, 4 + c, :], NAH[:, c, :], ALU.subtract).then_inc(na_AL, 1)
                    else:
                        DVE.scalar_tensor_tensor(NAL[:, c, :], ps[:, 4 + c, :], C("L3x_g2")[:, c:c + 1], NAH[:, c, :],
                                                 ALU.mult, ALU.subtract).then_inc(na_AL, 1)
                DVE.memset(NZT2[D2:D2 + 1], 1.0).then_inc(na_ones, 1)

                def norm(i):
                    t = 4 * k + i
                    dve.wait_ge(na_P, t + 1)
                    link(DVE.reciprocal(XRI[:, i:i + 1], XRS[:, i:i + 1]))
                    dve.wait_ge(na_Z, t + 1)
                    DVE.tensor_scalar(XZ[:, i % 2, :], bank(6, DC), XRI[:, i:i + 1], None, ALU.mult).then_inc(na_Zs, 1)
                    dve.wait_ge(na_ZT, t + 1)
                    c = slice(128 * i, 128 * i + 128)
                    if k == 0:
                        DVE.tensor_copy(NZT1[:, c], bank(6, 128, at=DC)).then_inc(na_ZTs, 1)
                        DVE.tensor_copy(NZT2[0:D2, c], bank(6, 128, rows=slice(0, D2), at=DC + 128)).then_inc(na_ZTs, 1)
                    else:
                        DVE.tensor_scalar(NZT1[:, c], bank(6, 128, at=DC), C("L3x_g2")[:, 0:1], C("L3x_b2")[:, 0:1],
                                          ALU.mult, ALU.add).then_inc(na_ZTs, 1)
                        DVE.tensor_scalar(NZT2[0:D2, c], bank(6, 128, rows=slice(0, D2), at=DC + 128),
                                          C("L3x_g2")[0:D2, 1:2], C("L3x_b2")[0:D2, 1:2],
                                          ALU.mult, ALU.add).then_inc(na_ZTs, 1)

                def spread(i):
                    for g in range(2):
                        dve.wait_ge(na_PTH, 2 * (4 * k + i) + g + 1)
                        c = slice(4 * g, 4 * g + 4)
                        DVE.tensor_tensor(PTL[:, i % 2, c, :], bank(4 + g, 4, 128), PTH[:, i % 2, c, :],
                                          ALU.subtract).then_inc(na_PTL, 1)

                for i in range(NT):
                    dve.wait_ge(na_S, 4 * k + i + 1)
                    DVE.tensor_reduce(XNM[:, i:i + 1], bank(2 * (i % 2), 1024), X, ALU.max, negate=True) \
                        .then_inc(na_max, 1)
                    if i >= 1:
                        spread(i - 1)
                        norm(i - 1)
                spread(NT - 1)
                norm(NT - 1)

            def self16(k):
                for h in range(2):
                    for r in (2, 3, 6, 7):
                        dve.wait_ge(sa_q, 8 * k + 4 * h + r // 2 + 1)
                        src = bank(r // 2, 256, at=256 * (r % 2))
                        if k == 0:
                            DVE.tensor_copy(QC[:, r, :], src).then_inc(sa_qs_dve, 1)
                        else:
                            DVE.tensor_scalar(QC[:, r, :], src, C("L1a_bq")[:, r:r + 1], None,
                                              ALU.add).then_inc(sa_qs_dve, 1)
                    if k == 0:
                        dve.wait_ge(sa_k0, h + 1)
                        DVE.tensor_copy(KC[:, 0, :], bank(4, 256)).then_inc(sa_ks0, 1)
                    else:
                        for r in (2, 3, 6, 7):
                            dve.wait_ge(sa_k, 4 * h + r // 2 + 1)
                            DVE.tensor_scalar(KC[:, r, :], bank(4 + r // 2, 256, at=256 * (r % 2)),
                                              C("L1a_bk")[:, r:r + 1], None, ALU.add).then_inc(sa_ks_dve, 1)
                    if h == 0:
                        link(DVE.memset(VB, 0.0))
                    dve.wait_ge(sa_v, 2 * k + h + 1)
                    for b in range(4):
                        for e in range(2):
                            R = half(e)
                            if k == 0:
                                src = bank(6, 4, 16, rows=R)[:, b:b + 1, :].to_broadcast([64, 8, 16])
                            else:
                                src = bank(6 + b // 2, 2, 8, 32, rows=R)[:, b % 2, :, 16 * e:16 * e + 16]
                            ins = DVE.tensor_copy(VB[R, b, :, 16 * e:16 * e + 16], src)
                    ins.then_inc(sa_vs, 1)

                    def soft(u):
                        t = 8 * k + 4 * h + u
                        p = u % 2
                        sc = SC[:, p, :].rearrange("p (a b) -> p a b", b=64)
                        raw = ps[:, p, :].rearrange("p (a b) -> p a b", b=64)
                        mx = AMX[:, p, :]
                        dve.wait_ge(sa_S, t + 1)
                        if u >= 2:
                            dve.wait_ge(sa_T, t - 1)
                        if k == 0:
                            link(DVE.tensor_tensor(sc, raw, C("causal").unsqueeze(1).to_broadcast([128, 8, 64]), ALU.add))
                            raw = sc
                        link(DVE.tensor_reduce(mx, raw, X, ALU.max))
                        DVE.tensor_tensor(sc, raw, mx.unsqueeze(2).to_broadcast([128, 8, 64]), ALU.subtract) \
                            .then_inc(sa_d, 1)

                    def norm(u):
                        t = 8 * k + 4 * h + u
                        p = u % 2
                        sc = SC[:, p, :].rearrange("p (a b) -> p a b", b=64)
                        dve.wait_ge(sa_exp, t + 1)
                        link(DVE.tensor_reduce(ASM[:, p, :], sc, X, ALU.add))
                        link(DVE.reciprocal(ARC[:, p, :], ASM[:, p, :]))
                        DVE.tensor_tensor(sc, sc, ARC[:, p, :].unsqueeze(2).to_broadcast([128, 8, 64]), ALU.mult) \
                            .then_inc(sa_P, 1)

                    soft(0)
                    for u in range(1, 4):
                        soft(u)
                        norm(u - 1)
                    norm(3)
                    dve.wait_ge(sa_y, 2 * k + h + 1)
                    DVE.tensor_copy(YT[:, 1, 256 * h:256 * h + 256], ps[:, 5, 256 * h:256 * h + 256]) \
                        .then_inc(sa_ys, 1)

            def self1(k):
                dve.wait_ge(s1_k, 1 + k)
                DVE.tensor_copy(SK, bank(4, 2, TOK)).then_inc(s1_ks, 1)
                dve.wait_ge(s1_v, 1 + k)
                DVE.tensor_copy(SV[:, 2:4, :], bank(7, 2, D)).then_inc(s1_vs, 1)
                dve.wait_ge(s1_S, 1 + k)
                mask = C("bcausal" if k == 0 else "bfull").unsqueeze(1).to_broadcast([128, NT, 128])
                link(DVE.tensor_tensor(SS, bank(0, NT, 128), mask, ALU.add))
                link(DVE.tensor_reduce(SMX, SS, X, ALU.max))
                DVE.tensor_tensor(SS, SS, SMX.unsqueeze(2).to_broadcast([128, NT, 128]), ALU.subtract) \
                    .then_inc(s1_d, 1)
                dve.wait_ge(s1_exp, 1 + k)
                link(DVE.tensor_reduce(SSM, SS, X, ALU.add))
                link(DVE.reciprocal(SRC, SSM))
                DVE.tensor_tensor(SS, SS, SRC.unsqueeze(2).to_broadcast([128, NT, 128]), ALU.mult) \
                    .then_inc(s1_P, 1)
                dve.wait_ge(s1_o, 1 + k)
                DVE.tensor_copy(SO[:, 1, :], ps[:, 3, :]).then_inc(s1_os, 1)

            def ranks(k):
                for i in range(NT):
                    if i >= 1:
                        dve.wait_ge(rk_spread, 4 * k + i)
                    DVE.tensor_tensor(RDL, RP[:, i, :].unsqueeze(2).to_broadcast([128, 8, 64]),
                                      C("delta").unsqueeze(1).to_broadcast([128, 8, 64]), ALU.mult) \
                        .then_inc(rk_diag, 1)
                for i in range(NT):
                    dve.wait_ge(rk_spread, 4 * k + i + 1)
                    other = bank(2 + i, 8, 64)
                    mine = RP[:, i, :].unsqueeze(2).to_broadcast([128, 8, 64])
                    DVE.tensor_tensor(RG, other, mine, ALU.is_gt)
                    link(DVE.tensor_tensor(RE, other, mine, ALU.is_equal))
                    link(DVE.tensor_tensor(RE, RE, C("before").unsqueeze(1).to_broadcast([128, 8, 64]), ALU.mult))
                    link(DVE.tensor_tensor(RG, RG, RE, ALU.add))
                    link(DVE.tensor_reduce(RK[:, i, :], RG, X, ALU.add))

            def first_hot(out, p, mx, tmp, vmx, rev, n):
                bc = lambda a: a.unsqueeze(2).to_broadcast([128, NT, n])
                link(DVE.tensor_reduce(mx, p, X, ALU.max))
                link(DVE.tensor_tensor(tmp, p, bc(mx), ALU.is_equal))
                link(DVE.tensor_tensor(tmp, tmp, C(rev).unsqueeze(1).to_broadcast([128, NT, n]), ALU.mult))
                link(DVE.tensor_reduce(vmx, tmp, X, ALU.max))
                link(DVE.tensor_tensor(out, tmp, bc(vmx), ALU.is_equal))

            layernorm(0)
            for g in range(NGROUP):
                split_low(0, g)
                if g >= 2:
                    spread_low(0, g - 2)
            spread_low(0, NGROUP - 2)
            spread_low(0, NGROUP - 1)
            narrow(0)
            add_x(0, (0, 1, 2, 3))
            layernorm(1)
            self16(0)
            add_x(1, (0, 1, 2, 3))
            layernorm(2)
            bc8 = lambda a: a.unsqueeze(2).to_broadcast([128, NT, 8])
            dve.wait_ge(router_logits, 1)
            link(DVE.tensor_reduce(RA, bank(2, NT, 8), X, ALU.max))
            DVE.tensor_tensor(RP, bank(2, NT, 8), bc8(RA), ALU.subtract).then_inc(router_d, 1)
            dve.wait_ge(router_exp, 1)
            link(DVE.tensor_reduce(RA, RP, X, ALU.add))
            link(DVE.reciprocal(RB_, RA))
            link(DVE.tensor_tensor(RP, RP, bc8(RB_), ALU.mult))
            ranks(0)
            for i in range(NT):
                ins = DVE.tensor_tensor(SEL[:, i], RK[:, i, :].unsqueeze(2).to_broadcast([128, 8, 32]),
                                        C("slot32").unsqueeze(1).to_broadcast([128, 8, 32]), ALU.is_equal)
            chain[0] += 1
            ins.then_inc(dve_step, 1)
            dve.wait_ge(dve_step, chain[0])
            for i in range(NT):
                ins = DVE.tensor_tensor(SELG[:, :, i], SEL[:, i], RP[:, i, :].unsqueeze(2).to_broadcast([128, 8, 32]),
                                        ALU.mult)
            ins.then_inc(L0f_sel, 1)
            for i in range(1, NT, 2):
                dve.wait_ge(gathered, i + 1)
                DVE.tensor_copy(XIN[:, :, :, i, :], bank(i, 2, 8, 32)).then_inc(xin_copied, 1)
            for e in range(8):
                dve.wait_ge(L0f_y, e + 1)
                DVE.tensor_copy(YS[:, e, :], bank(6 + e % 2, D)).then_inc(L0f_ys, 1)
            rb = wv(5184, D).bitcast(BF16)
            for i in range(NT):
                dve.wait_ge(layer_out, 4 * 2 + i + 1)
                o = rb[:, 256 * (i % 2):256 * (i % 2) + 256]
                link(DVE.tensor_copy(o, ps[:, i, 0:D]))
                ins = DVE.tensor_tensor(x[:, i, :], x[:, i, :], o, ALU.add)
                link(ins)
            layernorm(3)
            wide(0)
            add_x(3, (0, 1, 2, 3))
            layernorm(4)
            self16(1)
            add_x(4, (0, 1, 2, 3))
            layernorm(5)
            bc16 = lambda a: a.unsqueeze(2).to_broadcast([128, NT, 16])
            dve.wait_ge(router_logits, 2)
            link(DVE.tensor_reduce(TM1, bank(2, NT, 16), X, ALU.max))
            DVE.tensor_tensor(TP, bank(2, NT, 16), bc16(TM1), ALU.subtract).then_inc(router_d, 1)
            dve.wait_ge(router_exp, 2)
            link(DVE.tensor_reduce(TM1, TP, X, ALU.add))
            link(DVE.reciprocal(TM2, TM1))
            link(DVE.tensor_tensor(TP, TP, bc16(TM2), ALU.mult))
            first_hot(TOH1, TP, TM1, TT, TV, "rev16", 16)
            link(DVE.scalar_tensor_tensor(TP, TOH1, -2.0, TP, ALU.mult, ALU.add))
            first_hot(TOH2, TP, TM2, TT, TV, "rev16", 16)
            DVE.tensor_copy(TU, TOH1).then_inc(L1f_hot, 1)
            dve.wait_ge(L1f_cum, 1)
            DVE.tensor_tensor(TQ1, bank(3, NT, 16), TOH1, ALU.mult)
            link(DVE.tensor_tensor(TQ2, bank(3, NT, 16, at=64), TOH2, ALU.mult))
            bs = lambda a, i: a[:, i, :].unsqueeze(2).to_broadcast([128, 16, 16])
            slots = C("slot16").unsqueeze(1).to_broadcast([128, 16, 16])
            for i in range(NT):
                DVE.tensor_tensor(TD[:, i], bs(TQ1, i), slots, ALU.is_equal)
                ins = DVE.tensor_tensor(TX_[:, i], bs(TQ2, i), slots, ALU.is_equal)
            link(ins)
            for i in range(NT):
                ins = DVE.tensor_tensor(TD[:, i], TD[:, i], TX_[:, i], ALU.add)
            ins.then_inc(L1f_disp, 1)
            DVE.tensor_scalar(TQ1, TQ1, 8.0, None, ALU.min)
            link(DVE.tensor_scalar(TQ2, TQ2, 8.0, None, ALU.min))
            dve.wait_ge(L1f_disp, 1)
            for i in range(NT):
                DVE.tensor_tensor(TC[:, i], bs(TQ1, i), slots, ALU.is_equal)
                ins = DVE.tensor_tensor(TX_[:, i], bs(TQ2, i), slots, ALU.is_equal)
            link(ins)
            for i in range(NT):
                ins = DVE.tensor_scalar(TC[:, i], TC[:, i], TM1[:, i:i + 1], None, ALU.mult)
            link(ins)
            for i in range(NT):
                ins = DVE.scalar_tensor_tensor(TC[:, i], TX_[:, i], TM2[:, i:i + 1], TC[:, i], ALU.mult, ALU.add)
            ins.then_inc(L1f_comb, 1)
            for i in range(1, NT, 2):
                dve.wait_ge(gathered, i + 5)
                DVE.tensor_copy(TXIN[:, :, :, i, :], bank(i, 2, 16, 16)).then_inc(xin_copied, 1)
            for g in range(2):
                dve.wait_ge(L1f_silu, g + 1)
                dve.wait_ge(L1f_up, g + 1)
                DVE.tensor_tensor(THT[:, 8 * g:8 * g + 8, :], TSG[:, g, :].rearrange("p (a b) -> p a b", b=64),
                                  bank(2 * g + 1, 8, 64), ALU.mult).then_inc(L1f_hs, 1)
            dve.wait_ge(L1f_o, 1)
            for c in range(2):
                DVE.tensor_copy(TOT[:, c, :, 8:16, :].rearrange("p i e s -> p e i s"),
                                bank(4 + 2 * c + 1, 8, NT, 16)).then_inc(L1f_os, 1)
            for i in range(1, NT, 2):
                dve.wait_ge(L1f_oT, i + 1)
                DVE.tensor_copy(TON[:, i, :, :], bank(i, 2, D)).then_inc(L1f_ons, 1)
            add_x(5, (4, 5, 6, 7))
            layernorm(6)
            wide(1)
            add_x(6, (0, 1, 2, 3))
            layernorm(7)
            self1(0)
            add_x(7, (4, 5, 6, 7))
            layernorm(8)
            bc8 = lambda a: a.unsqueeze(2).to_broadcast([128, NT, 8])
            sq = wv(5184, D)
            for i in range(NT):
                link(DVE.tensor_tensor(sq, xn[:, i, :], xn[:, i, :], ALU.mult))
                link(DVE.tensor_reduce(RA[:, i:i + 1], sq, X, ALU.add))
            wf2 = wv(5696, 16)
            DVE.tensor_tensor(wf2, C("L2f_waff"), C("L2f_waff"), ALU.mult).then_inc(L2f_w2, 1)
            dve.wait_ge(L2f_wn, 1)
            DVE.tensor_copy(RS1, bank(3, 8)).then_inc(L2f_norms2, 2)
            dve.wait_ge(L2f_norms, 2)
            for i in range(NT):
                ins = DVE.tensor_scalar(RT[:, i, :], RS1, RA[:, i:i + 1], 1e-9, ALU.mult, ALU.add)
            link(ins)
            link(DVE.reciprocal(RL, RT))
            dve.wait_ge(router_logits, 3)
            link(DVE.tensor_tensor(RP, bank(2, NT, 8), RL, ALU.mult))
            link(DVE.tensor_reduce(RB_[:, 0:1], RP, mybir.AxisListType.XY, ALU.add))
            link(DVE.tensor_copy(RB_[:, 1:2], RB_[:, 0:1]))
            DVE.tensor_copy(RB_[:, 2:3], RB_[:, 0:1]).then_inc(L2f_rowsum, 1)
            link(DVE.tensor_reduce(RA, RP, X, ALU.max))
            DVE.tensor_tensor(RL, RP, bc8(RA), ALU.subtract).then_inc(router_d, 1)
            dve.wait_ge(L2f_total, 1)
            DVE.tensor_scalar(RC_[:, 0:1], bank(3, 1, at=8), 1.0 / (TOK * 8), C("L2f_thr"), ALU.mult,
                              ALU.subtract).then_inc(L2f_mean, 1)
            dve.wait_ge(router_exp, 3)
            link(DVE.tensor_reduce(RA, RL, X, ALU.add))
            link(DVE.reciprocal(RB_, RA))
            link(DVE.tensor_tensor(RL, RL, bc8(RB_), ALU.mult))
            first_hot(ROH, RL, RA, RT, RB_, "rev8", 8)
            dve.wait_ge(L2f_sig, 1)
            link(DVE.tensor_scalar(RC_[:, 2:3], RC_[:, 1:2], 1.0, None, ALU.add))
            link(DVE.reciprocal(RC_[:, 3:4], RC_[:, 2:3]))
            link(DVE.tensor_scalar(RC_[:, 2:3], RC_[:, 3:4], float(CAP), 4.0, ALU.mult, ALU.max))
            ranks(1)
            link(DVE.tensor_scalar(RK, RK, 1.0, RC_[:, 2:3], ALU.add, ALU.is_le))
            link(DVE.tensor_tensor(ROH, ROH, RK, ALU.mult))

            def pick(e):
                if e >= 2:
                    dve.wait_ge(L2f_xi, e - 1)
                DVE.tensor_tensor(EDG[:, e % 2], ident.unsqueeze(1).to_broadcast([128, NT, 128]),
                                  ROH[:, :, e:e + 1].to_broadcast([128, NT, 128]), ALU.mult) \
                    .then_inc(L2f_diag, 1)

            def copy_inputs(e):
                dve.wait_ge(L2f_xi, e + 1)
                if e >= 2:
                    dve.wait_ge(L2f_h, 8 * (e - 1))
                DVE.tensor_copy(EXI[:, e % 2, 1, :], ps[:, 7, :]).then_inc(L2f_xis_dve, 1)

            pick(0)
            copy_inputs(0)
            for e in range(8):
                if e < 7:
                    pick(e + 1)
                for g in (2 * e, 2 * e + 1):
                    context_stats(g)
                for g in (2 * e, 2 * e + 1):
                    context_norm(g)
                for g in (2 * e, 2 * e + 1):
                    split_low(1, g)
                if e < 7:
                    copy_inputs(e + 1)
                for g in (2 * e, 2 * e + 1):
                    spread_low(1, g)
            dve.wait_ge(layer_out, 4 * 8 + 4)
            for i in range(NT):
                ins = DVE.tensor_tensor(x[:, i, :], x[:, i, :], bank(i // 2, D, at=D * (i % 2)), ALU.add)
            link(ins)
            layernorm(9)
            layernorm("9b", affine=("L3x_g1", "L3x_b1"))
            link(DVE.memset(NKB, 0.0))
            dve.wait_ge(na_kb, 1)
            for c in range(2):
                DVE.tensor_scalar(NKB[:, c, 0:1], ps[:, 0, c:c + 1], C("L3x_bk")[:, c:c + 1], None, ALU.add)
                DVE.tensor_scalar(NKB[:, c, 32:33], ps[:, 0, c:c + 1], C("L3x_bk")[:, c:c + 1], None,
                                  ALU.add).then_inc(na_kbs, 1)
            narrow(1)
            dve.wait_ge(na_v, 2)
            DVE.tensor_copy(NV[:, 1, :], ps[:, 1, :]).then_inc(na_vs, 1)
            add_x(9, (2, 3, 4, 5))
            layernorm(10)
            self1(1)
            add_x(10, (4, 5, 6, 7))
            layernorm(11)
            dve.wait_ge(L3f_s, 1)
            DVE.tensor_scalar(FS, ps[:, 2, 0:256], C("L3f_bin"), None, ALU.add).then_inc(L3f_ss, 1)
            for h in range(16):
                dve.wait_ge(L3f_relu, h + 1)
                if h == 0:
                    ins = DVE.tensor_scalar(FG_, FT[:, 0, :], C("L3f_W2")[:, 0:1], C("L3f_b2"), ALU.mult, ALU.add)
                else:
                    ins = DVE.scalar_tensor_tensor(FG_, FT[:, h % 4, :], C("L3f_W2")[:, h:h + 1], FG_,
                                                   ALU.mult, ALU.add)
                ins.then_inc(L3f_acc, 1)
                dve.wait_ge(L3f_acc, h + 1)
            add_x(11, (3, 4, 5, 6))

        @block.tensor
        def _(pe):

            def loaded(name):
                n = UIDX[name]
                pe.wait_ge(slot_loaded[n % NSLOT], 16 * (n // NSLOT + 1))

            pe.wait_ge(consts_loaded, 16)

            def layernorm(key):
                for i in range(NT):
                    pe.wait_ge(ln_xn, 4 * LN[key] + i + 1)
                    for c in range(2):
                        ins = PE.transpose(ps[:, c, 128 * i:128 * i + 128], xn[:, i, 128 * c:128 * c + 128], ident)
                ins.then_inc(ln_T, 1)
                pe.wait_ge(ln_xnT_act, LNT[key] + 1)
                pe.wait_ge(ln_xnT_dve, LNT[key] + 1)

            tile = lambda i: slice(128 * i, 128 * i + 128)

            def project_out(l, banks, lhs, rhs, n, bias=None, ones=slice(0, 1), used=1):
                for i in range(NT):
                    o = ps[:, banks[i], 0:D]
                    if bias is not None:
                        mm(o, C("ones", ones), bias, True, False)
                    for c in range(n):
                        ins = mm(o, lhs(c, i), rhs(c), start=(c == 0 and bias is None), stop=(c == n - 1))
                    ins.then_inc(layer_out, 1)
                    if i == NT - 1 and used:
                        pe.wait_ge(layer_out, 4 * l + 4)
                        pe.sem_inc(units_used, used)

            def release(n):
                pe.sem_inc(units_used, n)

            def transpose_context(p, g):
                pe.wait_ge(cx_lo, NGROUP * p + g + 1)
                b0 = ctx_banks(p, g)
                before = 3 if p == 0 else 1
                if p == 1 or g >= before:
                    pe.wait_ge(cx_Ts_act, NGROUP * p + g + 1 - before)
                    pe.wait_ge(cx_Ts_dve, NGROUP * p + g + 1 - before)
                for m in range(GROUP):
                    for c, at in ((0, 0), (1, 128), (2, 256)):
                        o = bank(b0 + c // 2, 512).bitcast(F16)[:, 512 * (c % 2) + 128 * m:512 * (c % 2) + 128 * m + 128]
                        ins = PE.transpose(o, CN[:, GROUP * g + m, at:at + 128], ident16[:, :])
                ins.then_inc(cx_T, 1)

            def wide(k):
                L = "L1x" if k == 0 else "L2x"
                l = 3 if k == 0 else 6
                loaded(f"{L}_q")
                wq = unit(f"{L}_q", 0, 2, 1024)
                for r in range(NPAIR):
                    for c in range(2):
                        ins = mm(ps[:, r, :], wq[:, c, 128 * r:128 * r + 128], xnT[:, c, :], c == 0, c == 1)
                    ins.then_inc(xa_q, 1)
                pe.wait_ge(xa_q, 8 * k + 8)
                release(1)
                pe.wait_ge(xa_qs, 8 * k + 8)
                loaded(f"{L}_k0")
                loaded(f"{L}_k1")
                loaded(f"{L}_v")
                wkt = [unit(f"{L}_k{h}", 0, 4, 2, 256) for h in range(2)]
                wvv = unit(f"{L}_v", 0, 2, 1024)

                def queries(b, t, r, first):
                    if not first:
                        pe.wait_ge(xa_OT, t - 4)
                    for e in range(2):
                        wkr = wkt[r // 4][:, r % 4, e, :]
                        rhs = XQ[:, r, bass.ds(b * 64, 64)]
                        for c in range(2):
                            ins = mm(bank(7, 64, at=128 * c + 64 * e), wkr[:, 128 * c:128 * c + 128], rhs)
                    ins.then_inc(xa_A, 1)

                def scores(b, t, r, first):
                    pe.wait_ge(xa_AL, t + 1)
                    if not first:
                        pe.wait_ge(xa_P, t - 1)
                    ah, al = XAH[:, r % 2, :], XAL[:, r % 2, :]
                    for n in range(2):
                        o = ps[:, 2 * (r % 2) + n, :]
                        kk = bass.ds(b * LK + 512 * n, 512)
                        mm(o, ah[:, 0:128], CT[:, 0, kk], True, False)
                        mm(o, ah[:, 0:128], CT[:, 2, kk], False, False)
                        mm(o, al[:, 0:128], CT[:, 0, kk], False, False)
                        mm(o, ah[:, 128:256], CT[:, 1, kk], False, False)
                        ins = mm(o, al[:, 128:256], CT[:, 1, kk], False, True)
                    ins.then_inc(xa_S, 1)

                def transposes(t, r, first):
                    pe.wait_ge(xa_P, t + 1)
                    for g in range(2):
                        if not first:
                            pe.wait_ge(xa_PTL, 2 * t - 1 + g)
                        for m in range(4):
                            n = 4 * g + m
                            ins = PE.transpose(bank(4 + g, 128, at=128 * m), XP[:, r % 2, 128 * n:128 * n + 128], ident)
                        ins.then_inc(xa_T, 1)

                def attend(b, t, r, first):
                    pe.wait_ge(xa_PTL, 2 * t + 2)
                    if not first:
                        pe.wait_ge(xa_Zs, t)
                    for n in range(KT):
                        part = lambda a, z: CN[:, bass.ds(b * KT + n, 1), a:z].rearrange("p a d -> p (a d)")
                        ph, pl = PTH[:, r % 2, n, :], PTL[:, r % 2, n, :]
                        mm(bank(6, DC), ph, part(0, DC), n == 0, False)
                        mm(bank(6, D2, at=128), ph, part(DC, DC + D2), False, False)
                        mm(bank(6, 128), ph, part(DC + D2, 2 * DC), False, False)
                        ins = mm(bank(6, DC), pl, part(0, DC), False, n == KT - 1)
                    ins.then_inc(xa_Z, 1)

                def ztrans(t, r, first):
                    pe.wait_ge(xa_Zs, t + 1)
                    if not first:
                        pe.wait_ge(xa_ZTs, 2 * t)
                    PE.transpose(bank(6, 128, at=DC), XZ[:, r % 2, 0:128], ident)
                    PE.transpose(bank(6, 128, rows=slice(0, D2), at=DC + 128), XZ[:, r % 2, 128:DC], ident) \
                        .then_inc(xa_ZT, 1)

                def heads(t, r, before, first=False):
                    pe.wait_ge(xa_ZTs, 2 * t + 2)
                    if not first:
                        pe.wait_ge(xa_OT, t)
                    pe.wait_ge(xa_AL, before + 1)
                    for e in range(2):
                        o = bank(7, 64, rows=half(e), at=256)
                        h = 2 * r + e
                        c = slice(64 * e, 64 * e + 64)
                        mm(o, wvv[:, 0, 64 * h:64 * h + 64], XZT[:, r % 2, 64 * e:64 * e + 64], True, False)
                        ins = mm(o, wvv[0:D2, 1, 64 * h:64 * h + 64], XZT[0:D2, r % 2, 128 + 64 * e:192 + 64 * e],
                                 False, True)
                    ins.then_inc(xa_O, 1)

                def batch(b, first, last):
                    t0 = 64 * k + 8 * b if isinstance(b, int) else b * 8 + 64 * k
                    for r in range(NPAIR):
                        t = t0 + r
                        end = last and r == NPAIR - 1
                        scores(b, t, r, first and r < 2)
                        if not end:
                            queries(b if r < NPAIR - 1 else b + 1, t + 1, (r + 1) % NPAIR, first and r < 4)
                        if not (first and r < 3):
                            ztrans(t - 3, (r - 3) % NPAIR, first and r == 3)
                        if not (first and r < 1):
                            transposes(t - 1, (r - 1) % NPAIR, first and r == 1)
                        if not (first and r < 3):
                            heads(t - 3, (r - 3) % NPAIR, t if end else t + 1, first and r == 3)
                        if not (first and r < 2):
                            attend(b if r >= 2 else b - 1, t - 2, (r - 2) % NPAIR, first and r == 2)

                queries(0, 64 * k, 0, True)
                batch(0, True, False)
                with pe.Fori(1, B - 1) as b:
                    batch(b, False, False)
                batch(B - 1, False, True)
                t1 = 64 * (k + 1)
                ztrans(t1 - 3, 5, False)
                transposes(t1 - 1, 7, False)
                heads(t1 - 3, 5, t1 - 1)
                attend(B - 1, t1 - 2, 6, False)
                ztrans(t1 - 2, 6, False)
                heads(t1 - 2, 6, t1 - 1)
                attend(B - 1, t1 - 1, 7, False)
                ztrans(t1 - 1, 7, False)
                heads(t1 - 1, 7, t1 - 1)
                loaded(f"{L}_o")
                pe.wait_ge(xa_OT, t1)
                wo = unit(f"{L}_o", 0, 8, D)
                project_out(l, (0, 1, 2, 3), lambda c, i: XQ[:, c, tile(i)], lambda c: wo[:, c, :], 8,
                            bias=wvv[D2:D2 + 1, 1, 0:D],
                            ones=slice(D2, D2 + 1), used=4)

            def narrow(k):
                ua, ub = ("L0x_a", "L0x_b") if k == 0 else ("L3x_a", "L3x_b")
                wq, wkt = unit(ua, 0, 2, D), unit(ua, 512, 2, 256)
                kb = unit(ua, 1024, 2, 33) if k == 0 else NKB
                wvv = unit(ub, 0, 2, D)
                loaded(ua)
                for c in range(2):
                    for d in range(2):
                        ins = mm(ps[:, 2 + c, :], wq[:, d, 128 * c:128 * c + 128], xnT[:, d, :], d == 0, d == 1)
                    ins.then_inc(na_q, 1)
                pe.wait_ge(na_qs, 2 * k + 2)
                for a in range(3):
                    if a == 2 and k == 1:
                        pe.wait_ge(na_kbs, 2)
                    for c in range(2):
                        if a < 2:
                            ins = mm(ps[:, 4 + a, :], wkt[:, c, 128 * a:128 * a + 128], NQ[:, c, :], c == 0, c == 1)
                        else:
                            ins = mm(bank(6, TOK, rows=slice(0, 33)), kb[:, c, :], NQ[:, c, :], c == 0, c == 1)
                    ins.then_inc(na_A, 1)
                pe.wait_ge(na_AL, 3 * k + 3)
                R = slice(0, D2 + 1)

                def scores(i):
                    t = 4 * k + i
                    if i >= 2:
                        pe.wait_ge(na_P, t - 1)
                    for par in range(2):
                        b = 2 * i + par
                        q = slice(64 * b, 64 * b + 64)
                        for n in range(2):
                            o = ps[half(par), 2 * (i % 2) + n, :]
                            kk = slice(b * LK + 512 * n, b * LK + 512 * n + 512)
                            mm(o, NCR[:, q], ONES16, True, False)
                            mm(o, NAH[:, 0, q], CT[:, 0, kk], False, False)
                            mm(o, NAH[:, 0, q], CT[:, 2, kk], False, False)
                            mm(o, NAL[:, 0, q], CT[:, 0, kk], False, False)
                            mm(o, NAH[:, 1, q], CT[:, 1, kk], False, False)
                            ins = mm(o, NAL[:, 1, q], CT[:, 1, kk], False, True)
                    ins.then_inc(na_S, 1)

                def rest(i):
                    t = 4 * k + i
                    pe.wait_ge(na_P, t + 1)
                    for g in range(2):
                        if i >= 1:
                            pe.wait_ge(na_PTL, 2 * t - 1 + g)
                        for m in range(4):
                            n = 4 * g + m
                            ins = PE.transpose(bank(4 + g, 128, at=128 * m), XP[:, i % 2, 128 * n:128 * n + 128], ident)
                        ins.then_inc(na_T, 1)
                    pe.wait_ge(na_PTL, 2 * t + 2)
                    if i >= 1:
                        pe.wait_ge(na_Zs, t)
                    for par in range(2):
                        o = bank(6, DC, rows=half(par))
                        for n in range(KT):
                            kt = (2 * i + par) * KT + n
                            ph, pl = (a[:, i % 2, n, 64 * par:64 * par + 64] for a in (PTH, PTL))
                            mm(o, ph, CN[:, kt, 0:DC], n == 0, False)
                            mm(o[:, 128:DC], ph, CN[:, kt, DC:DC + D2], False, False)
                            mm(o[:, 0:128], ph, CN[:, kt, DC + D2:], False, False)
                            ins = mm(o, pl, CN[:, kt, 0:DC], False, n == KT - 1)
                    ins.then_inc(na_Z, 1)
                    pe.wait_ge(na_Zs, t + 1)
                    if i >= 1:
                        pe.wait_ge(na_ZTs, 2 * t)
                    PE.transpose(bank(6, 128, at=DC), XZ[:, i % 2, 0:128], ident)
                    PE.transpose(bank(6, 128, rows=slice(0, D2), at=DC + 128), XZ[:, i % 2, 128:DC], ident) \
                        .then_inc(na_ZT, 1)

                scores(0)
                for i in range(1, NT):
                    scores(i)
                    rest(i - 1)
                rest(NT - 1)
                pe.wait_ge(na_ZTs, 8 * k + 8)
                pe.wait_ge(na_ones, k + 1)
                loaded(ub)
                if k == 0:
                    project_out(0, (0, 1, 2, 3), lambda c, i: NZT1[:, tile(i)] if c == 0 else NZT2[R, tile(i)],
                                lambda c: wvv[:, 0, :] if c == 0 else wvv[R, 1, :], 2, used=2)
                else:
                    for c in range(2):
                        o = ps[:, c, :]
                        mm(o, wvv[:, 0, 128 * c:128 * c + 128], NZT1, True, False)
                        mm(o, wvv[R, 1, 128 * c:128 * c + 128], NZT2[R], False, True).then_inc(na_v, 1)
                    pe.wait_ge(na_vs, 2)
                    wo = unit(ub, 512, 2, D)
                    project_out(9, (2, 3, 4, 5), lambda c, i: NV[:, c, tile(i)], lambda c: wo[:, c, :], 2,
                                bias=unit(ub, 1024, D, rows=slice(0, 1)), used=2)

            def self16(k):
                l = 1 if k == 0 else 4
                for h in range(2):
                    tok = slice(256 * h, 256 * h + 256)
                    if h == 1:
                        pe.wait_ge(sa_d, 8 * k + 4)
                        pe.wait_ge(sa_PT, 8 * k + 4)
                        pe.wait_ge(sa_ys, 4 * k + 2)
                        pe.wait_ge(sa_vs, 2 * k + 1)
                    if k == 0:
                        wq = unit("L0a_a", 256, 1024)
                        wkk = unit("L0a_a", 1280, 128)
                        wvv = unit("L0a_a", 1408, 16)
                        for r in range(8):
                            ins = mm(bank(r // 2, 256, at=256 * (r % 2)), wq[:, 128 * r:128 * r + 128], LAT[:, tok])
                            if r % 2:
                                ins.then_inc(sa_q, 1)
                        mm(bank(4, 256), wkk, LAT[:, tok]).then_inc(sa_k0, 1)
                    else:
                        wq, wkk = unit("L1a_q", 0, 2, 1024), unit("L1a_k", 0, 2, 1024)
                        wvv = unit("L1a_v", 0, 2, D)
                        for done, ww, b0 in ((sa_q, wq, 0), (sa_k, wkk, 4)):
                            for r in range(8):
                                for c in range(2):
                                    ins = mm(bank(b0 + r // 2, 256, at=256 * (r % 2)), ww[:, c, 128 * r:128 * r + 128],
                                             xnT[:, c, tok], c == 0, c == 1)
                                if r % 2:
                                    ins.then_inc(done, 1)
                    pe.wait_ge(sa_qs_act, 8 * k + 4 * h + 4)
                    pe.wait_ge(sa_qs_dve, 8 * k + 4 * h + 4)
                    if k == 0:
                        pe.wait_ge(sa_ks0, h + 1)
                    else:
                        pe.wait_ge(sa_ks_act, 4 * h + 4)
                        pe.wait_ge(sa_ks_dve, 4 * h + 4)
                    for b in range(4):
                        t = slice(256 * h + 64 * b, 256 * h + 64 * b + 64)
                        for e in range(2):
                            if k == 0:
                                ins = mm(bank(6, 16, rows=half(e), at=16 * b), LAT[:, t], wvv)
                            else:
                                o = bank(6 + b // 2, D, rows=half(e), at=256 * (b % 2))
                                mm(o, C("ones", slice(0, 1))[:, 0:64], unit("L1a_v", 1024, D, rows=slice(0, 1)),
                                   True, False)
                                for c in range(2):
                                    ins = mm(o, xnT[:, c, t], wvv[:, c, :], False, c == 1)
                    ins.then_inc(sa_v, 1)

                    def scores(u):
                        t = 8 * k + 4 * h + u
                        ii, j = u // 2, u % 2
                        if u >= 2:
                            pe.wait_ge(sa_d, t - 1)
                        for par in range(2):
                            c = slice(64 * (2 * ii + par), 64 * (2 * ii + par) + 64)
                            R = slice(64 * j, 64 * j + (16 if k == 0 else 48))
                            for p in range(8):
                                ins = mm(bank(u % 2, 64, rows=half(par), at=64 * p), QC[R, p, c],
                                         KC[R, 0 if k == 0 else p, c])
                        ins.then_inc(sa_S, 1)

                    def attend(u):
                        t = 8 * k + 4 * h + u
                        ii, j = u // 2, u % 2
                        pe.wait_ge(sa_P, t + 1)
                        if u >= 2:
                            pe.wait_ge(sa_PT, t - 1)
                        for m in range(4):
                            ins = PE.transpose(bank(2 + u % 2, 128, at=128 * m), SC[:, u % 2, 128 * m:128 * m + 128],
                                               ident)
                        ins.then_inc(sa_T, 1)
                        pe.wait_ge(sa_PT, t + 1)
                        if u == 0:
                            pe.wait_ge(sa_vs, 2 * k + h + 1)
                        for par in range(2):
                            b = 2 * ii + par
                            for m in range(4):
                                ins = mm(bank(4 + j, 64, rows=slice(32 * m, 32 * m + 32), at=256 * h + 64 * b),
                                         VB[:, b, 4 * j + m, :], PT[:, u % 2, 128 * m + 64 * par:128 * m + 64 * par + 64])
                        if u == 3:
                            ins.then_inc(sa_y, 1)

                    scores(0)
                    for u in range(1, 4):
                        scores(u)
                        attend(u - 1)
                    attend(3)
                pe.wait_ge(sa_ys, 4 * k + 4)
                if k == 0:
                    loaded("L0a_b")
                    wo = unit("L0a_b", 0, 2, D)
                    project_out(1, (0, 1, 2, 3), lambda c, i: YT[:, c, tile(i)], lambda c: wo[:, c, :], 2, used=2)
                else:
                    wo = unit("L1a_v", 512, 2, D)
                    project_out(4, (0, 1, 2, 3), lambda c, i: YT[:, c, tile(i)], lambda c: wo[:, c, :], 2,
                                bias=unit("L1a_v", 1280, D, rows=slice(0, 1)), used=3)

            def self1(k):
                L, l = ("L2a", 7) if k == 0 else ("L3a", 10)
                loaded(L)
                wq, wkk, wvv, wo = (unit(L, 512 * n, 2, D) for n in range(4))
                for done, ww, b0 in ((s1_q, wq, 2), (s1_k, wkk, 4)):
                    for c in range(2):
                        for d in range(2):
                            ins = mm(ps[:, b0 + c, :], ww[:, d, 128 * c:128 * c + 128], xnT[:, d, :], d == 0, d == 1)
                    ins.then_inc(done, 1)
                for i in range(NT):
                    for d in range(2):
                        ins = mm(bank(6 + i // 2, D, at=256 * (i % 2)), xnT[:, d, tile(i)], wvv[:, d, :], d == 0, d == 1)
                ins.then_inc(s1_v, 1)
                pe.wait_ge(s1_qs, 1 + k)
                pe.wait_ge(s1_ks, 1 + k)
                for i in range(NT):
                    for c in range(2):
                        ins = mm(bank(0, 128, at=128 * i), SQ[:, c, tile(i)], SK[:, c, tile(i)], c == 0, c == 1)
                ins.then_inc(s1_S, 1)
                pe.wait_ge(s1_P, 1 + k)
                for i in range(NT):
                    ins = PE.transpose(bank(1, 128, at=128 * i), SS[:, i, :], ident)
                ins.then_inc(s1_T, 1)
                pe.wait_ge(s1_PT, 1 + k)
                pe.wait_ge(s1_vs, 2 * k + 2)
                for c in range(2):
                    for i in range(NT):
                        ins = mm(ps[:, 2 + c, tile(i)], SV[:, i, 128 * c:128 * c + 128], SPT[:, i, :])
                ins.then_inc(s1_o, 1)
                pe.wait_ge(s1_os, 2 * k + 2)
                project_out(l, (4, 5, 6, 7), lambda c, i: SO[:, c, tile(i)], lambda c: wo[:, c, :], 2, used=1)

            def spread_scores(k):
                for i in range(NT):
                    pe.wait_ge(rk_diag, 4 * k + i + 1)
                    mm(bank(2 + i, 512), C("same"), RDL).then_inc(rk_spread, 1)

            layernorm(0)
            for g in range(NGROUP):
                transpose_context(0, g)
            pe.wait_ge(cx_Ts_act, NGROUP)
            pe.wait_ge(cx_Ts_dve, NGROUP)
            narrow(0)
            layernorm(1)
            loaded("L0a_a")
            wd = unit("L0a_a", 0, 2, 128)
            for c in range(2):
                ins = mm(ps[:, 2, :], wd[:, c, :], xnT[:, c, :], c == 0, c == 1)
            ins.then_inc(sa_lat, 1)
            pe.wait_ge(sa_lats, 1)
            self16(0)
            layernorm(2)
            gate = C("L0f_gate").rearrange("p (c e) -> p c e", c=2)
            for i in range(NT):
                for c in range(2):
                    ins = mm(bank(2, 8, at=8 * i), xnT[:, c, tile(i)], gate[:, c, :], c == 0, c == 1)
            ins.then_inc(router_logits, 1)
            pe.wait_ge(router_d, 1)
            spread_scores(0)
            pe.wait_ge(L0f_sel, 1)
            for i in range(NT):
                for c in range(2):
                    ins = mm(bank(i, 256, at=256 * c), xn[:, i, 128 * c:128 * c + 128], SEL[:, i])
                ins.then_inc(gathered, 1)
            for e in range(8):
                ins = PE.transpose(bank(6, 128, at=128 * e), SELG[:, e], ident)
            ins.then_inc(comb_T, 1)
            pe.wait_ge(xin_copied, 4)
            pe.wait_ge(comb_Ts, 1)

            def up(e):
                loaded(f"L0f_{e}_w1")
                w1 = unit(f"L0f_{e}_w1", 0, 2, 1024)
                for g in range(2):
                    if e >= 1:
                        pe.wait_ge(L0f_hs, 2 * e - 1 + g)
                    for m in range(4):
                        f = 4 * g + m
                        for c in range(2):
                            ins = mm(bank(4 + g, 128, at=128 * m), w1[:, c, 128 * f:128 * f + 128], XIN[:, c, e],
                                     c == 0, c == 1)
                    ins.then_inc(L0f_h, 1)

            def down(e):
                loaded(f"L0f_{e}_w2")
                w2 = unit(f"L0f_{e}_w2", 0, 8, D)
                if e >= 2:
                    pe.wait_ge(L0f_ys, e - 1)
                pe.wait_ge(L0f_hs, 2 * e + 2)
                for f in range(8):
                    ins = mm(bank(6 + e % 2, D), HT0[:, e % 2, f, :], w2[:, f, :], f == 0, f == 7)
                ins.then_inc(L0f_y, 1)
                pe.wait_ge(L0f_y, e + 1)
                release(2)

            up(0)
            for e in range(8):
                if e < 7:
                    up(e + 1)
                down(e)
            pe.wait_ge(L0f_ys, 8)
            for i in range(NT):
                for e in range(8):
                    R = slice(32 * i, 32 * i + 32)
                    ins = PE.matmul(ps[:, i, 0:D], SGT[R, e, :], YS[R, e, :], start=(e == 0), stop=(e == 7),
                                    tile_position=(32 * i, 0))
                ins.then_inc(layer_out, 1)
            layernorm(3)
            wide(0)
            layernorm(4)
            loaded("L1a_q")
            loaded("L1a_k")
            loaded("L1a_v")
            self16(1)
            layernorm(5)
            router = C("L1f_router").rearrange("p (c e) -> p c e", c=2)
            for i in range(NT):
                for c in range(2):
                    ins = mm(bank(2, 16, at=16 * i), xnT[:, c, tile(i)], router[:, c, :], c == 0, c == 1)
            ins.then_inc(router_logits, 1)
            pe.wait_ge(L1f_hot, 1)
            mm(bank(3, 64), C("tri"), TOH1)
            mm(bank(3, 64, at=64), C("tri"), TOH2, True, False)
            mm(bank(3, 64, at=64), C("same"), TU, False, True).then_inc(L1f_cum, 1)
            pe.wait_ge(L1f_disp, 1)
            for i in range(NT):
                for c in range(2):
                    ins = mm(bank(i, 256, at=256 * c), xn[:, i, 128 * c:128 * c + 128], TD[:, i])
                ins.then_inc(gathered, 1)
            pe.wait_ge(L1f_comb, 1)
            for i in range(NT):
                for g in range(2):
                    ins = PE.transpose(bank(4, 128, at=256 * i + 128 * g), TC[:, i, 8 * g:8 * g + 8, :], ident)
            ins.then_inc(comb_T, 1)
            pe.wait_ge(xin_copied, 8)
            for g in range(2):
                for which, done, bk in ((0, L1f_gate, 2 * g), (1, L1f_up, 2 * g + 1)):
                    for m in range(8):
                        e = 8 * g + m
                        u = f"L1f_g{e // 4}"
                        if which == 0 and m % 4 == 0:
                            loaded(u)
                        ww = unit(u, 0, 4, 2, 256)[:, e % 4, :, 128 * which:128 * which + 128]
                        for c in range(2):
                            ins = mm(bank(bk, 64, at=64 * m), ww[:, c, :], TXIN[:, c, e], c == 0, c == 1)
                    ins.then_inc(done, 1)
                pe.wait_ge(L1f_up, g + 1)
                release(2)
            pe.wait_ge(comb_Ts, 2)
            pe.wait_ge(L1f_hs, 2)
            for c in range(2):
                for e in range(16):
                    if c == 0 and e % 8 == 0:
                        loaded(f"L1f_p{e // 8}")
                    wp = unit(f"L1f_p{e // 8}", 0, 8, D)
                    ins = mm(bank(4 + 2 * c, 64, at=64 * e), wp[:, e % 8, 128 * c:128 * c + 128], THT[:, e, :])
            ins.then_inc(L1f_o, 1)
            pe.wait_ge(L1f_o, 1)
            release(2)
            pe.wait_ge(L1f_os, 4)
            for i in range(NT):
                for g in range(2):
                    for c in range(2):
                        ins = PE.transpose(bank(i, 128, at=256 * g + 128 * c), TOT[:, c, i, 8 * g:8 * g + 8, :],
                                           ident)
                ins.then_inc(L1f_oT, 1)
            pe.wait_ge(L1f_ons, 4)
            for i in range(NT):
                for g in range(2):
                    ins = mm(ps[:, 4 + i, 0:D], TCT[:, i, g, :], TON[:, i, g, :], g == 0, g == 1)
                ins.then_inc(layer_out, 1)
            layernorm(6)
            wide(1)
            layernorm(7)
            self1(0)
            layernorm(8)
            waff = C("L2f_waff").rearrange("p (c e) -> p c e", c=2)
            for i in range(NT):
                for c in range(2):
                    ins = mm(bank(2, 8, at=8 * i), xnT[:, c, tile(i)], waff[:, c, :], c == 0, c == 1)
            ins.then_inc(router_logits, 1)
            pe.wait_ge(L2f_w2, 1)
            wf2 = wv(5696, 2, 8)
            for c in range(2):
                ins = mm(bank(3, 8), C("ones"), wf2[:, c, :], c == 0, c == 1)
            ins.then_inc(L2f_wn, 1)
            pe.wait_ge(L2f_rowsum, 1)
            mm(bank(3, 2, at=8), C("ones"), RB_[:, 0:2]).then_inc(L2f_total, 1)
            pe.wait_ge(L2f_mean, 1)
            spread_scores(1)
            loaded("L2f_b2")
            b2 = unit("L2f_b2", 0, 2 * D, rows=slice(0, 8))

            def gather(e):
                pe.wait_ge(L2f_diag, e + 1)
                if e >= 1:
                    pe.wait_ge(L2f_xis_act, e)
                    pe.wait_ge(L2f_xis_dve, e)
                for c in range(2):
                    for i in range(NT):
                        ins = mm(ps[:, 6 + c, tile(i)], xn[:, i, 128 * c:128 * c + 128], EDG[:, e % 2, i, :])
                ins.then_inc(L2f_xi, 1)

            def up(n):
                e, f = n // 8, n % 8
                w1 = unit(f"L2f_{e}_w1", 0, 2, 1024)
                if f == 0:
                    loaded(f"L2f_{e}_w1")
                    pe.wait_ge(L2f_xis_act, e + 1)
                    pe.wait_ge(L2f_xis_dve, e + 1)
                if n >= 2:
                    pe.wait_ge(L2f_hs, n - 1)
                for c in range(2):
                    ins = mm(ps[:, 4 + n % 2, :], w1[:, c, 128 * f:128 * f + 128], EXI[:, e % 2, c, :], c == 0, c == 1)
                ins.then_inc(L2f_h, 1)

            def down(n):
                e, f = n // 8, n % 8
                w2 = unit(f"L2f_{e}_w2", 0, 8, D)
                if f == 0:
                    loaded(f"L2f_{e}_w2")
                pe.wait_ge(L2f_hs, n + 1)
                for i in range(NT):
                    ins = mm(bank(i // 2, D, at=D * (i % 2)), EH[:, n % 4, tile(i)], w2[:, f, :], False,
                             n == 63 and i % 2 == 1)
                    if n == 63:
                        ins.then_inc(layer_out, 1)
                if n < 63:
                    ins.then_inc(L2f_y, 1)
                if f == 7 and e < 7:
                    pe.wait_ge(L2f_y, n + 1)
                    release(2)

            gather(0)
            pe.wait_ge(rk_spread, 8)
            pe.wait_ge(L2f_diag, 1)
            for n in range(2):
                mm(ps[:, n, :], C("ones", slice(0, 8)), b2, True, False)
            up(0)
            for n in range(64):
                if n % 8 == 4 and n // 8 < 7:
                    gather(n // 8 + 1)
                if n % 8 in (5, 7):
                    transpose_context(1, 2 * (n // 8) + (n % 8 == 7))
                if n < 63:
                    up(n + 1)
                down(n)
            pe.wait_ge(layer_out, 36)
            release(3)
            layernorm("9b")
            loaded("L3x_a")
            wkk = unit("L3x_a", 1024, 2, D)
            for c in range(2):
                mm(ps[:, 0, c:c + 1], wkk[:, 0, 128 * c:128 * c + 128], C("L3x_b2")[:, 0:1], True, False)
                ins = mm(ps[:, 0, c:c + 1], wkk[0:D2, 1, 128 * c:128 * c + 128], C("L3x_b2")[0:D2, 1:2],
                         False, True)
            ins.then_inc(na_kb, 1)
            pe.wait_ge(cx_Ts_act, 2 * NGROUP)
            pe.wait_ge(cx_Ts_dve, 2 * NGROUP)
            narrow(1)
            layernorm(10)
            self1(1)
            layernorm(11)
            loaded("L3f")
            win = unit("L3f", 0, 2, 64)
            wout = unit("L3f", 128, D)
            for h in range(2):
                for c in range(2):
                    ins = mm(ps[half(h), 2, 0:256], win[:, c, :], xnT[:, c, 256 * h:256 * h + 256], c == 0, c == 1)
            ins.then_inc(L3f_s, 1)
            pe.wait_ge(L3f_acc, 16)
            for i in range(NT):
                h = i // 2
                mm(ps[:, 3 + i, 0:D], C("ones", slice(0, 1)), unit("L3f", 384, D, rows=slice(0, 1)), True, False)
                mm(ps[:, 3 + i, 0:D], FG_[half(h), tile(i % 2)], wout[half(h)], False, True) \
                    .then_inc(layer_out, 1)


def chunks(a, width=None):
    k, n = a.shape
    c = -(-k // 128)
    p = np.zeros((c * 128, n), np.float32)
    p[:k] = a
    return p.reshape(c, 128, n).transpose(1, 0, 2).reshape(128, c * n)


def column(v):
    return chunks(np.asarray(v).reshape(-1, 1))


def row(v, width=None):
    p = np.zeros((128, v.size), np.float32)
    p[0] = v
    return p


def packed(g):
    u = {}
    cat = lambda *a: np.concatenate(a, axis=1)

    def keys_transposed(wk):
        return chunks(np.concatenate([wk.T, wk.T[:, 128:DC]], axis=1))

    def bias_columns(bk):
        p = np.zeros((bk.size, 33), np.float32)
        p[:, 0] = p[:, 32] = bk
        return chunks(p)

    def with_row(a, r):
        return np.concatenate([a, np.asarray(r).reshape(1, -1)], axis=0)

    u["L0x_a"] = cat(chunks(g["L0_xattn_Wq"]), keys_transposed(g["L0_xattn_Wk"]),
                     bias_columns(g["L0_xattn_bk"]))
    u["L0x_b"] = chunks(with_row(g["L0_xattn_Wv"], g["L0_xattn_bv"]))

    def slots16(a):
        p = np.zeros((a.shape[0], a.shape[1] // 16, 64), np.float32)
        p[:, :, 0:16] = a.reshape(a.shape[0], -1, 16)
        return p.reshape(a.shape[0], -1)

    order = lambda a: a.reshape(a.shape[0], 4, 2, 2, 16).transpose(0, 3, 1, 2, 4).reshape(a.shape[0], 256)
    kv = g["L0_attn_Wkv_up"]
    u["L0a_a"] = cat(chunks(g["L0_attn_Wc_down"]), slots16(g["L0_attn_Wq_up"]),
                     slots16(np.concatenate([kv[:, :16], kv[:, :16]], axis=1)), kv[:, 16:])
    u["L0a_b"] = chunks(order(g["L0_attn_Wc_proj"].T).T)
    for e in range(8):
        u[f"L0f_{e}_w1"] = chunks(g["L0_ffn_w1"][e])
        u[f"L0f_{e}_w2"] = chunks(g["L0_ffn_w2"][e])
        u[f"L2f_{e}_w1"] = chunks(g["L2_ffn_W1"][e])
        u[f"L2f_{e}_w2"] = chunks(g["L2_ffn_W2"][e])
    for L, n in (("L1x", "L1_xattn"), ("L2x", "L2_xattn")):
        u[f"{L}_q"] = chunks(g[n + "_Wq"])
        p = np.zeros((8, 2, 2, 64, 256), np.float32)
        wk = g[n + "_Wk"].T
        wk = np.concatenate([wk, wk[:, 128:DC]], axis=1).reshape(8, 2, 64, 256)
        for e in range(2):
            p[:, e, e] = wk[:, e]
        p = p.reshape(8, 2, 128, 256).transpose(2, 0, 1, 3)
        u[f"{L}_k0"] = p[:, 0:4].reshape(128, -1)
        u[f"{L}_k1"] = p[:, 4:8].reshape(128, -1)
        u[f"{L}_v"] = chunks(g[n + "_Wv"])
        u[f"{L}_v"][D2, 1024:1024 + D] = g[n + "_bo"]
        u[f"{L}_o"] = chunks(g[n + "_Wo"])

    def qr(q, r):
        p = np.zeros((q.shape[0], 16, 64), np.float32)
        p[:, :, 0:16] = q.reshape(-1, 16, 16)
        p[:, :, 16:48] = r.reshape(-1, 16, 32)
        return p.reshape(q.shape[0], 1024)

    u["L1a_q"] = chunks(qr(g["L1_attn_Wq"], g["L1_attn_Wr"]))
    u["L1a_k"] = chunks(qr(g["L1_attn_Wk"], g["L1_attn_Wr"]))
    u["L1a_v"] = cat(chunks(order(g["L1_attn_Wv"])), chunks(order(g["L1_attn_Wo"].T).T),
                     row(order(g["L1_attn_bv"].reshape(1, -1))[0]), row(g["L1_attn_bo"]))
    for q in range(4):
        u[f"L1f_g{q}"] = np.concatenate([chunks(np.concatenate([g["L1_ffn_w_gate"][e], g["L1_ffn_w_fc"][e]], axis=1))
                                         for e in range(4 * q, 4 * q + 4)], axis=1)
    for q in range(2):
        u[f"L1f_p{q}"] = np.concatenate([g["L1_ffn_w_proj"][e] for e in range(8 * q, 8 * q + 8)], axis=1)
    u["L2a"] = cat(*(chunks(g["L2_attn_" + n]) for n in ("Wq", "Wk", "Wv", "Wo")))
    b2 = np.zeros((128, 2 * D), np.float32)
    b2[:8, :D] = b2[:8, D:] = g["L2_ffn_b2"]
    u["L2f_b2"] = b2
    u["L3x_a"] = cat(chunks(g["L3_xattn_Wq"]), keys_transposed(g["L3_xattn_Wk"]),
                     chunks(g["L3_xattn_Wk"]))
    u["L3x_b"] = cat(chunks(with_row(g["L3_xattn_Wv"], g["L3_xattn_bv"])), chunks(g["L3_xattn_Wo"]),
                     row(g["L3_xattn_bo"]))
    w = g["L3_attn_W_qkv"]
    u["L3a"] = cat(*(chunks(w[n::3].T) for n in range(3)), chunks(g["L3_attn_W_out"].T))
    wout = g["L3_ffn_Wout"]
    u["L3f"] = cat(chunks(g["L3_ffn_Win"]), np.concatenate([wout, wout], axis=0), row(g["L3_ffn_bout"]))

    c = {}
    p = np.arange(128)
    par, t = p // 64, p % 64
    same = par[:, None] == par[None, :]
    c["ident"] = np.eye(128)
    c["ones"] = np.ones((128, 128))
    c["same"] = same
    c["tri"] = same & (t[:, None] <= t[None, :])
    s = np.arange(64)
    c["delta"] = t[:, None] == s[None, :]
    neg = -1e30
    c["causal"] = np.where(s[None, :] <= t[:, None], 0.0, neg)
    c["bfull"] = np.where(same, 0.0, neg)
    c["bcausal"] = np.where(same & (t[None, :] <= t[:, None]), 0.0, neg)
    c["before"] = s[None, :] < t[:, None]
    r = np.arange(32)
    c["slot32"] = np.where((r // 16)[None, :] == par[:, None], (r % 16)[None, :], -1)
    r = np.arange(16)
    c["slot16"] = np.where((r // 8)[None, :] == par[:, None], (r % 8)[None, :] + 1, -1)
    c["rev8"] = np.tile(8 - np.arange(8), (128, 1))
    c["rev16"] = np.tile(16 - np.arange(16), (128, 1))
    c["nhalf"] = np.full((128, 64), -0.5)
    c["half"] = np.full((128, 8), 0.5)
    c = {n: np.asarray(a, np.float32) for n, a in c.items()}
    c["L0x_bq"] = column(g["L0_xattn_bq"])
    c["L1a_bq"] = column(qr(g["L1_attn_bq"].reshape(1, -1), g["L1_attn_br"].reshape(1, -1))[0])
    c["L1a_bk"] = column(qr(g["L1_attn_bk"].reshape(1, -1), g["L1_attn_br"].reshape(1, -1))[0])
    c["L2f_b1"] = column(g["L2_ffn_b1"].reshape(-1))
    c["L2f_waff"] = chunks(g["L2_ffn_waff"].T)
    c["L2f_thr"] = np.broadcast_to(g["L2_ffn_affinity_threshold"].reshape(1, 1), (128, 1))
    c["L0f_gate"] = chunks(g["L0_ffn_gate_w"])
    c["L1f_router"] = chunks(g["L1_ffn_w_router"])
    for n, k in (("g1", "ln1_g"), ("b1", "ln1_b"), ("g2", "ln2_g"), ("b2", "ln2_b"), ("bq", "bq"), ("bk", "bk")):
        c["L3x_" + n] = column(g["L3_xattn_" + k])
    c["L3x_g2"][D2:, 1] = c["L3x_g2"][:D2, 1]
    twice = lambda a: np.concatenate([a, a], axis=0)
    c["L3f_bin"] = twice(g["L3_ffn_bin_"].reshape(-1, 1))
    c["L3f_W1"], c["L3f_b1"], c["L3f_W2"] = (twice(g["L3_ffn_" + n]) for n in ("W1", "b1", "W2"))
    c["L3f_b2"] = twice(g["L3_ffn_b2"].reshape(-1, 1))
    const = np.concatenate([c[n].reshape(128, -1) for n in CW], axis=1)
    assert const.shape == (128, NCONST)
    widths = {n: u[n].shape[1] for n in UNITS}
    assert max(widths.values()) <= SLOT, widths
    units = np.concatenate([u[n].reshape(-1) for n in UNITS])
    return widths, np.ascontiguousarray(units), np.ascontiguousarray(const)


def kernel(**inputs):
    import concourse.bacc as _bacc
    from concourse.bass_utils import run_bass_kernel_spmd as _run

    g = {k: np.asarray(v) for k, v in inputs.items()}
    widths, units, const = packed(g)
    c = g["ctx_768"]
    arrays = {
        "units": units, "consts": const,
        "context": np.ascontiguousarray(c.reshape(B * KT, 128, DC).transpose(1, 0, 2)),
        "x_in": np.ascontiguousarray(g["x"].reshape(NT, 128, D).transpose(1, 0, 2)),
    }
    nc = _bacc.Bacc("TRN2", target_bir_lowering=False, num_devices=1)
    aps = {n: nc.dram_tensor(n, a.shape, F32, kind="ExternalInput").ap() for n, a in arrays.items()}
    out = nc.dram_tensor("out", (128, NT, D), F32, kind="ExternalOutput").ap()
    build(nc, widths, aps["units"], aps["consts"], aps["context"], aps["x_in"], out)
    r = _run(nc, [arrays], core_ids=[0])
    return r.results[0]["out"].transpose(1, 0, 2).reshape(B, S, D)
```

```python
import numpy as np
import concourse.bass as bass
from concourse import mybir
from contextlib import ExitStack

F32 = mybir.dt.float32
BF16 = mybir.dt.bfloat16
F16 = mybir.dt.float16
ALU = mybir.AluOpType
ACT = mybir.ActivationFunctionType
X = mybir.AxisListType.X

B, S, D = 8, 64, 256
LK, DC = 1024, 192
TOK = B * S
NT = TOK // 128
KT = LK // 128
D2 = DC - 128
HB, DHB = 16, 64
NPAIR = HB // 2
LAYERS = 12
CAP = 512

SLOT = 2048
NSLOT = 6

GROUP = 4
NGROUP = B * KT // GROUP
STAGES = 6
FIRST_STAGE_SLOT = NSLOT - STAGES // 2

UNITS = ["L0x_a", "L0x_b", "L0a_a", "L0a_b"]
UNITS += [f"L0f_{e}_{w}" for e in range(8) for w in ("w1", "w2")]
UNITS += ["L1x_q", "L1x_k", "L1x_v", "L1x_o", "L1a_q", "L1a_k", "L1a_v"]
UNITS += [f"L1f_g{g}" for g in range(4)] + [f"L1f_p{g}" for g in range(2)]
UNITS += ["L2x_q", "L2x_k", "L2x_v", "L2x_o", "L2a", "L2f_b2"]
UNITS += [f"L2f_{e}_{w}" for e in range(8) for w in ("w1", "w2", "s1", "s2")]
UNITS += ["L3x_a", "L3x_b", "L3a", "L3f"]
UIDX = {u: n for n, u in enumerate(UNITS)}
SPLIT_UNITS = [u for u in UNITS if u[:4] == "L2f_" and u[-2] == "s"]

CW = {}
_at = 0
for _name, _width in (
    ("ident", 128), ("ones", 128), ("same", 128), ("tri", 128), ("delta", 64), ("causal", 64),
    ("bcausal", 128), ("bfull", 128), ("before", 64), ("slot32", 32), ("slot16", 16), ("rev8", 8),
    ("rev16", 16), ("nhalf", 64), ("half", 8),
    ("L0x_bq", 2), ("L1a_bq", 8), ("L1a_bk", 8), ("L2f_b1", 64), ("L2f_waff", 16), ("L2f_thr", 1),
    ("L0f_gate", 16), ("L1f_router", 32),
    ("L3x_g1", 2), ("L3x_b1", 2), ("L3x_g2", 2), ("L3x_b2", 2), ("L3x_bq", 2), ("L3x_bk", 2),
    ("L3f_bin", 1), ("L3f_W1", 16), ("L3f_b1", 16), ("L3f_W2", 16), ("L3f_b2", 1),
):
    CW[_name] = (_at, _width)
    _at += _width
NCONST = _at


def build(nc, widths, units_d, const_d, ctx_d, x_d, out_d):
    ctx = ExitStack()
    with ctx:
        sem = lambda name: ctx.enter_context(nc.semaphore(name))
        consts_loaded, out_stored, x_final, x_loaded = sem("consts_loaded"), sem("out_stored"), sem("x_final"), sem("x_loaded")
        units_used = sem("units_used")
        dve_step, pool_step = sem("dve_step"), sem("pool_step")
        ln_T, ln_rstd, ln_stats, ln_xn = sem("ln_T"), sem("ln_rstd"), sem("ln_stats"), sem("ln_xn")
        ln_xnT = sem("ln_xnT")
        layer_out = sem("layer_out")
        xa_A, xa_AH, xa_AL, xa_O, xa_OT = sem("xa_A"), sem("xa_AH"), sem("xa_AL"), sem("xa_O"), sem("xa_OT")
        xa_P, xa_PTH, xa_PTL, xa_S = sem("xa_P"), sem("xa_PTH"), sem("xa_PTL"), sem("xa_S")
        xa_T, xa_Z, xa_ZT, xa_ZTs = sem("xa_T"), sem("xa_Z"), sem("xa_ZT"), sem("xa_ZTs")
        xa_B, xa_PL, na_PL = sem("xa_B"), sem("xa_PL"), sem("na_PL")
        xa_Zs, xa_max, xa_q, xa_qs = sem("xa_Zs"), sem("xa_max"), sem("xa_q"), sem("xa_qs")
        xa_recip = sem("xa_recip")
        na_A, na_AH, na_AL, na_P = sem("na_A"), sem("na_AH"), sem("na_AL"), sem("na_P")
        na_PTH, na_PTL, na_S = sem("na_PTH"), sem("na_PTL"), sem("na_S")
        na_T, na_Z, na_ZT, na_ZTs = sem("na_T"), sem("na_Z"), sem("na_ZT"), sem("na_ZTs")
        na_Zs, na_kb, na_kbs, na_max = sem("na_Zs"), sem("na_kb"), sem("na_kbs"), sem("na_max")
        na_ones, na_q, na_qs = sem("na_ones"), sem("na_q"), sem("na_qs")
        na_v, na_vs = sem("na_v"), sem("na_vs")
        sa_P, sa_PT, sa_S, sa_T = sem("sa_P"), sem("sa_PT"), sem("sa_S"), sem("sa_T")
        sa_d, sa_exp, sa_k, sa_k0 = sem("sa_d"), sem("sa_exp"), sem("sa_k"), sem("sa_k0")
        sa_ks0, sa_ks, sa_lat = sem("sa_ks0"), sem("sa_ks"), sem("sa_lat")
        sa_lats, sa_q, sa_qs = sem("sa_lats"), sem("sa_q"), sem("sa_qs")
        sa_v, sa_vs, sa_y, sa_ys = sem("sa_v"), sem("sa_vs"), sem("sa_y"), sem("sa_ys")
        s1_P, s1_PT, s1_S, s1_T = sem("s1_P"), sem("s1_PT"), sem("s1_S"), sem("s1_T")
        s1_d, s1_exp, s1_k = sem("s1_d"), sem("s1_exp"), sem("s1_k")
        s1_o, s1_os, s1_q = sem("s1_o"), sem("s1_os"), sem("s1_q")
        s1_qks, s1_v, s1_vs = sem("s1_qks"), sem("s1_v"), sem("s1_vs")
        comb_T, comb_Ts, gathered, rk_diag = sem("comb_T"), sem("comb_Ts"), sem("gathered"), sem("rk_diag")
        rk_spread, router_d = sem("rk_spread"), sem("router_d")
        router_exp, router_logits = sem("router_exp"), sem("router_logits")
        xin_copied = sem("xin_copied")
        L0f_h, L0f_hs, L0f_sel, L0f_y = sem("L0f_h"), sem("L0f_hs"), sem("L0f_sel"), sem("L0f_y")
        L0f_ys = sem("L0f_ys")
        L1f_comb, L1f_cum, L1f_disp, L1f_gate = sem("L1f_comb"), sem("L1f_cum"), sem("L1f_disp"), sem("L1f_gate")
        L1f_hot, L1f_hs, L1f_o, L1f_oT = sem("L1f_hot"), sem("L1f_hs"), sem("L1f_o"), sem("L1f_oT")
        L1f_ons = sem("L1f_ons")
        L1f_os = sem("L1f_os")
        L1f_silu, L1f_up = sem("L1f_silu"), sem("L1f_up")
        L2f_diag, L2f_h, L2f_hs, L2f_mean = sem("L2f_diag"), sem("L2f_h"), sem("L2f_hs"), sem("L2f_mean")
        L2f_norms, L2f_norms2, L2f_sig = sem("L2f_norms"), sem("L2f_norms2"), sem("L2f_sig")
        L2f_sums, L2f_summed, L2f_xi = sem("L2f_sums"), sem("L2f_summed"), sem("L2f_xi")
        L2f_xih, L2f_xil, L2f_y = sem("L2f_xih"), sem("L2f_xil"), sem("L2f_y")
        L2f_xnh, L2f_xnl, L2f_wh, L2f_wl, L2f_hl = (sem("L2f_xnh"), sem("L2f_xnl"), sem("L2f_wh"), sem("L2f_wl"),
                                                    sem("L2f_hl"))
        cx_stats, cx_rstd, cx_n, cx_hi, cx_lo = sem("cx_stats"), sem("cx_rstd"), sem("cx_n"), sem("cx_hi"), sem("cx_lo")
        cx_T, cx_Ts_act, cx_Ts_dve = sem("cx_T"), sem("cx_Ts_act"), sem("cx_Ts_dve")
        L3f_acc, L3f_relu, L3f_s, L3f_ss = sem("L3f_acc"), sem("L3f_relu"), sem("L3f_s"), sem("L3f_ss")
        slot_loaded = [sem(f"slot{n}_loaded") for n in range(NSLOT)]
        stage_loaded = [sem(f"stage{n}_loaded") for n in range(STAGES)]

        sb = lambda name, shape, dt=F32: ctx.enter_context(nc.sbuf_tensor(name, shape, dt))
        CN = sb("ctx_keys", [128, B * KT, 2 * DC], F16)
        CT = sb("ctx_T", [128, 3, B * LK], F16)
        ident16 = sb("ident16", [128, 128], F16)
        ring = sb("ring", [128, NSLOT, SLOT])
        cst = sb("cst", [128, NCONST])
        x = sb("x", [128, NT, D])
        xn = sb("xn", [128, NT, D])
        xnT = sb("xnT", [128, 2, TOK])
        WORK = 11080
        wk = sb("wk", [128, WORK])
        ps = ctx.enter_context(nc.psum_tensor("ps", [128, 8, 512], F32))

        PE, DVE, ACTE, POOL = nc.tensor, nc.vector, nc.scalar, nc.gpsimd

        def C(name, rows=slice(0, 128)):
            at, width = CW[name]
            return cst[rows, at:at + width]

        def wv(at, *dims, rows=slice(0, 128)):
            n = int(np.prod(dims))
            assert at + n <= WORK
            ap = wk[rows, at:at + n]
            if len(dims) == 2:
                ap = ap.rearrange("p (a b) -> p a b", b=dims[1])
            if len(dims) == 3:
                ap = ap.rearrange("p (a b c) -> p a b c", b=dims[1], c=dims[2])
            if len(dims) == 4:
                ap = ap.rearrange("p (a b c d) -> p a b c d", b=dims[1], c=dims[2], d=dims[3])
            return ap

        def wh(at, *dims, rows=slice(0, 128)):
            n = int(np.prod(dims))
            assert n % 2 == 0 and at + n // 2 <= WORK
            ap = wk[rows, at:at + n // 2].bitcast(F16)
            if len(dims) == 2:
                ap = ap.rearrange("p (a b) -> p a b", b=dims[1])
            if len(dims) == 3:
                ap = ap.rearrange("p (a b c) -> p a b c", b=dims[1], c=dims[2])
            return ap

        def unit(name, at, *dims, rows=slice(0, 128)):
            n = int(np.prod(dims))
            assert at + n <= widths[name], (name, at, dims)
            ap = ring[rows, UIDX[name] % NSLOT, at:at + n]
            if len(dims) == 2:
                ap = ap.rearrange("p (a b) -> p a b", b=dims[1])
            if len(dims) == 3:
                ap = ap.rearrange("p (a b c) -> p a b c", b=dims[1], c=dims[2])
            return ap

        def load_value(name):
            n = UIDX[name]
            return 16 * sum(UNITS[m] not in SPLIT_UNITS for m in range(n % NSLOT, n + 1, NSLOT))

        def unit16(name, at, *dims):
            n = int(np.prod(dims))
            ap = ring[:, UIDX[name] % NSLOT, at // 2:(at + n) // 2].bitcast(F16)
            if len(dims) == 2:
                ap = ap.rearrange("p (a b) -> p a b", b=dims[1])
            return ap

        def bank(n, *dims, rows=slice(0, 128), at=0):
            m = int(np.prod(dims))
            nb = max(1, (at + m + 511) // 512)
            ap = ps[rows, n:n + nb, :].rearrange("p a b -> p (a b)")[:, at:at + m]
            if len(dims) == 2:
                ap = ap.rearrange("p (a b) -> p a b", b=dims[1])
            if len(dims) == 3:
                ap = ap.rearrange("p (a b c) -> p a b c", b=dims[1], c=dims[2])
            if len(dims) == 4:
                ap = ap.rearrange("p (a b c d) -> p a b c d", b=dims[1], c=dims[2], d=dims[3])
            return ap

        def half(par):
            return slice(64 * par, 64 * par + 64)

        def mm(out, lhsT, rhs, start=True, stop=True):
            return PE.matmul(out, lhsT, rhs, start=start, stop=stop)

        ident = C("ident")

        st6 = sb("st6", [128, NT, 6])
        mv = sb("mv", [128, NT, 2])
        rstd = sb("rstd", [128, 2 * NT])
        XQ = wv(0, NPAIR, TOK)
        XP = wv(4096, 1024)
        PL = wh(5120, 2, 1024)
        PH = wh(9800, 2, 1024)
        XB = wv(10824, 2, 128)
        PTH = wh(6144, 2, KT, 128)
        PTL = wh(7168, 2, KT, 128)
        XAH = wh(8192, 2, 256)
        XAL = wh(8448, 2, 256)
        XZ = wv(8704, 2, DC)
        XZT = wv(9088, 2, 256)
        XNM, XRS, XRI = wv(9600, 4), wv(9604, 4), wv(9608, 4)
        NAH, NAL = wh(0, 2, TOK), wh(512, 2, TOK)
        NCR, ONES16 = wh(8192, TOK, rows=slice(0, 33)), wh(8448, TOK, rows=slice(0, 33))
        NKB = wv(9100, 2, 33)
        NQ = wv(1024, 2, TOK)
        NZT1, NZT2 = wv(2048, TOK), wv(2560, TOK)
        NV = wv(3072, 2, TOK)
        QC, KC = wv(0, 8, 256), wv(2048, 8, 256)
        VB = wv(4096, 4, 8, 32)
        LAT = wv(5120, TOK)
        SC = wv(5632, 2, 512)
        PT = wv(6656, 2, 512)
        YT = wv(7680, 2, TOK)
        AMX, ASM, ARC = wv(8704, 2, 8), wv(8720, 2, 8), wv(8736, 2, 8)
        VALUES = ((0, slice(0, 128), 0), (1, slice(0, 128), 2), (2, slice(0, 128), 1), (3, half(0), 3), (3, half(1), 0))
        VALUES_AT = ((0, 2, 1, 3), (3, 0, 2, 1))
        SQ, SK = wv(0, 2, TOK), wv(1024, 2, TOK)
        SV = wv(2048, NT, D)
        SS = wv(3072, NT, 128)
        SPT = wv(3584, NT, 128)
        SO = wv(4096, 2, TOK)
        SMX, SSM, SRC = wv(5120, NT), wv(5124, NT), wv(5128, NT)
        RP = wv(9616, NT, 8)
        RK = wv(9648, NT, 8)
        RA, RB_, RC_ = wv(9680, 4), wv(9684, 4), wv(9688, 4)
        RL = wv(9692, NT, 8)
        ROH = wv(9724, NT, 8)
        RT = wv(9756, NT, 8)
        RS1 = wv(9788, 8)
        RDL = wv(7232, 8, 64)
        RG, RE, RBEF = wh(5184, 8, 64), wh(5696, 8, 64), wh(6208, 64)
        SEL = wv(64, NT, 8, 32)
        SELG = wv(1088, 8, NT, 32)
        SGTH, SGTL = wh(2112, 8, 128), wh(2624, 8, 128)
        XIN = wv(3136, 2, 8, NT, 32)
        HT0 = wv(5184, 2, 8, 128)
        YH, YL = wh(7232, 8, D), wh(8256, 8, D)
        TP = wv(0, NT, 16)
        TOH1, TOH2, TQ1, TQ2 = wv(64, NT, 16), wv(128, NT, 16), wv(192, NT, 16), wv(256, NT, 16)
        TT, TU = wv(320, NT, 16), wv(384, NT, 16)
        TM1, TM2, TV = wv(448, NT), wv(452, NT), wv(456, NT)
        TD = wv(1024, NT, 16, 16)
        TC = wv(2048, NT, 16, 16)
        TX_ = wv(6144, NT, 16, 16)
        TCT = wv(3072, NT, 2, 128)
        TXIN = wv(4096, 2, 16, NT, 16)
        TSG = wv(6144, 2, 512)
        THT = wv(7168, 16, 64)
        TOT = wv(4096, 2, NT, 16, 16)
        TON = wv(6144, NT, 2, D)
        EXH, EXL = wh(0, 4, TOK), wh(1024, 4, TOK)
        EDG = wh(2048, 2, NT, 128)
        EHH, EHL = wh(3072, 4, TOK), wh(4096, 4, TOK)
        EG = wv(5184, 4, TOK)
        XNH, XNL = wh(9800, NT, D), wh(10312, NT, D)
        FS, FT, FG_ = wv(0, 256), wv(256, 4, 256), wv(1280, 256)

        def stage(p, g):
            if p == 0:
                n = g % STAGES
                ap = ring[:, FIRST_STAGE_SLOT + n // 2, GROUP * DC * (n % 2):GROUP * DC * (n % 2 + 1)]
                return ap.rearrange("p (a b) -> p a b", b=DC)
            return wv(7744 + GROUP * DC * (g % 2), GROUP, DC)

        def stage_value(p, g):
            before = len(range(g % 2, NGROUP, STAGES))
            return 16 * (g // STAGES + 1) if p == 0 else 16 * (before + g // 2 + 1)

        PST6, PMV, PRS = wv(9280, 2, GROUP, 6), wv(9328, 2, GROUP, 2), wv(9344, 2, GROUP)

        def ctx_banks(p, g):
            return 4 + 2 * (g % 2) if p == 0 else 2

        LN = {l: l for l in range(10)} | {"9b": 10, 10: 11, 11: 12}
        LNT = {l: l for l in range(9)} | {"9b": 9, 10: 10, 11: 11}

        AT_Q, AT_A, AT_S = 0, 3, 7

        block = ctx.enter_context(nc.Block())

        @block.sync
        def _(sp):
            sp.dma_start(x[:, :, :], x_d).then_inc(x_loaded, 16)
            sp.dma_start(cst[:, :], const_d).then_inc(consts_loaded, 16)
            at = 0

            def load(n):
                nonlocal at
                name = UNITS[n]
                if n >= NSLOT and name not in SPLIT_UNITS:
                    sp.wait_ge(units_used, n - NSLOT + 1)
                w = widths[name]
                if name in SPLIT_UNITS:
                    return
                sp.dma_start(ring[:, n % NSLOT, 0:w], units_d[at:at + 128 * w].rearrange("(p w) -> p w", p=128)) \
                    .then_inc(slot_loaded[n % NSLOT], 16)
                at += 128 * w

            load(0)
            for g in range(NGROUP):
                if g >= STAGES:
                    sp.wait_ge(cx_lo, g - STAGES + 1)
                sp.dma_start(stage(0, g), ctx_d[:, GROUP * g:GROUP * g + GROUP, :]).then_inc(stage_loaded[g % STAGES], 16)
            for n in range(1, len(UNITS)):
                if n == FIRST_STAGE_SLOT:
                    sp.wait_ge(cx_lo, NGROUP)
                load(n)
                if UNITS[n][:4] == "L2f_" and UNITS[n][-2:] == "w2":
                    e = int(UNITS[n][4])
                    if e == 0:
                        sp.wait_ge(layer_out, 4 * 6 + 4)
                    for g in (2 * e, 2 * e + 1):
                        if g >= 2:
                            sp.wait_ge(cx_lo, NGROUP + g - 1)
                        sp.dma_start(stage(1, g), ctx_d[:, GROUP * g:GROUP * g + GROUP, :]).then_inc(stage_loaded[g % 2], 16)
            sp.wait_ge(x_final, NT)
            sp.dma_start(out_d, x[:, :, :]).then_inc(out_stored, 16)
            sp.wait_ge(out_stored, 16)

        @block.gpsimd
        def _(pool):
            pool.wait_ge(consts_loaded, 16)

            def rsqrt(n):
                pool.wait_ge(ln_stats, n + 1)
                r = rstd[:, 0:NT]
                POOL.tensor_tensor(r, r, C("nhalf")[:, 0:NT], ALU.pow).then_inc(ln_rstd, 1)

            def block_diagonal(k):
                pool.wait_ge(xa_qs, 8 * k + 8)

                def batch(b, first):
                    t0 = 64 * k + 8 * b if first else b * 8 + 64 * k
                    for r in range(NPAIR):
                        if not (first and r < 2):
                            pool.wait_ge(xa_A, t0 + r - 1)
                        POOL.tensor_tensor(XB[:, r % 2, :].rearrange("p (a b) -> p a b", b=64),
                                           XQ[:, r, bass.ds(b * 64, 64)].unsqueeze(1).to_broadcast([128, 2, 64]),
                                           C("same").rearrange("p (a b) -> p a b", b=64), ALU.mult).then_inc(xa_B, 1)

                batch(0, True)
                with pool.Fori(1, B) as b:
                    batch(b, False)

            n = 0
            for l in range(LAYERS):
                rsqrt(n)
                n += 1
                if l in (3, 6):
                    block_diagonal(l // 3 - 1)
                if l == 9:
                    rsqrt(n)
                    n += 1
                if l == 8:
                    pool.wait_ge(L2f_norms2, 2)
                    POOL.tensor_tensor(RA, RA, C("half")[:, 0:NT], ALU.pow).then_inc(L2f_norms, 1)
                    POOL.tensor_tensor(RS1, RS1, C("half")[:, 0:8], ALU.pow).then_inc(L2f_norms, 1)

                    pool.wait_ge(L2f_xnh, 1)
                    POOL.tensor_tensor(XNL, xn[:, :, :], XNH, ALU.subtract).then_inc(L2f_xnl, 1)

                    def weights_low(e, w):
                        pool.wait_ge(L2f_wh, 2 * e + w + 1)
                        src = unit(f"L2f_{e}_w{w + 1}", 0, SLOT)
                        POOL.tensor_tensor(unit16(f"L2f_{e}_s{w + 1}", SLOT, SLOT), src,
                                           unit16(f"L2f_{e}_s{w + 1}", 0, SLOT), ALU.subtract).then_inc(L2f_wl, 1)

                    def context_rstd(g):
                        pool.wait_ge(cx_stats, g + 1)
                        r = PRS[:, g % 2, :]
                        POOL.tensor_scalar(r, PMV[:, g % 2, :, 1], 1e-5, None, ALU.add).then_inc(pool_step, 1)
                        pool.wait_ge(pool_step, g + 1)
                        POOL.tensor_tensor(r, r, C("nhalf")[:, 0:GROUP], ALU.pow).then_inc(cx_rstd, 1)

                    weights_low(0, 0)
                    weights_low(0, 1)
                    for e in range(8):
                        context_rstd(2 * e)
                        if e < 7:
                            weights_low(e + 1, 0)
                        context_rstd(2 * e + 1)
                        if e < 7:
                            weights_low(e + 1, 1)

        @block.scalar
        def _(act):
            act.wait_ge(consts_loaded, 16)

            def layernorm(key, affine=None):
                act.wait_ge(ln_T, LNT[key] + 1)
                if affine is None:
                    ACTE.copy(xnT[:, 0, :], ps[:, 0, :]).then_inc(ln_xnT, 1)
                else:
                    g, b = affine
                    ACTE.activation(xnT[:, 0, :], ps[:, 0, :], ACT.Identity, scale=C(g)[:, 0:1],
                                    bias=C(b)[:, 0:1]).then_inc(ln_xnT, 1)

            def wide(k):
                for r in range(0, NPAIR, 2):
                    act.wait_ge(xa_q, 8 * k + r + 1)
                    ACTE.mul(XQ[:, r, :], ps[:, r, :], DHB ** -0.5).then_inc(xa_qs, 1)

                def queries(t, r):
                    act.wait_ge(xa_A, t + 1)
                    ACTE.copy(XAH[:, r % 2, :], bank(7, 256)).then_inc(xa_AH, 1)

                def exp(t, r, first, second):
                    act.wait_ge(xa_max, t + 1)
                    m = XNM[:, r % 4:r % 4 + 1]
                    if not first:
                        act.wait_ge(xa_PL, t)
                    ACTE.activation(XP, bank(2 * (r % 2), 1024), ACT.Exp, bias=m,
                                    accum_out=XRS[:, r % 4:r % 4 + 1]).then_inc(xa_P, 1)
                    if not (first or second):
                        act.wait_ge(xa_T, 2 * t - 3)
                    ACTE.activation(PH[:, r % 2, :], bank(2 * (r % 2), 1024), ACT.Exp, bias=m).then_inc(xa_P, 1)

                def spread(t, r, first):
                    if not first:
                        act.wait_ge(xa_Z, t - 1)
                    act.wait_ge(xa_T, 2 * t + 1)
                    ACTE.copy(PTH[:, r % 2, :, :], bank(4, 512).bitcast(F16).rearrange("p (a b) -> p a b", b=128)) \
                        .then_inc(xa_PTH, 1)

                def heads(t, r, b):
                    act.wait_ge(xa_O, t + 1)
                    ACTE.copy(XQ[:, r, bass.ds(b * 64, 64)], bank(7, 64, at=256)).then_inc(xa_OT, 1)

                def batch(b, first, last):
                    t0 = 64 * k + 8 * b if isinstance(b, int) else b * 8 + 64 * k
                    for r in range(NPAIR):
                        t = t0 + r
                        if not (last and r == NPAIR - 1):
                            queries(t + 1, r + 1)
                        exp(t, r, first and r == 0, first and r == 1)
                        if not (first and r < 1):
                            spread(t - 1, (r - 1) % NPAIR, first and r < 3)
                        if not (first and r < 3):
                            heads(t - 3, (r - 3) % NPAIR, b if r >= 3 else b - 1)

                queries(64 * k, 0)
                batch(0, True, False)
                with act.Fori(1, B - 1) as b:
                    batch(b, False, False)
                batch(B - 1, False, True)
                t1 = 64 * (k + 1)
                spread(t1 - 1, 7, False)
                for r in (5, 6, 7):
                    heads(t1 - 8 + r, r, B - 1)

            def split_high(p, g):
                if p == 0:
                    act.wait_ge(stage_loaded[g % STAGES], stage_value(0, g))
                else:
                    act.wait_ge(cx_n, g + 1)
                ACTE.copy(CN[:, GROUP * g:GROUP * g + GROUP, 0:DC], stage(p, g)).then_inc(cx_hi, 1)

            def spread_high(p, g):
                act.wait_ge(cx_T, NGROUP * p + g + 1)
                ACTE.copy(CT[:, 0:2, 512 * g:512 * g + 512],
                          bank(ctx_banks(p, g), 512).bitcast(F16).rearrange("p (a b) -> p a b", b=512)) \
                    .then_inc(cx_Ts_act, 1)

            def narrow_high(k, parts=range(3)):
                for c in parts:
                    act.wait_ge(na_A, 3 * k + c + 1)
                    if c == 2:
                        ACTE.copy(NCR, bank(2, TOK, rows=slice(0, 33))).then_inc(na_AH, 1)
                    elif k == 0:
                        ACTE.copy(NAH[:, c, :], ps[:, c, :]).then_inc(na_AH, 1)
                    else:
                        ACTE.activation(NAH[:, c, :], ps[:, c, :], ACT.Identity,
                                        scale=C("L3x_g2")[:, c:c + 1]).then_inc(na_AH, 1)

            def narrow_exp(k, i):
                t = 4 * k + i
                act.wait_ge(na_max, t + 1)
                if i >= 1:
                    act.wait_ge(na_PL, t)
                ACTE.activation(XP, bank(2 * (i % 2), 1024), ACT.Exp, bias=XNM[:, i:i + 1],
                                accum_out=XRS[:, i:i + 1]).then_inc(na_P, 1)
                if i >= 2:
                    act.wait_ge(na_T, 2 * t - 3)
                ACTE.activation(PH[:, i % 2, :], bank(2 * (i % 2), 1024), ACT.Exp,
                                bias=XNM[:, i:i + 1]).then_inc(na_P, 1)

            def narrow(k):
                def spread(i):
                    t = 4 * k + i
                    if i >= 2:
                        act.wait_ge(na_Z, t - 1)
                    act.wait_ge(na_T, 2 * t + 1)
                    ACTE.copy(PTH[:, i % 2, :, :], bank(4, 512).bitcast(F16).rearrange("p (a b) -> p a b", b=128)) \
                        .then_inc(na_PTH, 1)

                for i in range(NT):
                    if k == 1 or i >= 2:
                        narrow_exp(k, i)
                    if i >= 1:
                        spread(i - 1)
                spread(NT - 1)

            def self16(k):
                scale = 0.25 if k == 0 else 48 ** -0.5
                for h in range(2):
                    for r in (0, 1, 4, 5):
                        act.wait_ge(sa_q, 8 * k + 4 * h + r // 2 + 1)
                        src = bank(r // 2, 256, at=256 * (r % 2))
                        if k == 0:
                            ACTE.copy(QC[:, r, :], src).then_inc(sa_qs, 1)
                        else:
                            ACTE.activation(QC[:, r, :], src, ACT.Identity,
                                            bias=C("L1a_bq")[:, r:r + 1]).then_inc(sa_qs, 1)
                    for r in (0, 1, 4, 5):
                        if k == 1:
                            act.wait_ge(sa_k, 4 * h + r // 2 + 1)
                            ACTE.activation(KC[:, r, :], bank(4 + r // 2, 256, at=256 * (r % 2)), ACT.Identity,
                                            bias=C("L1a_bk")[:, r:r + 1]).then_inc(sa_ks, 1)
                    for u in range(4):
                        t = 8 * k + 4 * h + u
                        if u >= 1:
                            act.wait_ge(sa_T, t)
                            ACTE.copy(PT[:, (u - 1) % 2, :], ps[:, 2 + (u - 1) % 2, :]).then_inc(sa_PT, 1)
                        act.wait_ge(sa_d, t + 1)
                        ACTE.activation(SC[:, u % 2, :], SC[:, u % 2, :], ACT.Exp, scale=scale).then_inc(sa_exp, 1)
                    act.wait_ge(sa_T, 8 * k + 4 * h + 4)
                    ACTE.copy(PT[:, 1, :], ps[:, 3, :]).then_inc(sa_PT, 1)
                    act.wait_ge(sa_y, 2 * k + h + 1)
                    ACTE.copy(YT[:, 0, 256 * h:256 * h + 256], ps[:, 4, 256 * h:256 * h + 256]).then_inc(sa_ys, 1)

            def self1(k):
                act.wait_ge(s1_q, 1 + k)
                ACTE.copy(SQ, bank(2, 2, TOK)).then_inc(s1_qks, 1)
                act.wait_ge(s1_v, 1 + k)
                ACTE.copy(SV[:, 0:2, :], bank(6, 2, D)).then_inc(s1_vs, 1)
                act.wait_ge(s1_d, 1 + k)
                ACTE.activation(SS, SS, ACT.Exp, scale=D ** -0.5).then_inc(s1_exp, 1)
                act.wait_ge(s1_T, 1 + k)
                ACTE.copy(SPT, bank(1, NT, 128)).then_inc(s1_PT, 1)
                act.wait_ge(s1_o, 1 + k)
                ACTE.copy(SO[:, 0, :], ps[:, 2, :]).then_inc(s1_os, 1)

            layernorm(0)
            for g in range(NGROUP):
                if 0 <= g - AT_A - 2 < 3:
                    narrow_high(0, [g - AT_A - 2])
                if g == AT_S + 7:
                    narrow_exp(0, 0)
                split_high(0, g)
                if g >= 2:
                    spread_high(0, g - 2)
            spread_high(0, NGROUP - 2)
            spread_high(0, NGROUP - 1)
            narrow_exp(0, 1)
            narrow(0)
            layernorm(1)
            act.wait_ge(sa_lat, 1)
            ACTE.copy(LAT, ps[:, 2, :]).then_inc(sa_lats, 1)
            self16(0)
            layernorm(2)
            act.wait_ge(router_d, 1)
            ACTE.activation(RP, RP, ACT.Exp).then_inc(router_exp, 1)
            act.wait_ge(comb_T, 1)
            ACTE.copy(SGTH, bank(6, 8, 128)).then_inc(comb_Ts, 1)
            for i in range(0, NT, 2):
                act.wait_ge(gathered, i + 1)
                ACTE.copy(XIN[:, :, :, i, :], bank(i, 2, 8, 32)).then_inc(xin_copied, 1)
            for e in range(8):
                for g in range(2):
                    act.wait_ge(L0f_h, 2 * e + g + 1)
                    if e >= 2:
                        act.wait_ge(L0f_y, e - 1)
                    ACTE.activation(HT0[:, e % 2, 4 * g:4 * g + 4, :], bank(4 + g, 4, 128),
                                    ACT.Gelu_apprx_tanh).then_inc(L0f_hs, 1)
            layernorm(3)
            wide(0)
            layernorm(4)
            self16(1)
            layernorm(5)
            act.wait_ge(router_d, 2)
            ACTE.activation(TP, TP, ACT.Exp).then_inc(router_exp, 1)
            for i in range(0, NT, 2):
                act.wait_ge(gathered, i + 5)
                ACTE.copy(TXIN[:, :, :, i, :], bank(i, 2, 16, 16)).then_inc(xin_copied, 1)
            act.wait_ge(comb_T, 2)
            ACTE.copy(TCT, bank(4, NT, 2, 128)).then_inc(comb_Ts, 1)
            for g in range(2):
                act.wait_ge(L1f_gate, g + 1)
                ACTE.activation(TSG[:, g, :], ps[:, 2 * g, :], ACT.Silu).then_inc(L1f_silu, 1)
            act.wait_ge(L1f_o, 1)
            for c in range(2):
                for g in range(2):
                    if g == 0:
                        ACTE.copy(TOT[:, c, :, 8 * g:8 * g + 8, :].rearrange("p i e s -> p e i s"),
                                  bank(4 + 2 * c + g, 8, NT, 16)).then_inc(L1f_os, 1)
            for i in range(0, NT, 2):
                act.wait_ge(L1f_oT, i + 1)
                ACTE.copy(TON[:, i, :, :], bank(i, 2, D)).then_inc(L1f_ons, 1)
            layernorm(6)
            wide(1)
            layernorm(7)
            self1(0)
            layernorm(8)
            ACTE.copy(XNH, xn[:, :, :]).then_inc(L2f_xnh, 1)

            def weights_high(e, w):
                u = f"L2f_{e}_w{w + 1}"
                act.wait_ge(slot_loaded[UIDX[u] % NSLOT], load_value(u))
                if e >= 1:
                    act.wait_ge(L2f_wl, 2 * (e - 1) + w + 1)
                ACTE.copy(unit16(f"L2f_{e}_s{w + 1}", 0, SLOT), unit(u, 0, SLOT)).then_inc(L2f_wh, 1)

            weights_high(0, 0)
            weights_high(0, 1)
            act.wait_ge(router_d, 3)
            ACTE.activation(RL, RL, ACT.Exp).then_inc(router_exp, 1)
            act.wait_ge(L2f_mean, 1)
            ACTE.activation(RC_[:, 1:2], RC_[:, 0:1], ACT.Exp, scale=-1.0).then_inc(L2f_sig, 1)

            def copy_inputs(e):
                act.wait_ge(L2f_xi, e + 1)
                if e >= 2:
                    act.wait_ge(L2f_h, 8 * (e - 1))
                for c in range(2):
                    ACTE.copy(EXH[:, 2 * (e % 2) + c, :], ps[:, 6 + c, :]).then_inc(L2f_xih, 1)

            copy_inputs(0)
            for n in range(64):
                e, f = n // 8, n % 8
                if f == 0 and e > 0:
                    spread_high(1, 2 * e - 2)
                if f == 2:
                    split_high(1, 2 * e)
                if f == 3 and e < 7:
                    weights_high(e + 1, 0)
                if f == 4 and e < 7:
                    copy_inputs(e + 1)
                if f == 5 and e > 0:
                    spread_high(1, 2 * e - 1)
                if f == 5 and e < 7:
                    weights_high(e + 1, 1)
                if f == 6:
                    split_high(1, 2 * e + 1)
                act.wait_ge(L2f_h, n + 1)
                if n >= 4:
                    act.wait_ge(L2f_hl, n - 3)
                    act.wait_ge(L2f_y, n - 3)
                for out in (EG, EHH):
                    ACTE.activation(out[:, n % 4, :], ps[:, 4 + n % 2, :], ACT.Gelu,
                                    bias=C("L2f_b1")[:, n:n + 1]).then_inc(L2f_hs, 1)
            spread_high(1, NGROUP - 2)
            spread_high(1, NGROUP - 1)
            layernorm("9b", affine=("L3x_g1", "L3x_b1"))
            narrow_high(1)
            narrow(1)
            act.wait_ge(na_v, 1)
            ACTE.copy(NV[:, 0, :], ps[:, 0, :]).then_inc(na_vs, 1)
            layernorm(10)
            self1(1)
            layernorm(11)
            act.wait_ge(L3f_ss, 1)
            for h in range(16):
                if h >= 4:
                    act.wait_ge(L3f_acc, h - 3)
                ACTE.activation(FT[:, h % 4, :], FS, ACT.Relu, scale=C("L3f_W1")[:, h:h + 1],
                                bias=C("L3f_b1")[:, h:h + 1]).then_inc(L3f_relu, 1)

        @block.vector
        def _(dve):
            chain = [0]

            def link(ins):
                chain[0] += 1
                ins.then_inc(dve_step, 1)
                dve.wait_ge(dve_step, chain[0])

            dve.wait_ge(consts_loaded, 16)
            link(DVE.tensor_copy(ident16[:, :], ident))
            dve.wait_ge(x_loaded, 16)

            def layernorm(key, affine=None):
                n = LN[key]
                src = xn if key == "9b" else x
                if key in (0, "9b"):
                    for i in range(NT):
                        ins = DVE.bn_stats(st6[:, i, :], src[:, i, :])
                    link(ins)
                for i in range(NT):
                    ins = DVE.bn_aggr(mv[:, i, :], st6[:, i, :])
                link(ins)
                DVE.tensor_scalar(rstd[:, 0:NT], mv[:, :, 1], 1e-5, None, ALU.add).then_inc(ln_stats, 1)
                dve.wait_ge(ln_rstd, n + 1)
                for i in range(NT):
                    DVE.tensor_scalar(xn[:, i, :], src[:, i, :], mv[:, i, 0:1], rstd[:, i:i + 1], ALU.subtract,
                                      ALU.mult).then_inc(ln_xn, 1)
                if key == 9:
                    dve.wait_ge(ln_xn, 4 * (LN[9] + 1))
                    return
                dve.wait_ge(ln_T, LNT[key] + 1)
                if affine is None:
                    DVE.tensor_copy(xnT[:, 1, :], ps[:, 1, :]).then_inc(ln_xnT, 1)
                else:
                    g, b = affine
                    DVE.tensor_scalar(xnT[:, 1, :], ps[:, 1, :], C(g)[:, 1:2], C(b)[:, 1:2], ALU.mult,
                                      ALU.add).then_inc(ln_xnT, 1)

            def add_x(l, banks):
                for i in range(NT):
                    dve.wait_ge(layer_out, 4 * l + i + 1)
                    ins = DVE.tensor_tensor(x[:, i, :], x[:, i, :], ps[:, banks[i], 0:D], ALU.add)
                    if l == LAYERS - 1:
                        ins.then_inc(x_final, 1)
                    else:
                        link(ins)
                        ins = DVE.bn_stats(st6[:, i, :], x[:, i, :])
                        if i == NT - 1:
                            link(ins)

            def wide(k):
                for r in range(1, NPAIR, 2):
                    dve.wait_ge(xa_q, 8 * k + r + 1)
                    DVE.tensor_scalar(XQ[:, r, :], ps[:, r, :], DHB ** -0.5, None, ALU.mult).then_inc(xa_qs, 1)

                def rowmax(t, r):
                    dve.wait_ge(xa_S, t + 1)
                    DVE.tensor_reduce(XNM[:, r % 4:r % 4 + 1], bank(2 * (r % 2), 1024), X, ALU.max,
                                      negate=True).then_inc(xa_max, 1)

                def queries(t, r):
                    dve.wait_ge(xa_AH, t + 1)
                    DVE.tensor_tensor(XAL[:, r % 2, :], bank(7, 256), XAH[:, r % 2, :], ALU.subtract).then_inc(xa_AL, 1)

                def split(t, r, first):
                    dve.wait_ge(xa_P, 2 * t + 2)
                    if not first:
                        dve.wait_ge(xa_T, 2 * t - 2)
                    DVE.tensor_tensor(PL[:, r % 2, :], XP, PH[:, r % 2, :], ALU.subtract).then_inc(xa_PL, 1)

                def spread(t, r, first):
                    if not first:
                        dve.wait_ge(xa_Z, t - 1)
                    dve.wait_ge(xa_T, 2 * t + 2)
                    DVE.tensor_copy(PTL[:, r % 2, :, :], bank(5, 512).bitcast(F16).rearrange("p (a b) -> p a b", b=128)) \
                        .then_inc(xa_PTL, 1)

                def normalise(t, r):
                    dve.wait_ge(xa_P, 2 * t + 2)
                    recip = XRI[:, r % 4:r % 4 + 1]
                    DVE.reciprocal(recip, XRS[:, r % 4:r % 4 + 1]).then_inc(xa_recip, 1)
                    dve.wait_ge(xa_recip, 2 * t + 1)
                    dve.wait_ge(xa_Z, t + 1)
                    DVE.tensor_scalar(XZ[:, r % 2, :], bank(6, DC), recip, None, ALU.mult).then_inc(xa_recip, 1)
                    dve.wait_ge(xa_recip, 2 * t + 2)
                    for c, at in ((slice(128, DC), DC), (slice(0, 128), 256)):
                        z = XZ[:, r % 2, c]
                        DVE.scalar_tensor_tensor(z, bank(6, c.stop - c.start, at=at), recip, z, ALU.mult,
                                                 ALU.add).then_inc(xa_Zs, 1)

                def ztrans(t, r):
                    dve.wait_ge(xa_ZT, t + 1)
                    DVE.tensor_copy(XZT[:, r % 2, 0:128], bank(6, 128)).then_inc(xa_ZTs, 1)
                    DVE.tensor_copy(XZT[0:D2, r % 2, 128:256], bank(6, 128, rows=slice(0, D2), at=128)) \
                        .then_inc(xa_ZTs, 1)

                def batch(b, first, last):
                    t0 = 64 * k + 8 * b if isinstance(b, int) else b * 8 + 64 * k
                    for r in range(NPAIR):
                        t = t0 + r
                        if not (first and r < 3):
                            ztrans(t - 3, (r - 3) % NPAIR)
                        rowmax(t, r)
                        if not (last and r == NPAIR - 1):
                            queries(t + 1, r + 1)
                        if not (first and r < 1):
                            spread(t - 1, (r - 1) % NPAIR, first and r < 3)
                        if not (first and r < 2):
                            normalise(t - 2, (r - 2) % NPAIR)
                        split(t, r, first and r < 2)

                queries(64 * k, 0)
                batch(0, True, False)
                with dve.Fori(1, B - 1) as b:
                    batch(b, False, False)
                batch(B - 1, False, True)
                t1 = 64 * (k + 1)
                ztrans(t1 - 3, 5)
                spread(t1 - 1, 7, False)
                normalise(t1 - 2, 6)
                ztrans(t1 - 2, 6)
                normalise(t1 - 1, 7)
                ztrans(t1 - 1, 7)

            def context_stats(g):
                dve.wait_ge(stage_loaded[g % 2], stage_value(1, g))
                for m in range(GROUP):
                    ins = DVE.bn_stats(PST6[:, g % 2, m, :], stage(1, g)[:, m, :])
                link(ins)
                for m in range(GROUP):
                    ins = DVE.bn_aggr(PMV[:, g % 2, m, :], PST6[:, g % 2, m, :])
                ins.then_inc(cx_stats, 1)

            def context_norm(g):
                dve.wait_ge(cx_rstd, g + 1)
                for m in range(GROUP):
                    c = stage(1, g)[:, m, :]
                    ins = DVE.tensor_scalar(c, c, PMV[:, g % 2, m, 0:1], PRS[:, g % 2, m:m + 1], ALU.subtract, ALU.mult)
                ins.then_inc(cx_n, 1)

            def split_low(p, g):
                dve.wait_ge(cx_hi, NGROUP * p + g + 1)
                c = slice(GROUP * g, GROUP * g + GROUP)
                src = stage(p, g)
                DVE.tensor_tensor(CN[:, c, DC:DC + D2], src[:, :, 128:DC], CN[:, c, 128:DC], ALU.subtract)
                DVE.tensor_tensor(CN[:, c, DC + D2:], src[:, :, 0:128], CN[:, c, 0:128], ALU.subtract) \
                    .then_inc(cx_lo, 1)

            def spread_low(p, g):
                dve.wait_ge(cx_T, NGROUP * p + g + 1)
                DVE.tensor_copy(CT[:, 2, 512 * g:512 * g + 512], bank(ctx_banks(p, g) + 1, 256).bitcast(F16)) \
                    .then_inc(cx_Ts_dve, 1)

            def narrow_queries(k, parts=range(2)):
                for c in parts:
                    if c == 0:
                        DVE.memset(ONES16, 1.0)
                    dve.wait_ge(na_q, 2 * k + c + 1)
                    DVE.tensor_scalar(NQ[:, c, :], ps[:, 2 + c, :], C("L0x_bq" if k == 0 else "L3x_bq")[:, c:c + 1],
                                      D ** -0.5, ALU.add, ALU.mult).then_inc(na_qs, 1)

            def narrow_low(k, parts=range(3)):
                for c in parts:
                    dve.wait_ge(na_AH, 3 * k + c + 1)
                    if c == 2:
                        R = slice(32, 33)
                        DVE.tensor_tensor(NCR[R], bank(2, TOK, rows=R), NCR[R], ALU.subtract).then_inc(na_AL, 1)
                    elif k == 0:
                        DVE.tensor_tensor(NAL[:, c, :], ps[:, c, :], NAH[:, c, :], ALU.subtract).then_inc(na_AL, 1)
                    else:
                        DVE.scalar_tensor_tensor(NAL[:, c, :], ps[:, c, :], C("L3x_g2")[:, c:c + 1], NAH[:, c, :],
                                                 ALU.mult, ALU.subtract).then_inc(na_AL, 1)

            def narrow_max(k, i):
                dve.wait_ge(na_S, 4 * k + i + 1)
                DVE.tensor_reduce(XNM[:, i:i + 1], bank(2 * (i % 2), 1024), X, ALU.max, negate=True) \
                    .then_inc(na_max, 1)

            def narrow_split(k, i):
                t = 4 * k + i
                dve.wait_ge(na_P, 2 * t + 2)
                if i >= 2:
                    dve.wait_ge(na_T, 2 * t - 2)
                DVE.tensor_tensor(PL[:, i % 2, :], XP, PH[:, i % 2, :], ALU.subtract).then_inc(na_PL, 1)

            def narrow(k):
                DVE.memset(NZT2[D2:D2 + 1], 1.0).then_inc(na_ones, 1)

                def normalise(i):
                    t = 4 * k + i
                    dve.wait_ge(na_P, 2 * t + 2)
                    recip = XRI[:, i:i + 1]
                    link(DVE.reciprocal(recip, XRS[:, i:i + 1]))
                    dve.wait_ge(na_Z, t + 1)
                    link(DVE.tensor_scalar(XZ[:, i % 2, :], bank(6, DC), recip, None, ALU.mult))
                    for c, at in ((slice(128, DC), DC), (slice(0, 128), 256)):
                        z = XZ[:, i % 2, c]
                        DVE.scalar_tensor_tensor(z, bank(6, c.stop - c.start, at=at), recip, z, ALU.mult,
                                                 ALU.add).then_inc(na_Zs, 1)

                def ztrans(i):
                    t = 4 * k + i
                    dve.wait_ge(na_ZT, t + 1)
                    c = slice(128 * i, 128 * i + 128)
                    if k == 0:
                        DVE.tensor_copy(NZT1[:, c], bank(7, 128)).then_inc(na_ZTs, 1)
                        DVE.tensor_copy(NZT2[0:D2, c], bank(7, 128, rows=slice(0, D2), at=128)).then_inc(na_ZTs, 1)
                    else:
                        DVE.tensor_scalar(NZT1[:, c], bank(7, 128), C("L3x_g2")[:, 0:1], C("L3x_b2")[:, 0:1],
                                          ALU.mult, ALU.add).then_inc(na_ZTs, 1)
                        DVE.tensor_scalar(NZT2[0:D2, c], bank(7, 128, rows=slice(0, D2), at=128),
                                          C("L3x_g2")[0:D2, 1:2], C("L3x_b2")[0:D2, 1:2],
                                          ALU.mult, ALU.add).then_inc(na_ZTs, 1)

                def spread(i):
                    t = 4 * k + i
                    if i >= 2:
                        dve.wait_ge(na_Z, t - 1)
                    dve.wait_ge(na_T, 2 * t + 2)
                    DVE.tensor_copy(PTL[:, i % 2, :, :], bank(5, 512).bitcast(F16).rearrange("p (a b) -> p a b", b=128)) \
                        .then_inc(na_PTL, 1)

                for i in range(NT):
                    if k == 1 or i >= 2:
                        narrow_max(k, i)
                    if i >= 1:
                        spread(i - 1)
                    if k == 1 or i >= 1:
                        narrow_split(k, i)
                    if i >= 3:
                        ztrans(i - 3)
                    if i >= 2:
                        normalise(i - 2)
                spread(NT - 1)
                ztrans(NT - 3)
                normalise(NT - 2)
                ztrans(NT - 2)
                normalise(NT - 1)
                ztrans(NT - 1)

            def self16(k):
                for h in range(2):
                    for r in (2, 3, 6, 7):
                        dve.wait_ge(sa_q, 8 * k + 4 * h + r // 2 + 1)
                        src = bank(r // 2, 256, at=256 * (r % 2))
                        if k == 0:
                            DVE.tensor_copy(QC[:, r, :], src).then_inc(sa_qs, 1)
                        else:
                            DVE.tensor_scalar(QC[:, r, :], src, C("L1a_bq")[:, r:r + 1], None,
                                              ALU.add).then_inc(sa_qs, 1)
                    if k == 0:
                        dve.wait_ge(sa_k0, h + 1)
                        DVE.tensor_copy(KC[:, 0, :], bank(4, 256)).then_inc(sa_ks0, 1)
                    else:
                        for r in (2, 3, 6, 7):
                            dve.wait_ge(sa_k, 4 * h + r // 2 + 1)
                            DVE.tensor_scalar(KC[:, r, :], bank(4 + r // 2, 256, at=256 * (r % 2)),
                                              C("L1a_bk")[:, r:r + 1], None, ALU.add).then_inc(sa_ks, 1)
                    if h == 0:
                        link(DVE.memset(VB, 0.0))
                    dve.wait_ge(sa_v, 2 * k + h + 1)
                    for b in range(4):
                        for e in range(2):
                            R = half(e)
                            if k == 0:
                                src = bank(6, 4, 16, rows=R)[:, b:b + 1, :].to_broadcast([64, 8, 16])
                            else:
                                n = VALUES_AT[e][b]
                                src = bank(6 + n // 2, 2, 8, 32, rows=R)[:, n % 2, :, 16 * e:16 * e + 16]
                            ins = DVE.tensor_copy(VB[R, b, :, 16 * e:16 * e + 16], src)
                    ins.then_inc(sa_vs, 1)

                    def soft(u):
                        t = 8 * k + 4 * h + u
                        p = u % 2
                        sc = SC[:, p, :].rearrange("p (a b) -> p a b", b=64)
                        raw = ps[:, p, :].rearrange("p (a b) -> p a b", b=64)
                        mx = AMX[:, p, :]
                        dve.wait_ge(sa_S, t + 1)
                        if u >= 2:
                            dve.wait_ge(sa_T, t - 1)
                        if k == 0:
                            link(DVE.tensor_tensor(sc, raw, C("causal").unsqueeze(1).to_broadcast([128, 8, 64]), ALU.add))
                            raw = sc
                        link(DVE.tensor_reduce(mx, raw, X, ALU.max))
                        DVE.tensor_tensor(sc, raw, mx.unsqueeze(2).to_broadcast([128, 8, 64]), ALU.subtract) \
                            .then_inc(sa_d, 1)

                    def norm(u):
                        t = 8 * k + 4 * h + u
                        p = u % 2
                        sc = SC[:, p, :].rearrange("p (a b) -> p a b", b=64)
                        dve.wait_ge(sa_exp, t + 1)
                        link(DVE.tensor_reduce(ASM[:, p, :], sc, X, ALU.add))
                        link(DVE.reciprocal(ARC[:, p, :], ASM[:, p, :]))
                        DVE.tensor_tensor(sc, sc, ARC[:, p, :].unsqueeze(2).to_broadcast([128, 8, 64]), ALU.mult) \
                            .then_inc(sa_P, 1)

                    soft(0)
                    for u in range(1, 4):
                        norm(u - 1)
                        soft(u)
                    norm(3)
                    dve.wait_ge(sa_y, 2 * k + h + 1)
                    DVE.tensor_copy(YT[:, 1, 256 * h:256 * h + 256], ps[:, 5, 256 * h:256 * h + 256]) \
                        .then_inc(sa_ys, 1)

            def self1(k):
                dve.wait_ge(s1_k, 1 + k)
                DVE.tensor_copy(SK, bank(4, 2, TOK)).then_inc(s1_qks, 1)
                dve.wait_ge(s1_v, 1 + k)
                DVE.tensor_copy(SV[:, 2:4, :], bank(7, 2, D)).then_inc(s1_vs, 1)
                dve.wait_ge(s1_S, 1 + k)
                mask = C("bcausal" if k == 0 else "bfull").unsqueeze(1).to_broadcast([128, NT, 128])
                link(DVE.tensor_tensor(SS, bank(0, NT, 128), mask, ALU.add))
                link(DVE.tensor_reduce(SMX, SS, X, ALU.max))
                DVE.tensor_tensor(SS, SS, SMX.unsqueeze(2).to_broadcast([128, NT, 128]), ALU.subtract) \
                    .then_inc(s1_d, 1)
                dve.wait_ge(s1_exp, 1 + k)
                link(DVE.tensor_reduce(SSM, SS, X, ALU.add))
                link(DVE.reciprocal(SRC, SSM))
                DVE.tensor_tensor(SS, SS, SRC.unsqueeze(2).to_broadcast([128, NT, 128]), ALU.mult) \
                    .then_inc(s1_P, 1)
                dve.wait_ge(s1_o, 1 + k)
                DVE.tensor_copy(SO[:, 1, :], ps[:, 3, :]).then_inc(s1_os, 1)

            def ranks(k):
                for i in range(NT):
                    if i >= 1:
                        dve.wait_ge(rk_spread, 4 * k + i)
                    DVE.tensor_tensor(RDL, RP[:, i, :].unsqueeze(2).to_broadcast([128, 8, 64]),
                                      C("delta").unsqueeze(1).to_broadcast([128, 8, 64]), ALU.mult) \
                        .then_inc(rk_diag, 1)
                DVE.tensor_copy(RBEF, C("before"))
                for i in range(NT):
                    dve.wait_ge(rk_spread, 4 * k + i + 1)
                    other = bank(2 + i, 8, 64)
                    mine = RP[:, i, :].unsqueeze(2).to_broadcast([128, 8, 64])
                    DVE.tensor_tensor(RG, other, mine, ALU.is_gt)
                    link(DVE.tensor_tensor(RE, other, mine, ALU.is_equal))
                    link(DVE.tensor_tensor(RE, RE, RBEF.unsqueeze(1).to_broadcast([128, 8, 64]), ALU.mult))
                    link(DVE.tensor_tensor(RG, RG, RE, ALU.add))
                    link(DVE.tensor_reduce(RK[:, i, :], RG, X, ALU.add))

            def first_hot(out, p, mx, tmp, vmx, rev, n):
                bc = lambda a: a.unsqueeze(2).to_broadcast([128, NT, n])
                link(DVE.tensor_reduce(mx, p, X, ALU.max))
                link(DVE.tensor_tensor(tmp, p, bc(mx), ALU.is_equal))
                link(DVE.tensor_tensor(tmp, tmp, C(rev).unsqueeze(1).to_broadcast([128, NT, n]), ALU.mult))
                link(DVE.tensor_reduce(vmx, tmp, X, ALU.max))
                link(DVE.tensor_tensor(out, tmp, bc(vmx), ALU.is_equal))

            layernorm(0)
            for g in range(NGROUP):
                if 0 <= g - AT_Q - 2 < 2:
                    narrow_queries(0, [g - AT_Q - 2])
                if 0 <= g - AT_A - 2 < 3:
                    narrow_low(0, [g - AT_A - 2])
                if g == AT_S + 5:
                    narrow_max(0, 0)
                split_low(0, g)
                if g >= 2:
                    spread_low(0, g - 2)
            spread_low(0, NGROUP - 2)
            spread_low(0, NGROUP - 1)
            narrow_split(0, 0)
            narrow_max(0, 1)
            narrow(0)
            add_x(0, (0, 1, 2, 3))
            layernorm(1)
            self16(0)
            add_x(1, (0, 1, 2, 3))
            layernorm(2)
            bc8 = lambda a: a.unsqueeze(2).to_broadcast([128, NT, 8])
            dve.wait_ge(router_logits, 1)
            link(DVE.tensor_reduce(RA, bank(2, NT, 8), X, ALU.max))
            DVE.tensor_tensor(RP, bank(2, NT, 8), bc8(RA), ALU.subtract).then_inc(router_d, 1)
            dve.wait_ge(router_exp, 1)
            link(DVE.tensor_reduce(RA, RP, X, ALU.add))
            link(DVE.reciprocal(RB_, RA))
            link(DVE.tensor_tensor(RP, RP, bc8(RB_), ALU.mult))
            ranks(0)
            for i in range(NT):
                ins = DVE.tensor_tensor(SEL[:, i], RK[:, i, :].unsqueeze(2).to_broadcast([128, 8, 32]),
                                        C("slot32").unsqueeze(1).to_broadcast([128, 8, 32]), ALU.is_equal)
            chain[0] += 1
            ins.then_inc(dve_step, 1)
            dve.wait_ge(dve_step, chain[0])
            for i in range(NT):
                ins = DVE.tensor_tensor(SELG[:, :, i], SEL[:, i], RP[:, i, :].unsqueeze(2).to_broadcast([128, 8, 32]),
                                        ALU.mult)
            ins.then_inc(L0f_sel, 1)
            for i in range(1, NT, 2):
                dve.wait_ge(gathered, i + 1)
                DVE.tensor_copy(XIN[:, :, :, i, :], bank(i, 2, 8, 32)).then_inc(xin_copied, 1)
            dve.wait_ge(comb_Ts, 1)
            DVE.tensor_tensor(SGTL, bank(6, 8, 128), SGTH, ALU.subtract).then_inc(comb_Ts, 1)
            for e in range(8):
                dve.wait_ge(L0f_y, e + 1)
                link(DVE.tensor_copy(YH[:, e, :], bank(6 + e % 2, D)))
                DVE.tensor_tensor(YL[:, e, :], bank(6 + e % 2, D), YH[:, e, :], ALU.subtract).then_inc(L0f_ys, 1)
            rb = wv(5184, D).bitcast(BF16)
            for i in range(NT):
                dve.wait_ge(layer_out, 4 * 2 + i + 1)
                o = rb[:, 256 * (i % 2):256 * (i % 2) + 256]
                link(DVE.tensor_copy(o, ps[:, i, 0:D]))
                ins = DVE.tensor_tensor(x[:, i, :], x[:, i, :], o, ALU.add)
                link(ins)
                ins = DVE.bn_stats(st6[:, i, :], x[:, i, :])
                if i == NT - 1:
                    link(ins)
            layernorm(3)
            wide(0)
            add_x(3, (0, 1, 2, 3))
            layernorm(4)
            self16(1)
            add_x(4, (0, 1, 2, 3))
            layernorm(5)
            bc16 = lambda a: a.unsqueeze(2).to_broadcast([128, NT, 16])
            dve.wait_ge(router_logits, 2)
            link(DVE.tensor_reduce(TM1, bank(2, NT, 16), X, ALU.max))
            DVE.tensor_tensor(TP, bank(2, NT, 16), bc16(TM1), ALU.subtract).then_inc(router_d, 1)
            dve.wait_ge(router_exp, 2)
            link(DVE.tensor_reduce(TM1, TP, X, ALU.add))
            link(DVE.reciprocal(TM2, TM1))
            link(DVE.tensor_tensor(TP, TP, bc16(TM2), ALU.mult))
            first_hot(TOH1, TP, TM1, TT, TV, "rev16", 16)
            link(DVE.scalar_tensor_tensor(TP, TOH1, -2.0, TP, ALU.mult, ALU.add))
            first_hot(TOH2, TP, TM2, TT, TV, "rev16", 16)
            DVE.tensor_copy(TU, TOH1).then_inc(L1f_hot, 1)
            dve.wait_ge(L1f_cum, 1)
            DVE.tensor_tensor(TQ1, bank(3, NT, 16), TOH1, ALU.mult)
            link(DVE.tensor_tensor(TQ2, bank(3, NT, 16, at=64), TOH2, ALU.mult))
            bs = lambda a, i: a[:, i, :].unsqueeze(2).to_broadcast([128, 16, 16])
            slots = C("slot16").unsqueeze(1).to_broadcast([128, 16, 16])
            for i in range(NT):
                DVE.tensor_tensor(TD[:, i], bs(TQ1, i), slots, ALU.is_equal)
                ins = DVE.tensor_tensor(TX_[:, i], bs(TQ2, i), slots, ALU.is_equal)
            link(ins)
            for i in range(NT):
                ins = DVE.tensor_tensor(TD[:, i], TD[:, i], TX_[:, i], ALU.add)
            ins.then_inc(L1f_disp, 1)
            DVE.tensor_scalar(TQ1, TQ1, 8.0, None, ALU.min)
            link(DVE.tensor_scalar(TQ2, TQ2, 8.0, None, ALU.min))
            dve.wait_ge(L1f_disp, 1)
            for i in range(NT):
                DVE.tensor_tensor(TC[:, i], bs(TQ1, i), slots, ALU.is_equal)
                ins = DVE.tensor_tensor(TX_[:, i], bs(TQ2, i), slots, ALU.is_equal)
            link(ins)
            for i in range(NT):
                ins = DVE.tensor_scalar(TC[:, i], TC[:, i], TM1[:, i:i + 1], None, ALU.mult)
            link(ins)
            for i in range(NT):
                ins = DVE.scalar_tensor_tensor(TC[:, i], TX_[:, i], TM2[:, i:i + 1], TC[:, i], ALU.mult, ALU.add)
            ins.then_inc(L1f_comb, 1)
            for i in range(1, NT, 2):
                dve.wait_ge(gathered, i + 5)
                DVE.tensor_copy(TXIN[:, :, :, i, :], bank(i, 2, 16, 16)).then_inc(xin_copied, 1)
            for g in range(2):
                dve.wait_ge(L1f_silu, g + 1)
                dve.wait_ge(L1f_up, g + 1)
                DVE.tensor_tensor(THT[:, 8 * g:8 * g + 8, :], TSG[:, g, :].rearrange("p (a b) -> p a b", b=64),
                                  bank(2 * g + 1, 8, 64), ALU.mult).then_inc(L1f_hs, 1)
            dve.wait_ge(L1f_o, 1)
            for c in range(2):
                DVE.tensor_copy(TOT[:, c, :, 8:16, :].rearrange("p i e s -> p e i s"),
                                bank(4 + 2 * c + 1, 8, NT, 16)).then_inc(L1f_os, 1)
            for i in range(1, NT, 2):
                dve.wait_ge(L1f_oT, i + 1)
                DVE.tensor_copy(TON[:, i, :, :], bank(i, 2, D)).then_inc(L1f_ons, 1)
            add_x(5, (4, 5, 6, 7))
            layernorm(6)
            wide(1)
            add_x(6, (0, 1, 2, 3))
            layernorm(7)
            self1(0)
            add_x(7, (4, 5, 6, 7))
            layernorm(8)
            bc8 = lambda a: a.unsqueeze(2).to_broadcast([128, NT, 8])
            sq = wv(5184, D)
            for i in range(NT):
                link(DVE.tensor_tensor(sq, xn[:, i, :], xn[:, i, :], ALU.mult))
                link(DVE.tensor_reduce(RA[:, i:i + 1], sq, X, ALU.add))
            wf2 = wv(5696, 16)
            DVE.tensor_tensor(wf2, C("L2f_waff"), C("L2f_waff"), ALU.mult).then_inc(L2f_sums, 1)
            dve.wait_ge(L2f_summed, 1)
            DVE.tensor_copy(RS1, bank(3, 8)).then_inc(L2f_norms2, 2)
            dve.wait_ge(L2f_norms, 2)
            for i in range(NT):
                ins = DVE.tensor_scalar(RT[:, i, :], RS1, RA[:, i:i + 1], 1e-9, ALU.mult, ALU.add)
            link(ins)
            link(DVE.reciprocal(RL, RT))
            dve.wait_ge(router_logits, 3)
            link(DVE.tensor_tensor(RP, bank(2, NT, 8), RL, ALU.mult))
            link(DVE.tensor_reduce(RB_[:, 0:1], RP, mybir.AxisListType.XY, ALU.add))
            link(DVE.tensor_copy(RB_[:, 1:2], RB_[:, 0:1]))
            DVE.tensor_copy(RB_[:, 2:3], RB_[:, 0:1]).then_inc(L2f_sums, 1)
            link(DVE.tensor_reduce(RA, RP, X, ALU.max))
            DVE.tensor_tensor(RL, RP, bc8(RA), ALU.subtract).then_inc(router_d, 1)
            dve.wait_ge(L2f_summed, 2)
            DVE.tensor_scalar(RC_[:, 0:1], bank(3, 1, at=8), 1.0 / (TOK * 8), C("L2f_thr"), ALU.mult,
                              ALU.subtract).then_inc(L2f_mean, 1)
            dve.wait_ge(router_exp, 3)
            link(DVE.tensor_reduce(RA, RL, X, ALU.add))
            link(DVE.reciprocal(RB_, RA))
            link(DVE.tensor_tensor(RL, RL, bc8(RB_), ALU.mult))
            first_hot(ROH, RL, RA, RT, RB_, "rev8", 8)
            dve.wait_ge(L2f_sig, 1)
            link(DVE.tensor_scalar(RC_[:, 2:3], RC_[:, 1:2], 1.0, None, ALU.add))
            link(DVE.reciprocal(RC_[:, 3:4], RC_[:, 2:3]))
            link(DVE.tensor_scalar(RC_[:, 2:3], RC_[:, 3:4], float(CAP), 4.0, ALU.mult, ALU.max))
            ranks(1)
            link(DVE.tensor_scalar(RK, RK, 1.0, RC_[:, 2:3], ALU.add, ALU.is_le))
            link(DVE.tensor_tensor(ROH, ROH, RK, ALU.mult))

            def pick(e):
                if e >= 2:
                    dve.wait_ge(L2f_xi, e - 1)
                DVE.tensor_tensor(EDG[:, e % 2], ident.unsqueeze(1).to_broadcast([128, NT, 128]),
                                  ROH[:, :, e:e + 1].to_broadcast([128, NT, 128]), ALU.mult) \
                    .then_inc(L2f_diag, 1)

            def copy_inputs(e):
                for c in range(2):
                    dve.wait_ge(L2f_xih, 2 * e + c + 1)
                    h = 2 * (e % 2) + c
                    DVE.tensor_tensor(EXL[:, h, :], ps[:, 6 + c, :], EXH[:, h, :], ALU.subtract).then_inc(L2f_xil, 1)

            pick(0)
            copy_inputs(0)
            for n in range(64):
                e, f = n // 8, n % 8
                if f == 0:
                    if e > 0:
                        spread_low(1, 2 * e - 2)
                    if e < 7:
                        pick(e + 1)
                    context_stats(2 * e)
                if f == 1:
                    context_norm(2 * e)
                if f == 2:
                    context_stats(2 * e + 1)
                if f == 3 and e < 7:
                    copy_inputs(e + 1)
                if f == 4:
                    if e > 0:
                        spread_low(1, 2 * e - 1)
                    context_norm(2 * e + 1)
                if f == 5:
                    split_low(1, 2 * e)
                if f == 7:
                    split_low(1, 2 * e + 1)
                dve.wait_ge(L2f_hs, 2 * n + 2)
                if n >= 4:
                    dve.wait_ge(L2f_y, n - 3)
                DVE.tensor_tensor(EHL[:, n % 4, :], EG[:, n % 4, :], EHH[:, n % 4, :], ALU.subtract) \
                    .then_inc(L2f_hl, 1)
            spread_low(1, NGROUP - 2)
            spread_low(1, NGROUP - 1)
            dve.wait_ge(layer_out, 4 * 8 + 4)
            for i in range(NT):
                ins = DVE.tensor_tensor(x[:, i, :], x[:, i, :], bank(i // 2, D, at=D * (i % 2)), ALU.add)
            link(ins)
            for i in range(NT):
                ins = DVE.bn_stats(st6[:, i, :], x[:, i, :])
            link(ins)
            layernorm(9)
            layernorm("9b", affine=("L3x_g1", "L3x_b1"))
            link(DVE.memset(NKB, 0.0))
            dve.wait_ge(na_kb, 1)
            for c in range(2):
                DVE.tensor_scalar(NKB[:, c, 0:1], ps[:, 7, c:c + 1], C("L3x_bk")[:, c:c + 1], None, ALU.add)
                DVE.tensor_scalar(NKB[:, c, 32:33], ps[:, 7, c:c + 1], C("L3x_bk")[:, c:c + 1], None,
                                  ALU.add).then_inc(na_kbs, 1)
            narrow_queries(1)
            narrow_low(1)
            narrow(1)
            dve.wait_ge(na_v, 2)
            DVE.tensor_copy(NV[:, 1, :], ps[:, 1, :]).then_inc(na_vs, 1)
            add_x(9, (2, 3, 4, 5))
            layernorm(10)
            self1(1)
            add_x(10, (4, 5, 6, 7))
            layernorm(11)
            dve.wait_ge(L3f_s, 1)
            DVE.tensor_scalar(FS, ps[:, 2, 0:256], C("L3f_bin"), None, ALU.add).then_inc(L3f_ss, 1)
            for h in range(16):
                dve.wait_ge(L3f_relu, h + 1)
                if h == 0:
                    ins = DVE.tensor_scalar(FG_, FT[:, 0, :], C("L3f_W2")[:, 0:1], C("L3f_b2"), ALU.mult, ALU.add)
                else:
                    ins = DVE.scalar_tensor_tensor(FG_, FT[:, h % 4, :], C("L3f_W2")[:, h:h + 1], FG_,
                                                   ALU.mult, ALU.add)
                ins.then_inc(L3f_acc, 1)
                dve.wait_ge(L3f_acc, h + 1)
            add_x(11, (3, 4, 5, 6))

        @block.tensor
        def _(pe):

            def loaded(name):
                n = UIDX[name]
                pe.wait_ge(slot_loaded[n % NSLOT], load_value(name))

            pe.wait_ge(consts_loaded, 16)

            def layernorm(key):
                for i in range(NT):
                    pe.wait_ge(ln_xn, 4 * LN[key] + i + 1)
                    for c in range(2):
                        ins = PE.transpose(ps[:, c, 128 * i:128 * i + 128], xn[:, i, 128 * c:128 * c + 128], ident)
                ins.then_inc(ln_T, 1)
                pe.wait_ge(ln_xnT, 2 * LNT[key] + 2)

            tile = lambda i: slice(128 * i, 128 * i + 128)

            def project_out(l, banks, lhs, rhs, n, bias=None, ones=slice(0, 1), used=1):
                for i in range(NT):
                    o = ps[:, banks[i], 0:D]
                    if bias is not None:
                        mm(o, C("ones", ones), bias, True, False)
                    for c in range(n):
                        ins = mm(o, lhs(c, i), rhs(c), start=(c == 0 and bias is None), stop=(c == n - 1))
                    ins.then_inc(layer_out, 1)
                    if i == NT - 1 and used:
                        pe.wait_ge(layer_out, 4 * l + 4)
                        pe.sem_inc(units_used, used)

            def release(n):
                pe.sem_inc(units_used, n)

            def transpose_context(p, g):
                pe.wait_ge(cx_lo, NGROUP * p + g + 1)
                b0 = ctx_banks(p, g)
                before = 2 if p == 0 else 1
                if p == 1 or g >= before:
                    pe.wait_ge(cx_Ts_act, NGROUP * p + g + 1 - before)
                    pe.wait_ge(cx_Ts_dve, NGROUP * p + g + 1 - before)
                for m in range(GROUP):
                    for c, at in ((0, 0), (1, 128), (2, 256)):
                        o = bank(b0 + c // 2, 512).bitcast(F16)[:, 512 * (c % 2) + 128 * m:512 * (c % 2) + 128 * m + 128]
                        ins = PE.transpose(o, CN[:, GROUP * g + m, at:at + 128], ident16[:, :])
                ins.then_inc(cx_T, 1)

            def wide(k):
                L = "L1x" if k == 0 else "L2x"
                l = 3 if k == 0 else 6
                loaded(f"{L}_q")
                wq = unit(f"{L}_q", 0, 2, 1024)
                for r in range(NPAIR):
                    for c in range(2):
                        ins = mm(ps[:, r, :], wq[:, c, 128 * r:128 * r + 128], xnT[:, c, :], c == 0, c == 1)
                    ins.then_inc(xa_q, 1)
                pe.wait_ge(xa_q, 8 * k + 8)
                release(1)
                pe.wait_ge(xa_qs, 8 * k + 8)
                loaded(f"{L}_k")
                loaded(f"{L}_v")
                wkt = unit(f"{L}_k", 0, NPAIR, 256)
                wvv = unit(f"{L}_v", 0, 2, 1024)

                def queries(t, r, first):
                    pe.wait_ge(xa_B, t + 1)
                    if not first:
                        pe.wait_ge(xa_OT, t - 4)
                    for c in range(2):
                        ins = mm(bank(7, 128, at=128 * c), wkt[:, r, 128 * c:128 * c + 128], XB[:, r % 2, :])
                    ins.then_inc(xa_A, 1)

                def scores(b, t, r, first):
                    pe.wait_ge(xa_AL, t + 1)
                    if not first:
                        pe.wait_ge(xa_P, 2 * t - 2)
                    ah, al = XAH[:, r % 2, :], XAL[:, r % 2, :]
                    for n in range(2):
                        o = ps[:, 2 * (r % 2) + n, :]
                        kk = bass.ds(b * LK + 512 * n, 512)
                        mm(o, ah[:, 0:128], CT[:, 0, kk], True, False)
                        mm(o, ah[:, 0:128], CT[:, 2, kk], False, False)
                        mm(o, al[:, 0:128], CT[:, 0, kk], False, False)
                        mm(o, ah[:, 128:256], CT[:, 1, kk], False, False)
                        ins = mm(o, al[:, 128:256], CT[:, 1, kk], False, True)
                    ins.then_inc(xa_S, 1)

                def transposes(t, r, first):
                    pe.wait_ge(xa_PL, t + 1)
                    for g, src, copied in ((0, PH, xa_PTH), (1, PL, xa_PTL)):
                        if not first:
                            pe.wait_ge(copied, t)
                        for n in range(KT):
                            m = slice(128 * n, 128 * n + 128)
                            ins = PE.transpose(bank(4 + g, 512).bitcast(F16)[:, m], src[:, r % 2, m], ident16[:, :])
                        ins.then_inc(xa_T, 1)

                def attend(b, t, r, first):
                    pe.wait_ge(xa_PTH, t + 1)
                    pe.wait_ge(xa_PTL, t + 1)
                    if not first:
                        pe.wait_ge(xa_ZTs, 2 * t)
                    for n in range(KT):
                        part = lambda a, z: CN[:, bass.ds(b * KT + n, 1), a:z].rearrange("p a d -> p (a d)")
                        mm(bank(6, 2 * DC), PTH[:, r % 2, n, :], part(0, 2 * DC), n == 0, False)
                        ins = mm(bank(6, DC), PTL[:, r % 2, n, :], part(0, DC), False, n == KT - 1)
                    ins.then_inc(xa_Z, 1)

                def ztrans(t, r):
                    pe.wait_ge(xa_Zs, 2 * t + 2)
                    PE.transpose(bank(6, 128), XZ[:, r % 2, 0:128], ident)
                    PE.transpose(bank(6, 128, rows=slice(0, D2), at=128), XZ[:, r % 2, 128:DC], ident) \
                        .then_inc(xa_ZT, 1)

                def heads(t, r, before, first=False):
                    pe.wait_ge(xa_ZTs, 2 * t + 2)
                    if not first:
                        pe.wait_ge(xa_OT, t)
                    pe.wait_ge(xa_AL, before + 1)
                    for e in range(2):
                        o = bank(7, 64, rows=half(e), at=256)
                        h = 2 * r + e
                        c = slice(64 * e, 64 * e + 64)
                        mm(o, wvv[:, 0, 64 * h:64 * h + 64], XZT[:, r % 2, 64 * e:64 * e + 64], True, False)
                        ins = mm(o, wvv[0:D2, 1, 64 * h:64 * h + 64], XZT[0:D2, r % 2, 128 + 64 * e:192 + 64 * e],
                                 False, True)
                    ins.then_inc(xa_O, 1)

                def batch(b, first, last):
                    t0 = 64 * k + 8 * b if isinstance(b, int) else b * 8 + 64 * k
                    for r in range(NPAIR):
                        t = t0 + r
                        end = last and r == NPAIR - 1
                        scores(b, t, r, first and r < 2)
                        if not (first and r < 3):
                            ztrans(t - 3, (r - 3) % NPAIR)
                        if not end:
                            queries(t + 1, (r + 1) % NPAIR, first and r < 4)
                        if not (first and r < 1):
                            transposes(t - 1, (r - 1) % NPAIR, first and r == 1)
                        if not (first and r < 2):
                            attend(b if r >= 2 else b - 1, t - 2, (r - 2) % NPAIR, first and r == 2)
                        if not (first and r < 3):
                            heads(t - 3, (r - 3) % NPAIR, t if end else t + 1, first and r == 3)

                queries(64 * k, 0, True)
                batch(0, True, False)
                with pe.Fori(1, B - 1) as b:
                    batch(b, False, False)
                batch(B - 1, False, True)
                t1 = 64 * (k + 1)
                ztrans(t1 - 3, 5)
                transposes(t1 - 1, 7, False)
                attend(B - 1, t1 - 2, 6, False)
                heads(t1 - 3, 5, t1 - 1)
                ztrans(t1 - 2, 6)
                attend(B - 1, t1 - 1, 7, False)
                heads(t1 - 2, 6, t1 - 1)
                ztrans(t1 - 1, 7)
                heads(t1 - 1, 7, t1 - 1)
                loaded(f"{L}_o")
                pe.wait_ge(xa_OT, t1)
                wo = unit(f"{L}_o", 0, 8, D)
                project_out(l, (0, 1, 2, 3), lambda c, i: XQ[:, c, tile(i)], lambda c: wo[:, c, :], 8,
                            bias=wvv[D2:D2 + 1, 1, 0:D],
                            ones=slice(D2, D2 + 1), used=3)

            def narrow_queries(k, parts=range(2)):
                ua = "L0x_a" if k == 0 else "L3x_a"
                wq = unit(ua, 0, 2, D)
                loaded(ua)
                for c in parts:
                    for d in range(2):
                        ins = mm(ps[:, 2 + c, :], wq[:, d, 128 * c:128 * c + 128], xnT[:, d, :], d == 0, d == 1)
                    ins.then_inc(na_q, 1)

            def narrow_keys(k, parts=range(3)):
                ua = "L0x_a" if k == 0 else "L3x_a"
                wkt = unit(ua, 512, 2, 256)
                kb = unit(ua, 1024, 2, 33) if k == 0 else NKB
                pe.wait_ge(na_qs, 2 * k + 2)
                for a in parts:
                    if a == 2 and k == 1:
                        pe.wait_ge(na_kbs, 2)
                    for c in range(2):
                        if a < 2:
                            ins = mm(ps[:, a, :], wkt[:, c, 128 * a:128 * a + 128], NQ[:, c, :], c == 0, c == 1)
                        else:
                            ins = mm(bank(2, TOK, rows=slice(0, 33)), kb[:, c, :], NQ[:, c, :], c == 0, c == 1)
                    ins.then_inc(na_A, 1)

            def narrow_scores(k, i, parts=range(4)):
                pe.wait_ge(na_AL, 3 * k + 3)
                t = 4 * k + i
                if i >= 2:
                    pe.wait_ge(na_P, 2 * t - 2)
                for part in parts:
                    par, n = part // 2, part % 2
                    b = 2 * i + par
                    q = slice(64 * b, 64 * b + 64)
                    o = ps[half(par), 2 * (i % 2) + n, :]
                    kk = slice(b * LK + 512 * n, b * LK + 512 * n + 512)
                    mm(o, NCR[:, q], ONES16, True, False)
                    mm(o, NAH[:, 0, q], CT[:, 0, kk], False, False)
                    mm(o, NAH[:, 0, q], CT[:, 2, kk], False, False)
                    mm(o, NAL[:, 0, q], CT[:, 0, kk], False, False)
                    mm(o, NAH[:, 1, q], CT[:, 1, kk], False, False)
                    ins = mm(o, NAL[:, 1, q], CT[:, 1, kk], False, True)
                    if part == 3:
                        ins.then_inc(na_S, 1)

            def narrow(k):
                ub = "L0x_b" if k == 0 else "L3x_b"
                wvv = unit(ub, 0, 2, D)
                R = slice(0, D2 + 1)

                def transposes(i):
                    t = 4 * k + i
                    pe.wait_ge(na_PL, t + 1)
                    for g, src, copied in ((0, PH, na_PTH), (1, PL, na_PTL)):
                        if i >= 1:
                            pe.wait_ge(copied, t)
                        for n in range(KT):
                            m = slice(128 * n, 128 * n + 128)
                            ins = PE.transpose(bank(4 + g, 512).bitcast(F16)[:, m], src[:, i % 2, m], ident16[:, :])
                        ins.then_inc(na_T, 1)

                def attend(i):
                    t = 4 * k + i
                    pe.wait_ge(na_PTH, t + 1)
                    pe.wait_ge(na_PTL, t + 1)
                    if i >= 1:
                        pe.wait_ge(na_Zs, 2 * t)
                    for par in range(2):
                        o = bank(6, 2 * DC, rows=half(par))
                        for n in range(KT):
                            kt = (2 * i + par) * KT + n
                            ph, pl = (a[:, i % 2, n, 64 * par:64 * par + 64] for a in (PTH, PTL))
                            mm(o, ph, CN[:, kt, :], n == 0, False)
                            ins = mm(o[:, 0:DC], pl, CN[:, kt, 0:DC], False, n == KT - 1)
                    ins.then_inc(na_Z, 1)

                def ztrans(i):
                    t = 4 * k + i
                    pe.wait_ge(na_Zs, 2 * t + 2)
                    if i >= 1:
                        pe.wait_ge(na_ZTs, 2 * t)
                    PE.transpose(bank(7, 128), XZ[:, i % 2, 0:128], ident)
                    PE.transpose(bank(7, 128, rows=slice(0, D2), at=128), XZ[:, i % 2, 128:DC], ident) \
                        .then_inc(na_ZT, 1)

                for i in range(NT + 2):
                    if i < NT and (k == 1 or i >= 2):
                        narrow_scores(k, i)
                    if 1 <= i <= NT:
                        transposes(i - 1)
                    if i >= 3:
                        ztrans(i - 3)
                    if i >= 2:
                        attend(i - 2)
                ztrans(NT - 1)
                pe.wait_ge(na_ZTs, 8 * k + 8)
                pe.wait_ge(na_ones, k + 1)
                loaded(ub)
                if k == 0:
                    project_out(0, (0, 1, 2, 3), lambda c, i: NZT1[:, tile(i)] if c == 0 else NZT2[R, tile(i)],
                                lambda c: wvv[:, 0, :] if c == 0 else wvv[R, 1, :], 2, used=2)
                else:
                    for c in range(2):
                        o = ps[:, c, :]
                        mm(o, wvv[:, 0, 128 * c:128 * c + 128], NZT1, True, False)
                        mm(o, wvv[R, 1, 128 * c:128 * c + 128], NZT2[R], False, True).then_inc(na_v, 1)
                    pe.wait_ge(na_vs, 2)
                    wo = unit(ub, 512, 2, D)
                    project_out(9, (2, 3, 4, 5), lambda c, i: NV[:, c, tile(i)], lambda c: wo[:, c, :], 2,
                                bias=unit(ub, 1024, D, rows=slice(0, 1)), used=2)

            def self16(k):
                l = 1 if k == 0 else 4
                for h in range(2):
                    tok = slice(256 * h, 256 * h + 256)
                    if h == 1:
                        pe.wait_ge(sa_d, 8 * k + 4)
                        pe.wait_ge(sa_PT, 8 * k + 4)
                        pe.wait_ge(sa_ys, 4 * k + 2)
                        pe.wait_ge(sa_vs, 2 * k + 1)
                    if k == 0:
                        wq = unit("L0a_a", 256, 1024)
                        wkk = unit("L0a_a", 1280, 128)
                        wvv = unit("L0a_a", 1408, 16)
                        for r in range(8):
                            ins = mm(bank(r // 2, 256, at=256 * (r % 2)), wq[:, 128 * r:128 * r + 128], LAT[:, tok])
                            if r % 2:
                                ins.then_inc(sa_q, 1)
                        mm(bank(4, 256), wkk, LAT[:, tok]).then_inc(sa_k0, 1)
                    else:
                        wq, wkk = unit("L1a_q", 0, 2, 1024), unit("L1a_k", 0, 2, 1024)
                        wvv = unit("L1a_v", 0, 2, D)
                        for done, ww, b0 in ((sa_q, wq, 0), (sa_k, wkk, 4)):
                            for r in range(8):
                                for c in range(2):
                                    ins = mm(bank(b0 + r // 2, 256, at=256 * (r % 2)), ww[:, c, 128 * r:128 * r + 128],
                                             xnT[:, c, tok], c == 0, c == 1)
                                if r % 2:
                                    ins.then_inc(done, 1)
                    pe.wait_ge(sa_qs, 16 * k + 8 * h + 8)
                    if k == 0:
                        pe.wait_ge(sa_ks0, h + 1)
                    else:
                        pe.wait_ge(sa_ks, 8 * h + 8)
                    if k == 0:
                        for b in range(4):
                            t = slice(256 * h + 64 * b, 256 * h + 64 * b + 64)
                            for e in range(2):
                                ins = mm(bank(6, 16, rows=half(e), at=16 * b), LAT[:, t], wvv)
                    else:
                        for n, rows, first in VALUES:
                            m = rows.stop - rows.start
                            o = bank(6 + n // 2, D, rows=rows, at=256 * (n % 2))
                            mm(o, C("ones", slice(0, 1))[:, 0:m], unit("L1a_v", 1024, D, rows=slice(0, 1)), True, False)
                            for c in range(2):
                                t = 256 * h + 64 * first
                                ins = mm(o, xnT[:, c, t:t + m], wvv[:, c, :], False, c == 1)
                    ins.then_inc(sa_v, 1)

                    def scores(u):
                        t = 8 * k + 4 * h + u
                        ii, j = u // 2, u % 2
                        if u >= 2:
                            pe.wait_ge(sa_d, t - 1)
                        for par in range(2):
                            c = slice(64 * (2 * ii + par), 64 * (2 * ii + par) + 64)
                            R = slice(64 * j, 64 * j + (16 if k == 0 else 48))
                            for p in range(8):
                                ins = mm(bank(u % 2, 64, rows=half(par), at=64 * p), QC[R, p, c],
                                         KC[R, 0 if k == 0 else p, c])
                        ins.then_inc(sa_S, 1)

                    def attend(u):
                        t = 8 * k + 4 * h + u
                        ii, j = u // 2, u % 2
                        pe.wait_ge(sa_P, t + 1)
                        if u >= 2:
                            pe.wait_ge(sa_PT, t - 1)
                        for m in range(4):
                            ins = PE.transpose(bank(2 + u % 2, 128, at=128 * m), SC[:, u % 2, 128 * m:128 * m + 128],
                                               ident)
                        ins.then_inc(sa_T, 1)
                        pe.wait_ge(sa_PT, t + 1)
                        if u == 0:
                            pe.wait_ge(sa_vs, 2 * k + h + 1)
                        for par in range(2):
                            b = 2 * ii + par
                            for m in range(4):
                                ins = mm(bank(4 + j, 64, rows=slice(32 * m, 32 * m + 32), at=256 * h + 64 * b),
                                         VB[:, b, 4 * j + m, :], PT[:, u % 2, 128 * m + 64 * par:128 * m + 64 * par + 64])
                        if u == 3:
                            ins.then_inc(sa_y, 1)

                    scores(0)
                    for u in range(1, 4):
                        scores(u)
                        attend(u - 1)
                    attend(3)
                pe.wait_ge(sa_ys, 4 * k + 4)
                if k == 0:
                    loaded("L0a_b")
                    wo = unit("L0a_b", 0, 2, D)
                    project_out(1, (0, 1, 2, 3), lambda c, i: YT[:, c, tile(i)], lambda c: wo[:, c, :], 2, used=2)
                else:
                    wo = unit("L1a_v", 512, 2, D)
                    project_out(4, (0, 1, 2, 3), lambda c, i: YT[:, c, tile(i)], lambda c: wo[:, c, :], 2,
                                bias=unit("L1a_v", 1280, D, rows=slice(0, 1)), used=3)

            def self1(k):
                L, l = ("L2a", 7) if k == 0 else ("L3a", 10)
                loaded(L)
                wq, wkk, wvv, wo = (unit(L, 512 * n, 2, D) for n in range(4))
                for done, ww, b0 in ((s1_q, wq, 2), (s1_k, wkk, 4)):
                    for c in range(2):
                        for d in range(2):
                            ins = mm(ps[:, b0 + c, :], ww[:, d, 128 * c:128 * c + 128], xnT[:, d, :], d == 0, d == 1)
                    ins.then_inc(done, 1)
                for i in range(NT):
                    for d in range(2):
                        ins = mm(bank(6 + i // 2, D, at=256 * (i % 2)), xnT[:, d, tile(i)], wvv[:, d, :], d == 0, d == 1)
                ins.then_inc(s1_v, 1)
                pe.wait_ge(s1_qks, 2 * k + 2)
                for i in range(NT):
                    for c in range(2):
                        ins = mm(bank(0, 128, at=128 * i), SQ[:, c, tile(i)], SK[:, c, tile(i)], c == 0, c == 1)
                ins.then_inc(s1_S, 1)
                pe.wait_ge(s1_P, 1 + k)
                for i in range(NT):
                    ins = PE.transpose(bank(1, 128, at=128 * i), SS[:, i, :], ident)
                ins.then_inc(s1_T, 1)
                pe.wait_ge(s1_PT, 1 + k)
                pe.wait_ge(s1_vs, 2 * k + 2)
                for c in range(2):
                    for i in range(NT):
                        ins = mm(ps[:, 2 + c, tile(i)], SV[:, i, 128 * c:128 * c + 128], SPT[:, i, :])
                ins.then_inc(s1_o, 1)
                pe.wait_ge(s1_os, 2 * k + 2)
                project_out(l, (4, 5, 6, 7), lambda c, i: SO[:, c, tile(i)], lambda c: wo[:, c, :], 2, used=1)

            def spread_scores(k):
                for i in range(NT):
                    pe.wait_ge(rk_diag, 4 * k + i + 1)
                    mm(bank(2 + i, 512), C("same"), RDL).then_inc(rk_spread, 1)

            layernorm(0)
            for g in range(NGROUP):
                transpose_context(0, g)
                if 0 <= g - AT_Q < 2:
                    narrow_queries(0, [g - AT_Q])
                if 0 <= g - AT_A < 3:
                    narrow_keys(0, [g - AT_A])
                if 0 <= g - AT_S < 8:
                    i, part = (g - AT_S) // 4, (g - AT_S) % 4
                    pe.wait_ge(cx_Ts_act, 4 * i + 4)
                    pe.wait_ge(cx_Ts_dve, 4 * i + 4)
                    narrow_scores(0, i, [part])
            pe.wait_ge(cx_Ts_act, NGROUP)
            pe.wait_ge(cx_Ts_dve, NGROUP)
            narrow(0)
            layernorm(1)
            loaded("L0a_a")
            wd = unit("L0a_a", 0, 2, 128)
            for c in range(2):
                ins = mm(ps[:, 2, :], wd[:, c, :], xnT[:, c, :], c == 0, c == 1)
            ins.then_inc(sa_lat, 1)
            pe.wait_ge(sa_lats, 1)
            self16(0)
            layernorm(2)
            gate = C("L0f_gate").rearrange("p (c e) -> p c e", c=2)
            for i in range(NT):
                for c in range(2):
                    ins = mm(bank(2, 8, at=8 * i), xnT[:, c, tile(i)], gate[:, c, :], c == 0, c == 1)
            ins.then_inc(router_logits, 1)
            pe.wait_ge(router_d, 1)
            spread_scores(0)
            pe.wait_ge(L0f_sel, 1)
            for i in range(NT):
                for c in range(2):
                    ins = mm(bank(i, 256, at=256 * c), xn[:, i, 128 * c:128 * c + 128], SEL[:, i])
                ins.then_inc(gathered, 1)
            for e in range(8):
                ins = PE.transpose(bank(6, 128, at=128 * e), SELG[:, e], ident)
            ins.then_inc(comb_T, 1)
            pe.wait_ge(xin_copied, 4)
            pe.wait_ge(comb_Ts, 2)

            def up(e):
                loaded(f"L0f_{e}_w1")
                w1 = unit(f"L0f_{e}_w1", 0, 2, 1024)
                for g in range(2):
                    if e >= 1:
                        pe.wait_ge(L0f_hs, 2 * e - 1 + g)
                    for m in range(4):
                        f = 4 * g + m
                        for c in range(2):
                            ins = mm(bank(4 + g, 128, at=128 * m), w1[:, c, 128 * f:128 * f + 128], XIN[:, c, e],
                                     c == 0, c == 1)
                    ins.then_inc(L0f_h, 1)

            def down(e):
                loaded(f"L0f_{e}_w2")
                w2 = unit(f"L0f_{e}_w2", 0, 8, D)
                if e >= 2:
                    pe.wait_ge(L0f_ys, e - 1)
                pe.wait_ge(L0f_hs, 2 * e + 2)
                for f in range(8):
                    ins = mm(bank(6 + e % 2, D), HT0[:, e % 2, f, :], w2[:, f, :], f == 0, f == 7)
                ins.then_inc(L0f_y, 1)
                pe.wait_ge(L0f_y, e + 1)
                release(2)

            up(0)
            for e in range(8):
                if e < 7:
                    up(e + 1)
                down(e)
            pe.wait_ge(L0f_ys, 8)
            for i in range(NT):
                for e in range(8):
                    R = slice(32 * i, 32 * i + 32)
                    for n, (a, y) in enumerate(((SGTH, YH), (SGTH, YL), (SGTL, YH))):
                        ins = PE.matmul(ps[:, i, 0:D], a[R, e, :], y[R, e, :], start=(e == 0 and n == 0),
                                        stop=(e == 7 and n == 2), tile_position=(32 * i, 0))
                ins.then_inc(layer_out, 1)
            layernorm(3)
            wide(0)
            layernorm(4)
            loaded("L1a_q")
            loaded("L1a_k")
            loaded("L1a_v")
            self16(1)
            layernorm(5)
            router = C("L1f_router").rearrange("p (c e) -> p c e", c=2)
            for i in range(NT):
                for c in range(2):
                    ins = mm(bank(2, 16, at=16 * i), xnT[:, c, tile(i)], router[:, c, :], c == 0, c == 1)
            ins.then_inc(router_logits, 1)
            pe.wait_ge(L1f_hot, 1)
            mm(bank(3, 64), C("tri"), TOH1)
            mm(bank(3, 64, at=64), C("tri"), TOH2, True, False)
            mm(bank(3, 64, at=64), C("same"), TU, False, True).then_inc(L1f_cum, 1)
            pe.wait_ge(L1f_disp, 1)
            for i in range(NT):
                for c in range(2):
                    ins = mm(bank(i, 256, at=256 * c), xn[:, i, 128 * c:128 * c + 128], TD[:, i])
                ins.then_inc(gathered, 1)
            pe.wait_ge(L1f_comb, 1)
            for i in range(NT):
                for g in range(2):
                    ins = PE.transpose(bank(4, 128, at=256 * i + 128 * g), TC[:, i, 8 * g:8 * g + 8, :], ident)
            ins.then_inc(comb_T, 1)
            pe.wait_ge(xin_copied, 8)
            for g in range(2):
                for which, done, bk in ((0, L1f_gate, 2 * g), (1, L1f_up, 2 * g + 1)):
                    for m in range(8):
                        e = 8 * g + m
                        u = f"L1f_g{e // 4}"
                        if which == 0 and m % 4 == 0:
                            loaded(u)
                        ww = unit(u, 0, 4, 2, 256)[:, e % 4, :, 128 * which:128 * which + 128]
                        for c in range(2):
                            ins = mm(bank(bk, 64, at=64 * m), ww[:, c, :], TXIN[:, c, e], c == 0, c == 1)
                    ins.then_inc(done, 1)
                pe.wait_ge(L1f_up, g + 1)
                release(2)
            pe.wait_ge(comb_Ts, 3)
            pe.wait_ge(L1f_hs, 2)
            for c in range(2):
                for e in range(16):
                    if c == 0 and e % 8 == 0:
                        loaded(f"L1f_p{e // 8}")
                    wp = unit(f"L1f_p{e // 8}", 0, 8, D)
                    ins = mm(bank(4 + 2 * c, 64, at=64 * e), wp[:, e % 8, 128 * c:128 * c + 128], THT[:, e, :])
            ins.then_inc(L1f_o, 1)
            pe.wait_ge(L1f_o, 1)
            release(2)
            pe.wait_ge(L1f_os, 4)
            for i in range(NT):
                for g in range(2):
                    for c in range(2):
                        ins = PE.transpose(bank(i, 128, at=256 * g + 128 * c), TOT[:, c, i, 8 * g:8 * g + 8, :],
                                           ident)
                ins.then_inc(L1f_oT, 1)
            pe.wait_ge(L1f_ons, 4)
            for i in range(NT):
                for g in range(2):
                    ins = mm(ps[:, 4 + i, 0:D], TCT[:, i, g, :], TON[:, i, g, :], g == 0, g == 1)
                ins.then_inc(layer_out, 1)
            layernorm(6)
            wide(1)
            layernorm(7)
            self1(0)
            layernorm(8)
            waff = C("L2f_waff").rearrange("p (c e) -> p c e", c=2)
            for i in range(NT):
                for c in range(2):
                    ins = mm(bank(2, 8, at=8 * i), xnT[:, c, tile(i)], waff[:, c, :], c == 0, c == 1)
            ins.then_inc(router_logits, 1)
            pe.wait_ge(L2f_sums, 1)
            wf2 = wv(5696, 2, 8)
            for c in range(2):
                ins = mm(bank(3, 8), C("ones"), wf2[:, c, :], c == 0, c == 1)
            ins.then_inc(L2f_summed, 1)
            pe.wait_ge(L2f_sums, 2)
            mm(bank(3, 2, at=8), C("ones"), RB_[:, 0:2]).then_inc(L2f_summed, 1)
            pe.wait_ge(L2f_mean, 1)
            spread_scores(1)
            loaded("L2f_b2")
            b2 = unit("L2f_b2", 0, 2 * D, rows=slice(0, 8))

            def gather(e):
                pe.wait_ge(L2f_diag, e + 1)
                if e >= 1:
                    pe.wait_ge(L2f_xil, 2 * e)
                for c in range(2):
                    for i in range(NT):
                        for part in (XNH, XNL):
                            ins = mm(ps[:, 6 + c, tile(i)], part[:, i, 128 * c:128 * c + 128], EDG[:, e % 2, i, :],
                                     part is XNH, part is XNL)
                ins.then_inc(L2f_xi, 1)

            def up(n):
                e, f = n // 8, n % 8
                wh1, wl1 = (unit16(f"L2f_{e}_s1", at, 2, 1024) for at in (0, SLOT))
                if f == 0:
                    pe.wait_ge(L2f_wl, 2 * e + 1)
                    pe.wait_ge(L2f_xil, 2 * e + 2)
                if n >= 2:
                    pe.wait_ge(L2f_hs, 2 * n - 2)
                c128 = slice(128 * f, 128 * f + 128)
                for c in range(2):
                    o, x_ = ps[:, 4 + n % 2, :], 2 * (e % 2) + c
                    mm(o, wh1[:, c, c128], EXH[:, x_, :], c == 0, False)
                    mm(o, wh1[:, c, c128], EXL[:, x_, :], False, False)
                    ins = mm(o, wl1[:, c, c128], EXH[:, x_, :], False, c == 1)
                ins.then_inc(L2f_h, 1)

            def down(n):
                e, f = n // 8, n % 8
                wh2, wl2 = (unit16(f"L2f_{e}_s2", at, 8, D) for at in (0, SLOT))
                if f == 0:
                    pe.wait_ge(L2f_wl, 2 * e + 2)
                    release(2)
                pe.wait_ge(L2f_hl, n + 1)
                for i in range(NT):
                    o = bank(i // 2, D, at=D * (i % 2))
                    mm(o, EHH[:, n % 4, tile(i)], wh2[:, f, :], False, False)
                    mm(o, EHH[:, n % 4, tile(i)], wl2[:, f, :], False, False)
                    ins = mm(o, EHL[:, n % 4, tile(i)], wh2[:, f, :], False, n == 63 and i % 2 == 1)
                    if n == 63:
                        ins.then_inc(layer_out, 1)
                if n < 63:
                    ins.then_inc(L2f_y, 1)
                if f == 7 and e < 7:
                    pe.wait_ge(L2f_y, n + 1)
                    release(2)

            pe.wait_ge(L2f_xnl, 1)
            gather(0)
            pe.wait_ge(rk_spread, 8)
            pe.wait_ge(L2f_diag, 1)
            for n in range(2):
                mm(ps[:, n, :], C("ones", slice(0, 8)), b2, True, False)
            up(0)
            pe.wait_ge(L2f_h, 1)
            release(1)
            up(1)
            for n in range(64):
                if n % 8 == 2 and n // 8 < 7:
                    gather(n // 8 + 1)
                if n % 8 == 2 and n >= 8:
                    transpose_context(1, 2 * (n // 8) - 1)
                if n % 8 == 7:
                    transpose_context(1, 2 * (n // 8))
                if n < 62:
                    up(n + 2)
                down(n)
            transpose_context(1, NGROUP - 1)
            pe.wait_ge(layer_out, 36)
            release(2)
            layernorm("9b")
            loaded("L3x_a")
            wkk = unit("L3x_a", 1024, 2, D)
            for c in range(2):
                mm(ps[:, 7, c:c + 1], wkk[:, 0, 128 * c:128 * c + 128], C("L3x_b2")[:, 0:1], True, False)
                ins = mm(ps[:, 7, c:c + 1], wkk[0:D2, 1, 128 * c:128 * c + 128], C("L3x_b2")[0:D2, 1:2],
                         False, True)
            ins.then_inc(na_kb, 1)
            pe.wait_ge(cx_Ts_act, 2 * NGROUP)
            pe.wait_ge(cx_Ts_dve, 2 * NGROUP)
            narrow_queries(1)
            narrow_keys(1)
            narrow(1)
            layernorm(10)
            self1(1)
            layernorm(11)
            loaded("L3f")
            win = unit("L3f", 0, 2, 64)
            wout = unit("L3f", 128, D)
            for h in range(2):
                for c in range(2):
                    ins = mm(ps[half(h), 2, 0:256], win[:, c, :], xnT[:, c, 256 * h:256 * h + 256], c == 0, c == 1)
            ins.then_inc(L3f_s, 1)
            pe.wait_ge(L3f_acc, 16)
            for i in range(NT):
                h = i // 2
                mm(ps[:, 3 + i, 0:D], C("ones", slice(0, 1)), unit("L3f", 384, D, rows=slice(0, 1)), True, False)
                mm(ps[:, 3 + i, 0:D], FG_[half(h), tile(i % 2)], wout[half(h)], False, True) \
                    .then_inc(layer_out, 1)


def chunks(a):
    k, n = a.shape
    c = -(-k // 128)
    p = np.zeros((c * 128, n), np.float32)
    p[:k] = a
    return p.reshape(c, 128, n).transpose(1, 0, 2).reshape(128, c * n)


def column(v):
    return chunks(np.asarray(v).reshape(-1, 1))


def row(v):
    p = np.zeros((128, v.size), np.float32)
    p[0] = v
    return p


def packed(g):
    u = {}
    cat = lambda *a: np.concatenate(a, axis=1)

    def keys_transposed(wk):
        return chunks(np.concatenate([wk.T, wk.T[:, 128:DC]], axis=1))

    def bias_columns(bk):
        p = np.zeros((bk.size, 33), np.float32)
        p[:, 0] = p[:, 32] = bk
        return chunks(p)

    def with_row(a, r):
        return np.concatenate([a, np.asarray(r).reshape(1, -1)], axis=0)

    u["L0x_a"] = cat(chunks(g["L0_xattn_Wq"]), keys_transposed(g["L0_xattn_Wk"]),
                     bias_columns(g["L0_xattn_bk"]))
    u["L0x_b"] = chunks(with_row(g["L0_xattn_Wv"], g["L0_xattn_bv"]))

    def slots16(a):
        p = np.zeros((a.shape[0], a.shape[1] // 16, 64), np.float32)
        p[:, :, 0:16] = a.reshape(a.shape[0], -1, 16)
        return p.reshape(a.shape[0], -1)

    order = lambda a: a.reshape(a.shape[0], 4, 2, 2, 16).transpose(0, 3, 1, 2, 4).reshape(a.shape[0], 256)
    kv = g["L0_attn_Wkv_up"]
    u["L0a_a"] = cat(chunks(g["L0_attn_Wc_down"]), slots16(g["L0_attn_Wq_up"]),
                     slots16(np.concatenate([kv[:, :16], kv[:, :16]], axis=1)), kv[:, 16:])
    u["L0a_b"] = chunks(order(g["L0_attn_Wc_proj"].T).T)
    for e in range(8):
        u[f"L0f_{e}_w1"] = chunks(g["L0_ffn_w1"][e])
        u[f"L0f_{e}_w2"] = chunks(g["L0_ffn_w2"][e])
        u[f"L2f_{e}_w1"] = chunks(g["L2_ffn_W1"][e])
        u[f"L2f_{e}_w2"] = chunks(g["L2_ffn_W2"][e])
    for L, n in (("L1x", "L1_xattn"), ("L2x", "L2_xattn")):
        u[f"{L}_q"] = chunks(g[n + "_Wq"])
        u[f"{L}_k"] = keys_transposed(g[n + "_Wk"])
        u[f"{L}_v"] = chunks(g[n + "_Wv"])
        u[f"{L}_v"][D2, 1024:1024 + D] = g[n + "_bo"]
        u[f"{L}_o"] = chunks(g[n + "_Wo"])

    def qr(q, r):
        p = np.zeros((q.shape[0], 16, 64), np.float32)
        p[:, :, 0:16] = q.reshape(-1, 16, 16)
        p[:, :, 16:48] = r.reshape(-1, 16, 32)
        return p.reshape(q.shape[0], 1024)

    u["L1a_q"] = chunks(qr(g["L1_attn_Wq"], g["L1_attn_Wr"]))
    u["L1a_k"] = chunks(qr(g["L1_attn_Wk"], g["L1_attn_Wr"]))
    u["L1a_v"] = cat(chunks(order(g["L1_attn_Wv"])), chunks(order(g["L1_attn_Wo"].T).T),
                     row(order(g["L1_attn_bv"].reshape(1, -1))[0]), row(g["L1_attn_bo"]))
    for q in range(4):
        u[f"L1f_g{q}"] = np.concatenate([chunks(np.concatenate([g["L1_ffn_w_gate"][e], g["L1_ffn_w_fc"][e]], axis=1))
                                         for e in range(4 * q, 4 * q + 4)], axis=1)
    for q in range(2):
        u[f"L1f_p{q}"] = np.concatenate([g["L1_ffn_w_proj"][e] for e in range(8 * q, 8 * q + 8)], axis=1)
    u["L2a"] = cat(*(chunks(g["L2_attn_" + n]) for n in ("Wq", "Wk", "Wv", "Wo")))
    b2 = np.zeros((128, 2 * D), np.float32)
    b2[:8, :D] = b2[:8, D:] = g["L2_ffn_b2"]
    u["L2f_b2"] = b2
    u["L3x_a"] = cat(chunks(g["L3_xattn_Wq"]), keys_transposed(g["L3_xattn_Wk"]),
                     chunks(g["L3_xattn_Wk"]))
    u["L3x_b"] = cat(chunks(with_row(g["L3_xattn_Wv"], g["L3_xattn_bv"])), chunks(g["L3_xattn_Wo"]),
                     row(g["L3_xattn_bo"]))
    w = g["L3_attn_W_qkv"]
    u["L3a"] = cat(*(chunks(w[n::3].T) for n in range(3)), chunks(g["L3_attn_W_out"].T))
    wout = g["L3_ffn_Wout"]
    u["L3f"] = cat(chunks(g["L3_ffn_Win"]), np.concatenate([wout, wout], axis=0), row(g["L3_ffn_bout"]))

    c = {}
    p = np.arange(128)
    par, t = p // 64, p % 64
    same = par[:, None] == par[None, :]
    c["ident"] = np.eye(128)
    c["ones"] = np.ones((128, 128))
    c["same"] = same
    c["tri"] = same & (t[:, None] <= t[None, :])
    s = np.arange(64)
    c["delta"] = t[:, None] == s[None, :]
    neg = -1e30
    c["causal"] = np.where(s[None, :] <= t[:, None], 0.0, neg)
    c["bfull"] = np.where(same, 0.0, neg)
    c["bcausal"] = np.where(same & (t[None, :] <= t[:, None]), 0.0, neg)
    c["before"] = s[None, :] < t[:, None]
    r = np.arange(32)
    c["slot32"] = np.where((r // 16)[None, :] == par[:, None], (r % 16)[None, :], -1)
    r = np.arange(16)
    c["slot16"] = np.where((r // 8)[None, :] == par[:, None], (r % 8)[None, :] + 1, -1)
    c["rev8"] = np.tile(8 - np.arange(8), (128, 1))
    c["rev16"] = np.tile(16 - np.arange(16), (128, 1))
    c["nhalf"] = np.full((128, 64), -0.5)
    c["half"] = np.full((128, 8), 0.5)
    c = {n: np.asarray(a, np.float32) for n, a in c.items()}
    c["L0x_bq"] = column(g["L0_xattn_bq"])
    c["L1a_bq"] = column(qr(g["L1_attn_bq"].reshape(1, -1), g["L1_attn_br"].reshape(1, -1))[0])
    c["L1a_bk"] = column(qr(g["L1_attn_bk"].reshape(1, -1), g["L1_attn_br"].reshape(1, -1))[0])
    c["L2f_b1"] = column(g["L2_ffn_b1"].reshape(-1))
    c["L2f_waff"] = chunks(g["L2_ffn_waff"].T)
    c["L2f_thr"] = np.broadcast_to(g["L2_ffn_affinity_threshold"].reshape(1, 1), (128, 1))
    c["L0f_gate"] = chunks(g["L0_ffn_gate_w"])
    c["L1f_router"] = chunks(g["L1_ffn_w_router"])
    for n, k in (("g1", "ln1_g"), ("b1", "ln1_b"), ("g2", "ln2_g"), ("b2", "ln2_b"), ("bq", "bq"), ("bk", "bk")):
        c["L3x_" + n] = column(g["L3_xattn_" + k])
    c["L3x_g2"][D2:, 1] = c["L3x_g2"][:D2, 1]
    twice = lambda a: np.concatenate([a, a], axis=0)
    c["L3f_bin"] = twice(g["L3_ffn_bin_"].reshape(-1, 1))
    c["L3f_W1"], c["L3f_b1"], c["L3f_W2"] = (twice(g["L3_ffn_" + n]) for n in ("W1", "b1", "W2"))
    c["L3f_b2"] = twice(g["L3_ffn_b2"].reshape(-1, 1))
    const = np.concatenate([c[n].reshape(128, -1) for n in CW], axis=1)
    assert const.shape == (128, NCONST)
    widths = {n: SLOT if n in SPLIT_UNITS else u[n].shape[1] for n in UNITS}
    assert max(widths.values()) <= SLOT, widths
    units = np.concatenate([u[n].reshape(-1) for n in UNITS if n not in SPLIT_UNITS])
    return widths, np.ascontiguousarray(units), np.ascontiguousarray(const)


def kernel(**inputs):
    import concourse.bacc as _bacc
    from concourse.bass_utils import run_bass_kernel_spmd as _run

    g = {k: np.asarray(v) for k, v in inputs.items()}
    widths, units, const = packed(g)
    c = g["ctx_768"]
    arrays = {
        "units": units, "consts": const,
        "context": np.ascontiguousarray(c.reshape(B * KT, 128, DC).transpose(1, 0, 2)),
        "x_in": np.ascontiguousarray(g["x"].reshape(NT, 128, D).transpose(1, 0, 2)),
    }
    nc = _bacc.Bacc("TRN2", target_bir_lowering=False, num_devices=1)
    aps = {n: nc.dram_tensor(n, a.shape, F32, kind="ExternalInput").ap() for n, a in arrays.items()}
    out = nc.dram_tensor("out", (128, NT, D), F32, kind="ExternalOutput").ap()
    build(nc, widths, aps["units"], aps["consts"], aps["context"], aps["x_in"], out)
    r = _run(nc, [arrays], core_ids=[0])
    return r.results[0]["out"].transpose(1, 0, 2).reshape(B, S, D)
```
